# Optimizing a Trainium2 kernel written in Bass

```python
import numpy as np
import jax
import jax.numpy as jnp

def _softmax(x, axis=-1):
    return jax.nn.softmax(x, axis=axis)

def _gelu(x):
    return jax.nn.gelu(x, approximate=True)

def _silu(x):
    return jax.nn.silu(x)

def _sigmoid(x):
    return jax.nn.sigmoid(x)

def _layernorm(x, axis=-1, eps=1e-05):
    m = jnp.mean(x, axis=axis, keepdims=True)
    v = jnp.var(x, axis=axis, keepdims=True)
    return (x - m) / jnp.sqrt(v + eps)

def _scatter_add(tgt, idx, src, axis=0):
    return tgt.at[idx].add(src)

def _segment_sum(src, seg, n):
    return jax.ops.segment_sum(src, seg, n)
kernel_name = 'mk_gnn_resnorm_d4_gnn_r8_5e50b2'

def setup_inputs(seed: int=0):
    np.random.seed(seed)
    _w = jnp.asarray

    def _rec_inputs():
        import jax
        import jax.numpy as jnp
        _gk = jax.random.key(seed)
        x = -0.0005121 + 1.001 * jax.random.normal(jax.random.fold_in(_gk, 1), (12500, 64), jnp.float32)
        src = jax.random.randint(jax.random.fold_in(_gk, 2), (200000,), 0, 12500, jnp.int32)
        dst = jax.random.randint(jax.random.fold_in(_gk, 3), (200000,), 0, 12500, jnp.int32)
        _o = jnp.argsort(dst, stable=True)
        src = src[_o]
        dst = dst[_o]
        edge_attr_16 = -0.00010739 + 0.99994 * jax.random.normal(jax.random.fold_in(_gk, 12), (200000, 16), jnp.float32)
        edge_type_32 = jax.random.randint(jax.random.fold_in(_gk, 14), (200000,), 0, 32, jnp.int32)
        edge_weight = jax.random.uniform(jax.random.fold_in(_gk, 15), (200000,), jnp.float32, 0.0, 0.999998)
        return (x, src, dst, edge_attr_16, edge_type_32, edge_weight)
    x, src, dst, edge_attr_16, edge_type_32, edge_weight = _rec_inputs()

    def _L0_gnn_setup():
        import jax, jax.numpy as jnp
        import numpy as np
        N, D, E, DE, DG, H, DOUT = (6250, 64, 100000, 16, 64, 256, 64)

        def mish(x):
            return x * jnp.tanh(jax.nn.softplus(x))
        key = jax.random.key(seed)
        ks = jax.random.split(key, 8)
        return {'nodes': jax.random.normal(ks[0], (N, D), dtype=jnp.float32), 'edges': jax.random.normal(ks[1], (E, DE), dtype=jnp.float32), 'globals_': jax.random.normal(ks[2], (1, DG), dtype=jnp.float32), 'senders': jax.random.randint(ks[3], (E,), 0, N, dtype=jnp.int32), 'receivers': jax.random.randint(ks[4], (E,), 0, N, dtype=jnp.int32), 'We_kernel': jax.random.normal(ks[5], (DE, D), dtype=jnp.float32) * (1.0 / np.sqrt(DE)), 'We_bias': jnp.zeros((D,), dtype=jnp.float32), 'epsilon': jnp.zeros((1, 1), dtype=jnp.float32), 'W1': jax.random.normal(ks[6], (D + DG, H), dtype=jnp.float32) * (1.0 / np.sqrt(D + DG)), 'b1': jnp.zeros((H,), dtype=jnp.float32), 'W2': jax.random.normal(ks[7], (H, DOUT), dtype=jnp.float32) * (1.0 / np.sqrt(H)), 'b2': jnp.zeros((DOUT,), dtype=jnp.float32)}
    _L0_gnn_all = _L0_gnn_setup()
    _L0_gnn_in = {k: v for k, v in _L0_gnn_all.items() if k in ('globals_', 'We_kernel', 'We_bias', 'epsilon', 'W1', 'b1', 'W2', 'b2')}
    del _L0_gnn_all

    def _L1_gnn_setup():
        import jax, jax.numpy as jnp
        import numpy as np
        K_HOPS = 2
        key = jax.random.key(seed)
        k1, k2, k3, k4 = jax.random.split(key, 4)
        N, E, D_IN, D_OUT = (6250, 100000, 64, 64)
        x = jax.random.normal(k1, (N, D_IN), dtype=jnp.float32)
        edge_index = jax.random.randint(k2, (2, E), 0, N, dtype=jnp.int64)
        edge_weights = jax.random.uniform(k3, (E,), dtype=jnp.float32)
        weight = jax.random.normal(k4, (D_OUT, D_IN), dtype=jnp.float32) * (1.0 / np.sqrt(D_IN))
        bias = jnp.zeros((D_OUT,), dtype=jnp.float32)
        return {'x': x, 'edge_index': edge_index, 'edge_weights': edge_weights, 'weight': weight, 'bias': bias}
    _L1_gnn_all = _L1_gnn_setup()
    _L1_gnn_in = {k: v for k, v in _L1_gnn_all.items() if k in ('weight', 'bias')}
    del _L1_gnn_all

    def _L2_gnn_setup():
        import jax, jax.numpy as jnp
        import numpy as np
        N_NODES = 6250
        N_EDGES = 100000
        D = 64
        EPS = 1e-05
        key = jax.random.key(seed)
        k1, k2, k3 = jax.random.split(key, 3)
        z = jax.random.normal(k1, (N_NODES, D), dtype=jnp.float32)
        src = jax.random.randint(k2, (N_EDGES,), 0, N_NODES)
        dst = jax.random.randint(k3, (N_EDGES,), 0, N_NODES)
        gamma = jnp.ones((D,), dtype=jnp.float32)
        beta = jnp.zeros((D,), dtype=jnp.float32)
        return {'z': z, 'src': src, 'dst': dst, 'gamma': gamma, 'beta': beta}
    _L2_gnn_all = _L2_gnn_setup()
    _L2_gnn_in = {k: v for k, v in _L2_gnn_all.items() if k in ('gamma', 'beta')}
    del _L2_gnn_all

    def _L3_gnn_setup():
        import jax, jax.numpy as jnp
        import numpy as np
        N_NODES = 12500
        N_EDGES = 125000
        IN_F = 64
        OUT_F = 64
        N_REL = 32
        N_BASES = 30
        key = jax.random.key(seed)
        k = jax.random.split(key, 8)
        node_features = jax.random.normal(k[0], (N_NODES, IN_F), dtype=jnp.float32)
        senders = jax.random.randint(k[1], (N_EDGES,), 0, N_NODES, dtype=jnp.int32)
        receivers = jax.random.randint(k[2], (N_EDGES,), 0, N_NODES, dtype=jnp.int32)
        relation_types = jax.random.randint(k[3], (N_EDGES,), 0, N_REL, dtype=jnp.int32)
        basis = jax.random.normal(k[4], (N_BASES, IN_F, OUT_F), dtype=jnp.float32) * 0.01
        coeff = jax.random.normal(k[5], (N_REL, N_BASES), dtype=jnp.float32) * 0.01
        self_weight = jax.random.normal(k[6], (IN_F, OUT_F), dtype=jnp.float32) * 0.01
        bias = jnp.zeros((OUT_F,), dtype=jnp.float32)
        return {'node_features': node_features, 'senders': senders, 'receivers': receivers, 'relation_types': relation_types, 'basis': basis, 'coeff': coeff, 'self_weight': self_weight, 'bias': bias}
    _L3_gnn_all = _L3_gnn_setup()
    _L3_gnn_in = {k: v for k, v in _L3_gnn_all.items() if k in ('basis', 'coeff', 'self_weight', 'bias')}
    del _L3_gnn_all
    return {'x': x, 'src': src, 'dst': dst, 'edge_attr_16': edge_attr_16, 'edge_type_32': edge_type_32, 'edge_weight': edge_weight, 'L0_gnn_globals_': _L0_gnn_in['globals_'], 'L0_gnn_We_kernel': _L0_gnn_in['We_kernel'], 'L0_gnn_We_bias': _L0_gnn_in['We_bias'], 'L0_gnn_epsilon': _L0_gnn_in['epsilon'], 'L0_gnn_W1': _L0_gnn_in['W1'], 'L0_gnn_b1': _L0_gnn_in['b1'], 'L0_gnn_W2': _L0_gnn_in['W2'], 'L0_gnn_b2': _L0_gnn_in['b2'], 'L1_gnn_weight': _L1_gnn_in['weight'], 'L1_gnn_bias': _L1_gnn_in['bias'], 'L2_gnn_gamma': _L2_gnn_in['gamma'], 'L2_gnn_beta': _L2_gnn_in['beta'], 'L3_gnn_basis': _L3_gnn_in['basis'], 'L3_gnn_coeff': _L3_gnn_in['coeff'], 'L3_gnn_self_weight': _L3_gnn_in['self_weight'], 'L3_gnn_bias': _L3_gnn_in['bias']}

def reference(x, src, dst, edge_attr_16, edge_type_32, edge_weight, L0_gnn_globals_, L0_gnn_We_kernel, L0_gnn_We_bias, L0_gnn_epsilon, L0_gnn_W1, L0_gnn_b1, L0_gnn_W2, L0_gnn_b2, L1_gnn_weight, L1_gnn_bias, L2_gnn_gamma, L2_gnn_beta, L3_gnn_basis, L3_gnn_coeff, L3_gnn_self_weight, L3_gnn_bias):
    import jax
    import jax.numpy as jnp

    def _L0_gnn_ref(nodes, edges, globals_, senders, receivers, We_kernel, We_bias, epsilon, W1, b1, W2, b2):
        import jax, jax.numpy as jnp
        import numpy as np
        N, D, E, DE, DG, H, DOUT = (6250, 64, 100000, 16, 64, 256, 64)

        def mish(x):
            return x * jnp.tanh(jax.nn.softplus(x))
        num_nodes = nodes.shape[-2]
        sent = jnp.take(nodes, senders, axis=0)
        edge_feat = mish(sent + edges @ We_kernel + We_bias)
        aggr = jax.ops.segment_sum(edge_feat, receivers, num_segments=num_nodes)
        nodes = (1.0 + epsilon) * nodes + aggr
        glob = jnp.repeat(globals_, num_nodes, axis=-2)
        nodes = jnp.concatenate([nodes, glob], axis=-1)
        hidden = mish(nodes @ W1 + b1)
        out = hidden @ W2 + b2
        return out

    def _L1_gnn_ref(x, edge_index, edge_weights, weight, bias):
        import jax, jax.numpy as jnp
        import numpy as np
        K_HOPS = 2
        N = x.shape[0]
        self_loops = jnp.arange(N, dtype=edge_index.dtype)
        src = jnp.concatenate([edge_index[0], self_loops])
        dst = jnp.concatenate([edge_index[1], self_loops])
        ones = jnp.ones(src.shape[0], dtype=x.dtype)
        deg = jax.ops.segment_sum(ones, dst, num_segments=N)
        deg_inv_sqrt = jnp.where(deg > 0, jax.lax.rsqrt(deg), 0.0)
        norm = deg_inv_sqrt[src] * deg_inv_sqrt[dst]
        h = x
        for _ in range(K_HOPS):
            msg = h[src] * norm[:, None]
            h = jax.ops.segment_sum(msg, dst, num_segments=N)
        return h @ weight.T + bias

    def _L2_gnn_ref(z, src, dst, gamma, beta):
        import jax, jax.numpy as jnp
        import numpy as np
        N_NODES = 6250
        N_EDGES = 100000
        D = 64
        EPS = 1e-05
        n = z.shape[0]
        z_src = z[src]
        z_dst = z[dst]
        e = jax.nn.relu(jnp.sum(z_src * z_dst, axis=-1))
        e_max = jax.ops.segment_max(e, dst, num_segments=n)
        e_exp = jnp.exp(e - e_max[dst])
        denom = jax.ops.segment_sum(e_exp, dst, num_segments=n)
        alpha = e_exp / denom[dst]
        h = jax.ops.segment_sum(alpha[:, None] * z_src, dst, num_segments=n)
        mean = jnp.mean(h, axis=0)
        var = jnp.var(h, axis=0)
        h = (h - mean) * jax.lax.rsqrt(var + EPS) * gamma + beta
        return jax.nn.relu(h)

    def _L3_gnn_ref(node_features, senders, receivers, relation_types, basis, coeff, self_weight, bias):
        import jax, jax.numpy as jnp
        import numpy as np
        N_NODES = 12500
        N_EDGES = 125000
        IN_F = 64
        OUT_F = 64
        N_REL = 32
        N_BASES = 30
        num_nodes = node_features.shape[0]
        n_edges = senders.shape[0]
        rel_weights = jnp.einsum('rb,bio->rio', coeff, basis)
        src_features = node_features[senders]
        seg_ids = receivers * N_REL + relation_types
        agg = jax.ops.segment_sum(src_features, seg_ids, num_segments=num_nodes * N_REL)
        agg = agg.reshape(num_nodes, N_REL, node_features.shape[1])
        aggregated = jnp.einsum('nri,rio->no', agg, rel_weights)
        ones = jnp.ones((n_edges,), dtype=node_features.dtype)
        in_degree = jax.ops.segment_sum(ones, receivers, num_segments=num_nodes)
        in_degree = jnp.maximum(in_degree, 1.0)
        out = aggregated / in_degree[:, None]
        out = out + node_features @ self_weight
        out = out + bias
        return out
    edge_index = jnp.stack([src, dst])
    x = _layernorm(x + _L0_gnn_ref(x, edge_attr_16, L0_gnn_globals_, src, dst, L0_gnn_We_kernel, L0_gnn_We_bias, L0_gnn_epsilon, L0_gnn_W1, L0_gnn_b1, L0_gnn_W2, L0_gnn_b2), axis=-1)
    x = _layernorm(x + _L1_gnn_ref(x, edge_index, edge_weight, L1_gnn_weight, L1_gnn_bias), axis=-1)
    x = _layernorm(x + _L2_gnn_ref(x, src, dst, L2_gnn_gamma, L2_gnn_beta), axis=-1)
    x = _layernorm(x + _L3_gnn_ref(x, src, dst, edge_type_32, L3_gnn_basis, L3_gnn_coeff, L3_gnn_self_weight, L3_gnn_bias), axis=-1)
    return x

_drawn_inputs = setup_inputs


def setup_inputs(seed=0):
    import zlib

    import numpy as np

    out = dict(_drawn_inputs(seed))
    spreads = {'L0_gnn_We_bias': (0.0, 0.1),
     'L0_gnn_b1': (0.0, 0.304),
     'L0_gnn_b2': (0.0, 0.288),
     'L1_gnn_bias': (0.0, 0.1),
     'L2_gnn_gamma': (1.0, 0.2),
     'L2_gnn_beta': (0.0, 0.1),
     'L3_gnn_bias': (0.0, 0.1)}
    factors = {'L3_gnn_basis': 8.0, 'L3_gnn_coeff': 8.0}
    for name, (base, spread) in spreads.items():
        noise = np.random.default_rng([zlib.crc32(name.encode()), seed]).standard_normal(out[name].shape)
        drawn = base * np.exp(spread * noise) if base else spread * noise
        out[name] = jnp.asarray(drawn.astype(out[name].dtype))
    for name, factor in factors.items():
        out[name] = (out[name] * factor).astype(out[name].dtype)
    return out
```

```python
from contextlib import ExitStack

import concourse.bass as bass
from concourse import mybir

F32 = mybir.dt.float32
I32 = mybir.dt.int32
ALU = mybir.AluOpType
ACT = mybir.ActivationFunctionType
AX = mybir.AxisListType.X

P = 128
N, E, D = 12500, 200000, 64
DE = 16
H = 256
NREL, NBASE = 32, 30
EPS = 1e-5
TINY = 1e-30
MISH_CAP = 10.0

C = 8
GE = P * C
NG = -(-E // GE)
TAIL = E - (NG - 1) * GE
TAILP = TAIL // C
R = 4
NI = NG // R
HG = NG // 2
W = 128
M1 = D + 1

CB = 7
NB = -(-N // P)
NCH = NB // CB
CW = CB * P
CD = CB * D
NP = NB * P
NACC = NP + W
LASTN = N - (NB - 1) * P
NPAD = NP - N
HALF = CW // 2
YW = NREL * D
assert NI * R == NG and HG * 2 == NG and NB == NCH * CB and TAILP * C == TAIL and R % 2 == 0

MESSAGES, HOP1, HOP2, ATTENTION, RELATIONS = range(5)


class Steps:

    def __init__(self, eng, sem):
        self.eng, self.sem, self.done, self.at, self.index, self.per = eng, sem, 0, 0, 0, 0

    def turn(self, index, per):
        self.index, self.per, self.at = index, per, 0

    def link(self, ins):
        ins.then_inc(self.sem, 1)
        self.at += 1
        self.eng.wait_ge(self.sem, self.index * self.per + (self.done + self.at))

    def end(self, turns):
        assert self.at == self.per, (self.at, self.per)
        self.done += turns * self.per
        self.index, self.per, self.at = 0, 0, 0


def gnn(nc, a, out, stop=9):
    with ExitStack() as ctx:
        def sb(name, shape, dt=F32):
            return ctx.enter_context(nc.sbuf_tensor(name, shape, dt))

        def sem(name):
            return ctx.enter_context(nc.semaphore(name))

        def psum(name, cols):
            return ctx.enter_context(nc.psum_tensor(name, [P, cols], F32))

        def scratch(name, shape, dt=F32):
            return nc.dram_tensor(name, shape, dt, kind="Internal").ap()

        table = {HOP1: scratch("hop1_table", (NP, D)), HOP2: scratch("hop2_table", (NP, D)),
                 ATTENTION: scratch("attention_table", (NP, D)),
                 RELATIONS: scratch("relation_table", (NP * NREL, D))}
        src_index = scratch("src_index", (NG * GE,), I32)
        rel_index = scratch("rel_index", (NG * GE,), I32)
        group_dram = scratch("group_dram", (NG, 4), I32)
        relw_dram = scratch("relw_dram", (NREL, D, D))

        acc = sb("acc", [P, NACC])
        zT = sb("zT", [P, NACC])
        xn = sb("xn", [P, NB, D])
        dstrel = sb("dstrel", [P, NG + 1, C])
        grow = sb("grow", [1, NG * 4], I32)
        idx = sb("idx", [P, R, C], I32)
        rows = sb("rows", [P, R, C, M1])
        attrs = sb("attrs", [P, R, C * DE])
        attrT = sb("attrT", [P, 2, P])
        msg = sb("msg", [P, C, M1])
        onehot = sb("onehot", [P, 2, C, W])
        prod = sb("prod", [P, C, W])
        rowsT = sb("rowsT", [D, C * P])
        score8 = sb("score8", [P, 4, C])
        dx = sb("dx", [P, C])
        chunkT = sb("chunkT", [P, CW])
        hid = sb("hid", [P, 2, CW])
        tmp = sb("tmp", [P, 2, CW])
        stage = sb("stage", [P, CD])
        small = sb("small", [P, 8, CB])
        gtab = sb("gtab", [P, 2, 4], I32)
        dinv = sb("dinv", [P, NB])
        cinv = sb("cinv", [P, NB])
        valid = sb("valid", [P, NB])
        ident = sb("ident", [P, P])
        iota = sb("iota", [P, W])
        ones = sb("ones", [P, P])
        attrw = sb("attrw", [P, C * D])
        rowb = sb("rowb", [1, 2, C * D])
        w1 = sb("w1", [D, 2, H])
        w2 = sb("w2", [P, 2, D])
        cols = sb("cols", [P, 8])
        bvec = sb("bvec", [P, 4, D])
        bn = sb("bn", [P, 6, D])
        w3 = sb("w3", [D, 3, D])
        coeff = sb("coeff", [NREL, NBASE])
        coeffT = sb("coeffT", [NBASE, NREL])
        relw = sb("relw", [D, NREL, D])

        def edge_view(k):
            return zT[0:HG, 2 * GE * k:2 * GE * (k + 1)].rearrange("p (h e) -> p h e", h=2)
        dst_i, dst_f = edge_view(0).bitcast(I32), edge_view(1)
        src_i, typ_i = edge_view(2).bitcast(I32), edge_view(3).bitcast(I32)
        basis = zT[0:NBASE, 8 * GE:8 * GE + D * D]
        relw_flat = zT[0:NREL, 0:D * D]
        hn = zT[:, 0:NB * D].rearrange("p (b d) -> p b d", d=D)
        ybuf = [zT[:, NB * D + YW * k:NB * D + YW * (k + 1)] for k in range(2)]

        tmp_flat, hid_flat = (t[:, :, :].rearrange("p m n -> p (m n)") for t in (tmp, hid))
        def third(t, j):
            return t[:, C * D * j:C * D * (j + 1)]
        msg_v, msg_u = [third(tmp_flat, j) for j in range(2)], [third(hid_flat, j) for j in range(2)]
        msg_n, msg_r = third(tmp_flat, 2), third(hid_flat, 2)

        def blocks(t):
            return t.rearrange("p (b d) -> p b d", d=D)

        S2, T2, H2 = psum("S2", 1024), psum("T2", 1024), psum("H2", 1024)
        A1, O1 = psum("A1", 512), psum("O1", 512)

        names = """pool_const iota_ready small_loaded edges_loaded x_loaded pads_ready dve_steps
            weights_zero matrices_ready setup_pe setup_dve index_stored rel_index_ready group_ready group_stored
            group_loaded relw_ready relw_stored relw_loaded
            gather_started onehot_ready window_summed acc_added extra_ready extra_summed
            score_extra_ready score_extra_summed attrs_turned attrs_copied attrs_mixed exp_in exp_out msg_ready
            rows_turned rows_copied scored scores_read
            again_turned again_copied inverse_in inverse_out log_done root_log
            init_staged init_turned init_copied zeros_ready zero_copied x_final out_stored
            act_started pe_started dve_started root_in root_out product_ready low_copied high_copied y_free bn_sum_ready bn_summed""".split()
        s = {n: sem(n) for n in names}
        idx_ready = [sem(f"idx_ready{k}") for k in range(R)]
        gathered = [sem(f"gathered{k}") for k in range(R)]
        attr_loaded = [sem(f"attr_loaded{k}") for k in range(R)]
        y_stored = [sem(f"y_stored{k}") for k in range(2)]
        st = {p: {n: sem(f"stage{p}_{n}") for n in ["acc_copied", "hidden", "capped", "exp", "mish", "counts", "product", "staged",
                                                    "stage_free", "turned", "taken", "stored"]} for p in range(5)}

        block = ctx.enter_context(nc.Block())

        def table_chunk(p, it):
            return table[p].rearrange("(i b p) d -> i p b d", b=CB, p=P)[bass.ds(it, 1)].rearrange(
                "a p b d -> (a p) b d")

        def one(view, g):
            return view[bass.ds(g, 1)].rearrange("a p c -> (a p) c")

        def acc_chunk(m, it):
            return acc[0:m, bass.ds(it * CW, CW)]

        def acc_total(p):
            return (p + 1) * NG + R

        src_v = src_index.rearrange("(g p c) -> g p c", p=P, c=C)
        rel_v = rel_index.rearrange("(g p c) -> g p c", p=P, c=C)
        attr_v = a["edge_attr_16"][0:(NG - 1) * GE].rearrange("(g p c) k -> g p (c k)", p=P, c=C)
        attr_tail = a["edge_attr_16"][(NG - 1) * GE:E].rearrange("(p c) k -> p (c k)", c=C)
        ROOTS = {MESSAGES: 0, HOP2: NCH, "bn": 2 * NCH, ATTENTION: 2 * NCH + 1, RELATIONS: 3 * NCH + 1}
        SMALL_LOADS = 3 * C + 2 + 2 + 1 + 4 + 3

        def group_values(eng, g, words):
            most = (N, NP // W, NG * NP // W, NG * NP // W)
            return [eng.value_load(grow[0:1, bass.ds(g * 4 + j, 1)], min_val=0, max_val=most[j]) for j in words]

        def further(eng, w, i):
            return bass.ds(nc.s_assert_within(w + i * W + W, W, NP, skip_runtime_bounds_check_because="further windows end with the last node"), W)

        @block.sync
        def _(sp):
            def edges(view, name):
                x = a[name]
                full = x[0:(NG - 1) * GE].rearrange("(q e) -> q e", e=GE)
                sp.dma_start(view[:, 0, :], full[0:HG]).then_inc(s["edges_loaded"], 16)
                sp.dma_start(view[0:HG - 1, 1, :], full[HG:NG - 1]).then_inc(s["edges_loaded"], 16)
                sp.dma_start(view[HG - 1:HG, 1, 0:TAIL],
                             x[(NG - 1) * GE:E].rearrange("(q e) -> q e", q=1)).then_inc(s["edges_loaded"], 16)

            sp.wait_ge(s["pads_ready"], 4)
            edges(src_i, "src")
            edges(dst_i, "dst")
            edges(typ_i, "edge_type_32")
            sp.dma_start(xn[:, 0:NB - 1, :], a["x"][0:(NB - 1) * P].rearrange("(b p) d -> p b d", p=P)).then_inc(
                s["x_loaded"], 16)
            sp.dma_start(xn[0:LASTN, NB - 1, :], a["x"][(NB - 1) * P:N]).then_inc(s["x_loaded"], 16)
            sp.dma_start(basis, a["L3_gnn_basis"].rearrange("b i o -> b (i o)")).then_inc(s["x_loaded"], 16)
            sp.wait_ge(s["edges_loaded"], 16 * 9)
            sp.dma_start(src_index.rearrange("(h q e) -> q h e", h=2, e=GE), src_i).then_inc(s["index_stored"], 16)
            sp.wait_ge(s["index_stored"], 16)
            sp.wait_ge(s["group_ready"], 1)
            sp.dma_start(group_dram.rearrange("(h q) w -> q h w", h=2), gtab[0:HG]).then_inc(s["group_stored"], 16)
            sp.wait_ge(s["group_stored"], 16)
            sp.dma_start(grow[:, :], group_dram.rearrange("g w -> (g w)").rearrange("(a n) -> a n", a=1)).then_inc(
                s["group_loaded"], 16)
            sp.wait_ge(s["rel_index_ready"], 1)
            sp.dma_start(rel_index.rearrange("(h q e) -> q h e", h=2, e=GE), typ_i).then_inc(s["index_stored"], 16)
            sp.wait_ge(s["relw_ready"], 8)
            sp.dma_start(relw_dram.rearrange("r i o -> r (i o)"), relw_flat).then_inc(s["relw_stored"], 16)
            sp.wait_ge(s["relw_stored"], 16)
            sp.dma_start(relw[:, :, :], relw_dram.rearrange("r i o -> i r o")).then_inc(s["relw_loaded"], 16)

            def edge_pass(p, view):
                attributes = p == MESSAGES
                for k in range(R):
                    if p:
                        sp.wait_ge(gathered[k], p * NI * C * 16)
                    if p == RELATIONS and k == 0:
                        sp.wait_ge(s["index_stored"], 32)
                    sp.dma_start(idx[:, k, :], view[k]).then_inc(idx_ready[k], 16)
                    if attributes:
                        sp.dma_start(attrs[:, k, :], attr_v[k]).then_inc(attr_loaded[k], 16)
                with sp.Fori(0, NI - 2) as it:
                    for k in range(R):
                        sp.wait_ge(gathered[k], it * (C * 16) + (p * NI + 1) * (C * 16))
                        sp.dma_start(idx[:, k, :], one(view, it * R + (R + k))).then_inc(idx_ready[k], 16)
                        if attributes:
                            sp.wait_ge(s["attrs_turned"], it * R + (k + 1))
                            sp.dma_start(attrs[:, k, :], one(attr_v, it * R + (R + k))).then_inc(attr_loaded[k], 16)
                for k in range(R):
                    g = NG - R + k
                    sp.wait_ge(gathered[k], (p * NI + NI - 1) * (C * 16))
                    sp.dma_start(idx[:, k, :], view[g]).then_inc(idx_ready[k], 16)
                    if attributes:
                        sp.wait_ge(s["attrs_turned"], g - R + 1)
                        if g < NG - 1:
                            sp.dma_start(attrs[:, k, :], attr_v[g]).then_inc(attr_loaded[k], 16)
                        else:
                            sp.dma_start(attrs[0:TAILP, k, :], attr_tail).then_inc(attr_loaded[k], 16)

            def store_table(p):
                q = st[p - 1]
                sp.sem_inc(q["stage_free"], 1)
                with sp.Fori(0, NCH) as it:
                    sp.wait_ge(q["staged"], it + 1)
                    sp.dma_start(table_chunk(p, it), blocks(stage[:, :])).then_inc(q["stored"], 16)
                    sp.wait_ge(q["stored"], it * 16 + 16)
                    sp.sem_inc(q["stage_free"], 1)

            edge_pass(MESSAGES, src_v)
            store_table(HOP1)
            if stop >= 1:
                edge_pass(HOP1, src_v)
                store_table(HOP2)
                edge_pass(HOP2, src_v)
            if stop >= 2:
                store_table(ATTENTION)
                edge_pass(ATTENTION, src_v)
            if stop >= 3:
                sp.sem_inc(s["y_free"], 2)
                y_rows = table[RELATIONS].rearrange("(n p r) d -> n p (r d)", p=P, r=NREL)
                with sp.Fori(0, NCH) as it:
                    for b in range(CB):
                        sp.wait_ge(s["low_copied"], it * CB + (b + 2))
                        sp.wait_ge(s["high_copied"], it * CB + (b + 2))
                        sp.dma_start(one(y_rows, it * CB + b), ybuf[b % 2]).then_inc(y_stored[b % 2], 16)
                        for c in ([b - 1] if 0 < b < CB - 1 else [b - 1, b] if b else []):
                            before = sum(x % 2 == c % 2 for x in range(CB))
                            sp.wait_ge(y_stored[c % 2], it * (16 * before) + 16 * (c // 2 + 1))
                            sp.sem_inc(s["y_free"], 1)
                edge_pass(RELATIONS, rel_v)
            sp.wait_ge(s["index_stored"], 32)
            sp.wait_ge(s["relw_loaded"], 16)
            sp.wait_ge(s["x_final"], 1)
            sp.dma_start(out[0:(NB - 1) * P].rearrange("(b p) d -> p b d", p=P), xn[:, 0:NB - 1, :]).then_inc(
                s["out_stored"], 16)
            sp.dma_start(out[(NB - 1) * P:N], xn[0:LASTN, NB - 1, :]).then_inc(s["out_stored"], 16)
            sp.wait_ge(s["out_stored"], 32)

        @block.gpsimd
        def _(pool):
            pool.iota(prod[:, 0, :].bitcast(I32), pattern=[[1, W]], base=0, channel_multiplier=0).then_inc(
                s["iota_ready"], 1)
            pool.memset(ident[:, :], 0.0).then_inc(s["pool_const"], 1)
            pool.memset(valid[:, :], 1.0).then_inc(s["pool_const"], 1)
            pool.memset(prod[:, 1, :], 1.0).then_inc(s["pool_const"], 1)
            pool.wait_ge(s["pool_const"], 3)
            pool.affine_select(out=ident[:, :], in_=ident[:, :], compare_op=ALU.not_equal, fill=1.0, base=0,
                               pattern=[[-1, P]], channel_multiplier=1).then_inc(s["pool_const"], 1)
            pool.affine_select(out=valid[:, :], in_=valid[:, :], compare_op=ALU.is_ge, fill=0.0, base=N - 1,
                               pattern=[[-P, NB]], channel_multiplier=-1).then_inc(s["pool_const"], 1)
            pool.affine_select(out=prod[:, 1, :], in_=prod[:, 1, :], compare_op=ALU.is_ge, fill=0.0, base=-1,
                               pattern=[[1, P]], channel_multiplier=-1).then_inc(s["pool_const"], 1)

            def edge_pass(p, tab):
                with pool.Fori(0, NI) as it:
                    for k in range(R):
                        pool.wait_ge(s["acc_added"], it * R + (p * NG + k + 1))
                        pool.wait_ge(idx_ready[k], it * 16 + (p * NI + 1) * 16)
                        pool.sem_inc(s["gather_started"], 1)
                        for c in range(C):
                            pool.indirect_dma_start(
                                out=rows[:, k, c, 0:D], out_offset=None, in_=tab,
                                in_offset=bass.IndirectOffsetOnAxis(ap=idx[:, k, c:c + 1], axis=0)).then_inc(
                                gathered[k], 16)

            edge_pass(MESSAGES, a["x"])
            for p in [HOP1, HOP2] * (stop >= 1) + [ATTENTION] * (stop >= 2):
                pool.wait_ge(st[p - 1]["stored"], 16 * NCH)
                edge_pass(p, table[p])
            if stop >= 3:
                pool.wait_ge(s["y_free"], 2 + NCH * CB)
                edge_pass(RELATIONS, table[RELATIONS])

        @block.scalar
        def _(act):
            act.preload_act_table_set("natural_log_exp_and_others")
            loads = []

            def load(dst, src):
                act.dma_start(dst, src).then_inc(s["small_loaded"], 16)
                loads.append(1)

            act.wait_ge(s["weights_zero"], 1)
            for c in range(C):
                load(attrw[DE * c:DE * (c + 1), D * c:D * (c + 1)], a["L0_gnn_We_kernel"])
                load(rowb[0:1, 0, D * c:D * (c + 1)], a["L0_gnn_We_bias"].rearrange("(a d) -> a d", a=1))
                load(rowb[0:1, 1, D * c:D * (c + 1)], a["L0_gnn_b2"].rearrange("(a d) -> a d", a=1))
            load(w1[:, :, :], a["L0_gnn_W1"].rearrange("(t p) h -> p t h", t=2))
            load(w2[:, :, :], a["L0_gnn_W2"].rearrange("(t p) h -> p t h", t=2))
            with nc.allow_non_contiguous_dma(reason="columns of small vectors"):
                load(cols[0:D, 0:1], a["L0_gnn_globals_"].rearrange("a d -> d a"))
                load(cols[:, 1:3], a["L0_gnn_b1"].rearrange("(m p) -> p m", m=2))
            load(cols[0:D, 3:4], a["L0_gnn_epsilon"][0].partition_broadcast(D))
            for k, name in enumerate(["L1_gnn_bias", "L2_gnn_gamma", "L2_gnn_beta", "L3_gnn_bias"]):
                load(bvec[:, k, :], a[name].partition_broadcast(P))
            load(w3[:, 0, :], a["L1_gnn_weight"])
            load(w3[:, 2, :], a["L3_gnn_self_weight"])
            load(coeff[:, :], a["L3_gnn_coeff"])
            assert len(loads) == SMALL_LOADS

            act.wait_ge(s["setup_dve"], 1)
            act.wait_ge(s["x_loaded"], 48)
            with act.Fori(0, NCH) as it:
                act.activation(stage[:, :], xn[:, bass.ds(it * CB, CB), :].rearrange("p b d -> p (b d)"),
                               ACT.Copy).then_inc(s["init_staged"], 1)
                act.wait_ge(s["init_turned"], it + 1)
                act.sem_inc(s["act_started"], 1)
                act.activation(acc_chunk(D, it), H2[0:D, 0:CW], ACT.Identity, bias=0.0,
                               scale=cols[0:D, 3:4]).then_inc(s["init_copied"], 1)

            def root(out_, in_, value):
                act.wait_ge(s["root_in"], value)
                act.activation(out_, in_, ACT.Ln).then_inc(s["root_log"], 1)
                act.wait_ge(s["root_log"], value)
                act.activation(out_, out_, ACT.Exp, scale=-0.5).then_inc(s["root_out"], 1)

            def reciprocal(out_, in_, value):
                act.activation(out_, in_, ACT.Ln, bias=cols[:, 6:7]).then_inc(s["log_done"], 1)
                act.wait_ge(s["log_done"], value)
                act.activation(out_, out_, ACT.Exp, scale=-1.0).then_inc(s["inverse_out"], 1)

            def ring_loop(ahead, now):
                ahead(0, 0)
                with act.Fori(0, NI - 1) as it:
                    for k in range(R):
                        ahead(it * R + (k + 1), k + 1)
                        now(it * R + k)
                for k in range(R):
                    if k < R - 1:
                        ahead(NG - R + k + 1, k + 1)
                    now(NG - R + k)

            def copy_attrs(g, k):
                act.wait_ge(s["attrs_turned"], g + 1)
                act.activation(attrT[:, k % 2, :], T2[:, 512 * (k % 2):512 * (k % 2) + P], ACT.Copy).then_inc(
                    s["attrs_copied"], 1)

            def exp_messages(g, k):
                act.wait_ge(s["exp_in"], g + 1)
                act.activation(msg_u[k % 2], msg_u[k % 2], ACT.Exp).then_inc(s["exp_out"], 1)

            def invert(g):
                act.wait_ge(s["inverse_in"], g + 1)
                reciprocal(msg_r, msg_n, g + 1)

            def message_step(g, k, more=True):
                if more:
                    copy_attrs(g + 2, k + 2)
                invert(g + 1)
                if more:
                    exp_messages(g + 2, k + 2)

            copy_attrs(0, 0)
            exp_messages(0, 0)
            copy_attrs(1, 1)
            invert(0)
            exp_messages(1, 1)
            with act.Fori(0, NI - 1) as it:
                for k in range(R):
                    message_step(it * R + k, k)
            for k in range(R - 1):
                message_step(NG - R + k, k, k < R - 2)

            act.wait_ge(s["acc_added"], acc_total(MESSAGES))
            q = st[MESSAGES]
            with act.Fori(0, NCH) as it:
                act.activation(chunkT[0:M1, :], acc_chunk(M1, it), ACT.Copy).then_inc(q["acc_copied"], 1)
                for m in range(2):
                    act.wait_ge(q["capped"], it * 2 + (m + 1))
                    act.activation(hid[:, m, :], hid[:, m, :], ACT.Exp).then_inc(q["exp"], 1)
                for m in range(2):
                    act.wait_ge(s["inverse_in"], it * 2 + (NG + m + 1))
                    reciprocal(tmp[:, 1, :], tmp[:, 0, :], it * 2 + (NG + m + 1))
                root(small[:, 5:7, :], small[:, 2:4, :], it + (ROOTS[MESSAGES] + 1))
                act.wait_ge(q["turned"], it + 1)
                act.sem_inc(s["act_started"], 1)
                act.activation(acc_chunk(D, it), H2[0:D, 0:CW], ACT.Copy).then_inc(q["taken"], 1)

            if stop >= 1:
                act.wait_ge(s["acc_added"], acc_total(HOP1))
                q = st[HOP1]
                with act.Fori(0, NCH) as it:
                    act.activation(chunkT[0:D, :], acc_chunk(D, it), ACT.Copy).then_inc(q["acc_copied"], 1)
                    act.wait_ge(q["turned"], it + 1)
                    act.sem_inc(s["act_started"], 1)
                    act.activation(acc_chunk(D, it), H2[0:D, 0:CW], ACT.Copy).then_inc(q["taken"], 1)
                act.wait_ge(s["acc_added"], acc_total(HOP2))
                act.wait_ge(s["zeros_ready"], 2)
                q = st[HOP2]
                with act.Fori(0, NCH) as it:
                    act.activation(chunkT[0:D, :], acc_chunk(D, it), ACT.Copy).then_inc(q["acc_copied"], 1)
                    act.wait_ge(q["acc_copied"], it + 1)
                    act.sem_inc(s["act_started"], 1)
                    act.activation(acc_chunk(M1, it), hid[0:M1, 1, :], ACT.Copy).then_inc(s["zero_copied"], 1)
                    root(small[:, 5, :], small[:, 2, :], it + (ROOTS[HOP2] + 1))
                    act.wait_ge(q["turned"], it + 1)
                    act.sem_inc(s["act_started"], 1)
                    act.activation(zT[0:D, bass.ds(it * CW, CW)], H2[0:D, 0:CW], ACT.Copy).then_inc(q["taken"], 1)
            if stop >= 2:
                def copy_rows(g, k):
                    for h in range(2):
                        act.wait_ge(s["rows_turned"], g * 2 + (h + 1))
                        act.activation(rowsT[:, 512 * h:512 * (h + 1)], T2[0:D, 512 * h:512 * (h + 1)],
                                       ACT.Copy).then_inc(s["rows_copied"], 1)

                def exp_scores(g):
                    nx, = group_values(act, g, [1])
                    with act.If(nx > 0):
                        before, = group_values(act, g, [2])
                        with act.Fori(0, nx) as i:
                            act.wait_ge(s["again_turned"], before + i + 1)
                            act.sem_inc(s["act_started"], 1)
                            act.activation(rowsT[:, :], T2[0:D, :], ACT.Copy).then_inc(s["again_copied"], 1)
                    act.wait_ge(s["exp_in"], g + (NG + 1))
                    act.activation(score8[:, 1, :], score8[:, 0, :], ACT.Exp).then_inc(s["exp_out"], 1)

                ring_loop(copy_rows, exp_scores)
                act.wait_ge(s["acc_added"], acc_total(ATTENTION))
                q = st[ATTENTION]
                with act.Fori(0, NCH) as it:
                    act.activation(chunkT[0:M1, :], acc_chunk(M1, it), ACT.Copy).then_inc(q["acc_copied"], 1)
                    act.wait_ge(q["acc_copied"], it + 1)
                    act.sem_inc(s["act_started"], 1)
                    act.activation(acc_chunk(D, it), hid[0:D, 1, :], ACT.Copy).then_inc(s["zero_copied"], 1)
                    act.wait_ge(q["product"], it + 1)
            if stop >= 3:
                q = st[RELATIONS]
                act.sem_inc(s["high_copied"], 1)
                root(bn[:, 5, :], bn[:, 0, :], ROOTS["bn"] + 1)
                with act.Fori(0, NCH) as it:
                    root(small[:, 5, :], small[:, 2, :], it + (ROOTS[ATTENTION] + 1))
                    act.wait_ge(st[ATTENTION]["turned"], it + 1)
                    act.activation(chunkT[0:D, :], H2[0:D, 0:CW], ACT.Copy).then_inc(st[ATTENTION]["taken"], 1)
                    for b in range(CB):
                        act.wait_ge(s["product_ready"], it * (2 * CB) + (2 * b + 2))
                        act.wait_ge(s["y_free"], it * CB + (max(b, 1) + 1))
                        act.activation(ybuf[b % 2][:, 1024:2048], T2[:, :], ACT.Copy).then_inc(s["high_copied"], 1)
                act.wait_ge(s["acc_added"], acc_total(RELATIONS))
                with act.Fori(0, NCH) as it:
                    act.activation(chunkT[0:D, :], acc_chunk(D, it), ACT.Copy).then_inc(q["acc_copied"], 1)
                    act.wait_ge(q["product"], it + 1)
                    root(small[:, 5, :], small[:, 2, :], it + (ROOTS[RELATIONS] + 1))

        @block.tensor
        def _(pe):
            def turn_chunk():
                pe.sem_inc(s["pe_started"], 1)
                for b in range(CB):
                    last = pe.transpose(H2[0:D, P * b:P * (b + 1)], stage[:, D * b:D * (b + 1)], ident[:, :])
                return last

            def turn_back(m):
                pe.sem_inc(s["pe_started"], 1)
                for b in range(CB):
                    last = pe.transpose(A1[:, m * b:m * (b + 1)], chunkT[0:m, P * b:P * (b + 1)], ident[0:m, 0:m])
                return last

            pe.wait_ge(s["pool_const"], 6)
            pe.wait_ge(s["matrices_ready"], 1)
            pe.wait_ge(s["small_loaded"], 16 * SMALL_LOADS)
            pe.transpose(A1[0:D, 0:D], w3[:, 0, :], ident[0:D, 0:D])
            pe.transpose(A1[0:NBASE, 64:64 + NREL], coeff[:, :], ident[0:NREL, 0:NREL])
            for m in range(2):
                last = pe.matmul(A1[:, 128 + m:129 + m], w1[:, 1, P * m:P * (m + 1)], cols[0:D, 0:1],
                                 start=True, stop=True)
            last.then_inc(s["setup_pe"], 1)
            pe.wait_ge(s["setup_dve"], 2)
            for h in range(2):
                for c in range(C):
                    last = pe.transpose([S2, T2][h][:, c * P:c * P + HG],
                                        dst_f[:, h, :].rearrange("q (p c) -> q c p", c=C)[:, c, :],
                                        ident[0:HG, 0:HG])
            last.then_inc(s["setup_pe"], 1)
            pe.wait_ge(s["setup_dve"], 3)
            tri, count = prod[0:HG, 1, 0:HG], [score8[0:HG, 0, h:h + 1] for h in range(2)]
            pe.matmul(O1[0:HG, 0:1], tri, count[0], start=True, stop=True)
            pe.matmul(O1[0:HG, 1:2], tri, count[1], start=True, stop=False)
            pe.matmul(O1[0:HG, 1:2], ones[0:HG, 0:HG], count[0], start=False, stop=True)
            pe.matmul(O1[0:HG, 2:3], ones[0:HG, 0:HG], count[0], start=True, stop=False)
            pe.matmul(O1[0:HG, 2:3], ones[0:HG, 0:HG], count[1], start=False, stop=True).then_inc(s["setup_pe"], 1)
            pe.wait_ge(s["x_loaded"], 48)
            pe.wait_ge(s["setup_dve"], 6)
            for k in range(D * D // 512):
                if k:
                    pe.wait_ge(s["relw_ready"], k)
                pe.matmul(A1[0:NREL, :], coeffT[:, :], basis[:, 512 * k:512 * (k + 1)], start=True,
                          stop=True).then_inc(s["setup_pe"], 1)
            with pe.Fori(0, NCH) as it:
                pe.wait_ge(s["init_staged"], it + 1)
                turn_chunk().then_inc(s["init_turned"], 1)
                pe.wait_ge(s["init_copied"], it + 1)
            pe.wait_ge(s["group_loaded"], 16)

            def ring_loop(ahead, now, by):
                for k in range(by):
                    ahead(k, k, 0)
                with pe.Fori(0, NI - 1) as it:
                    for k in range(R):
                        ahead(it * R + (k + by), (k + by) % R, it + (k + by) // R)
                        now(it * R + k, k, it)
                for k in range(R):
                    if k < R - by:
                        ahead(NG - R + k + by, k + by, NI - 1)
                    now(NG - R + k, k, NI - 1)

            def window_sum(p, lhs, width, wait_input):
                def now(g, k, it):
                    nx, = group_values(pe, g, [1])
                    wait_input(g, k, it)
                    pe.wait_ge(s["onehot_ready"], g + (p * (NG + 1) + 1))
                    pe.wait_ge(s["acc_added"], g + (p * NG + R - 1))
                    o = [A1, O1][k % 2][0:width, 0:W]
                    for c in range(C):
                        last = pe.matmul(o, lhs(k, c), onehot[:, k % 2, c, :], start=(c == 0), stop=(c == C - 1))
                    last.then_inc(s["window_summed"], 1)
                    with pe.If(nx > 0):
                        before, total = group_values(pe, g, [2, 3])
                        with pe.Fori(0, nx) as i:
                            pe.wait_ge(s["extra_ready"], before + total * p + i + 1)
                            for c in range(C):
                                last = pe.matmul(H2[0:width, 512:512 + W], lhs(k, c), prod[:, c, :], start=(c == 0),
                                                 stop=(c == C - 1))
                            last.then_inc(s["extra_summed"], 1)
                return now

            def mix_attrs(g, k, it):
                at = slice(512 * (k % 2), 512 * (k % 2) + 512)
                pe.wait_ge(attr_loaded[k], it * 16 + 16)
                pe.transpose(T2[:, at.start:at.start + P], attrs[:, k, :], ident[:, :]).then_inc(
                    s["attrs_turned"], 1)
                pe.matmul(S2[:, at], ones[0:1, :], rowb[0:1, 0, :], start=True, stop=False)
                pe.wait_ge(s["attrs_copied"], g + 1)
                pe.matmul(S2[:, at], attrT[:, k % 2, :], attrw[:, :], start=False, stop=True).then_inc(
                    s["attrs_mixed"], 1)

            ring_loop(mix_attrs, window_sum(MESSAGES, lambda k, c: msg[:, c, :], M1,
                                            lambda g, k, it: pe.wait_ge(s["msg_ready"], g + 1)), 2)

            q = st[MESSAGES]
            with pe.Fori(0, NCH) as it:
                pe.wait_ge(q["acc_copied"], it + 1)
                for m in range(2):
                    for j in range(2):
                        last = pe.matmul([S2, T2][m][:, 512 * j:512 * j + HALF], w1[:, 0, P * m:P * (m + 1)],
                                         chunkT[0:D, HALF * j:HALF * (j + 1)], start=True, stop=True)
                    last.then_inc(q["hidden"], 1)
                turn_back(M1).then_inc(q["counts"], 1)
                pe.matmul(O1[:, 0:CD], ones[0:1, :], rowb[0:1, 1, 0:CD], start=True, stop=False,
                          skip_group_check=True)
                pe.wait_ge(q["mish"], it + 1)
                for b in range(CB):
                    for m in range(2):
                        last = pe.matmul(O1[:, D * b:D * (b + 1)], hid[:, m, P * b:P * (b + 1)], w2[:, m, :],
                                         start=False, stop=(b == CB - 1 and m == 1), skip_group_check=True)
                last.then_inc(q["product"], 1)
                pe.wait_ge(q["staged"], it + 1)
                turn_chunk().then_inc(q["turned"], 1)
                pe.wait_ge(q["taken"], it + 1)

            def hop(p):
                now = window_sum(p, lambda k, c: rows[:, k, c, 0:D], D,
                                 lambda g, k, it: pe.wait_ge(gathered[k], it * (C * 16) + (p * NI + 1) * (C * 16)))
                with pe.Fori(0, NI) as it:
                    for k in range(R):
                        now(it * R + k, k, it)

            if stop >= 1:
                for p in (HOP1, HOP2):
                    hop(p)
                    q = st[p]
                    with pe.Fori(0, NCH) as it:
                        pe.wait_ge(q["acc_copied"], it + 1)
                        if p == HOP1:
                            turn_back(D).then_inc(q["product"], 1)
                        else:
                            for b in range(CB):
                                last = pe.matmul(A1[:, D * b:D * (b + 1)], chunkT[0:D, P * b:P * (b + 1)],
                                                 w3[:, 1, :], start=True, stop=True)
                            last.then_inc(q["product"], 1)
                        pe.wait_ge(q["staged"], it + 1)
                        turn_chunk().then_inc(q["turned"], 1)
                        pe.wait_ge(q["taken"], it + 1)
            if stop >= 2:
                def score(g, k, it):
                    w, = group_values(pe, g, [0])
                    pe.wait_ge(gathered[k], it * (C * 16) + (ATTENTION * NI + 1) * (C * 16))
                    pe.sem_inc(s["pe_started"], 1)
                    for c in range(C):
                        ins = pe.transpose(T2[0:D, P * c:P * (c + 1)], rows[:, k, c, 0:D], ident[:, :])
                        if c % 4 == 3:
                            ins.then_inc(s["rows_turned"], 1)
                    pe.wait_ge(s["scores_read"], g + 1)
                    for c in range(C):
                        if c % 4 == 0:
                            pe.wait_ge(s["rows_copied"], g * 2 + (c // 4 + 1))
                            pe.sem_inc(s["pe_started"], 1)
                        last = pe.matmul(S2[:, P * c:P * (c + 1)], rowsT[:, P * c:P * (c + 1)],
                                         zT[0:D, bass.ds(w, W)], start=True, stop=True)
                    last.then_inc(s["scored"], 1)

                def score_further(g, k, it):
                    nx, = group_values(pe, g, [1])
                    with pe.If(nx > 0):
                        w, before = group_values(pe, g, [0, 2])
                        with pe.Fori(0, nx) as i:
                            for c in range(C):
                                ins = pe.transpose(T2[0:D, P * c:P * (c + 1)], rows[:, k, c, 0:D], ident[:, :])
                            ins.then_inc(s["again_turned"], 1)
                            pe.wait_ge(s["again_copied"], before + i + 1)
                            pe.wait_ge(s["score_extra_ready"], before + i + 1)
                            pe.sem_inc(s["pe_started"], 1)
                            for c in range(C):
                                last = pe.matmul(H2[:, P * c:P * (c + 1)], rowsT[:, P * c:P * (c + 1)],
                                                 zT[0:D, further(pe, w, i)], start=True, stop=True)
                            last.then_inc(s["score_extra_summed"], 1)
                    pe.wait_ge(s["msg_ready"], g + (NG + 1))

                ring_loop(score, window_sum(ATTENTION, lambda k, c: msg[:, c, :], M1, score_further), 1)
                q = st[ATTENTION]
                with pe.Fori(0, NCH) as it:
                    pe.wait_ge(q["acc_copied"], it + 1)
                    turn_back(M1).then_inc(q["product"], 1)
                    pe.wait_ge(q["counts"], it + 1)
            if stop >= 3:
                for k in range(2):
                    pe.wait_ge(s["bn_sum_ready"], k + 1)
                    pe.matmul(O1[:, 0:CD], ones[:, :], hid[:, 0, 0:CD], start=True, stop=True).then_inc(
                        s["bn_summed"], 1)
                with pe.Fori(0, NCH) as it:
                    pe.wait_ge(q["staged"], it + 1)
                    turn_chunk().then_inc(q["turned"], 1)
                    pe.wait_ge(q["taken"], it + 1)
                    for b in range(CB):
                        last = pe.matmul(A1[:, D * b:D * (b + 1)], chunkT[0:D, P * b:P * (b + 1)], w3[:, 2, :],
                                         start=True, stop=True)
                    last.then_inc(q["hidden"], 1)
                    for b in range(CB):
                        for m, free in enumerate(("low_copied", "high_copied")):
                            pe.wait_ge(s[free], it * CB + (b + 1))
                            for j in range(2):
                                last = pe.matmul([S2, T2][m][:, 512 * j:512 * (j + 1)],
                                                 chunkT[0:D, P * b:P * (b + 1)],
                                                 relw[:, :, :].rearrange("p r d -> p (r d)")[
                                                     :, 1024 * m + 512 * j:1024 * m + 512 * (j + 1)],
                                                 start=True, stop=True)
                            last.then_inc(s["product_ready"], 1)
                hop(RELATIONS)
                q = st[RELATIONS]
                with pe.Fori(0, NCH) as it:
                    pe.wait_ge(q["acc_copied"], it + 1)
                    turn_back(D).then_inc(q["product"], 1)
                    pe.wait_ge(q["counts"], it + 1)

        @block.vector
        def _(dve):
            steps = Steps(dve, s["dve_steps"])
            link = steps.link
            tt, ts, stt = dve.tensor_tensor, dve.tensor_scalar, dve.scalar_tensor_tensor

            def by_node(t):
                return t.unsqueeze(2).to_broadcast([P, CB, D])

            def by_feature(t):
                return t.unsqueeze(1).to_broadcast([P, CB, D])

            def nodes(t, it):
                return t[:, bass.ds(it * CB, CB)]

            dve.memset(src_i, 0).then_inc(s["pads_ready"], 1)
            dve.memset(dst_i, N).then_inc(s["pads_ready"], 1)
            dve.memset(typ_i, 0).then_inc(s["pads_ready"], 1)
            dve.memset(xn[:, NB - 1, :], 0.0).then_inc(s["pads_ready"], 1)
            dve.memset(attrw[:, :], 0.0).then_inc(s["weights_zero"], 1)
            dve.memset(ones[:, :], 1.0).then_inc(s["matrices_ready"], 1)
            link(dve.memset(cols[:, 6:7], 2.0))
            link(dve.memset(msg[:, :, :], 1.0))
            link(dve.memset(rows[:, :, :, :], 1.0))
            link(dve.memset(gtab[:, :, :], 0))
            link(dve.memset(dstrel[:, NG, :], 0.0))
            dve.wait_ge(s["iota_ready"], 1)
            link(dve.tensor_copy(iota[:, :], prod[:, 0, :].bitcast(I32)))
            dve.wait_ge(s["small_loaded"], 16 * SMALL_LOADS)
            ts(cols[0:D, 3:4], cols[0:D, 3:4], 1.0, None, ALU.add).then_inc(s["setup_dve"], 1)

            dve.wait_ge(s["edges_loaded"], 16 * 9)
            link(dve.tensor_copy(dst_f, dst_i))
            lo, hi, span = (small[0:HG, k, 0:2] for k in range(3))
            link(dve.tensor_reduce(lo, dst_f, AX, ALU.min))
            link(dve.tensor_reduce(hi, dst_f, AX, ALU.max))
            link(tt(span, hi, lo, ALU.subtract))
            link(ts(dst_f[:, 0, :], dst_f[:, 0, :], small[0:HG, 0, 0:1], None, ALU.subtract))
            ts(dst_f[:, 1, :], dst_f[:, 1, :], small[0:HG, 0, 1:2], None, ALU.subtract).then_inc(s["setup_dve"], 1)
            link(dve.tensor_copy(gtab[0:HG, :, 0], lo))
            link(dve.tensor_copy(gtab[0:HG, :, 1], span))
            link(ts(gtab[0:HG, :, 1], gtab[0:HG, :, 1], W.bit_length() - 1, None, ALU.logical_shift_right))
            dve.tensor_copy(score8[0:HG, 0, 0:2], gtab[0:HG, :, 1]).then_inc(s["setup_dve"], 1)
            dve.wait_ge(s["setup_pe"], 1)
            dve.tensor_copy(w3[:, 1, :], A1[0:D, 0:D]).then_inc(s["setup_dve"], 1)
            dve.tensor_copy(coeffT[:, :], A1[0:NBASE, 64:64 + NREL]).then_inc(s["setup_dve"], 1)
            tt(cols[:, 4:6], A1[:, 128:130], cols[:, 1:3], ALU.add).then_inc(s["setup_dve"], 1)
            dve.wait_ge(s["setup_pe"], 2)
            for h in range(2):
                link(dve.tensor_copy(dstrel[:, HG * h:HG * (h + 1), :].rearrange("p q c -> p c q"),
                                     [S2, T2][h][:, :].rearrange("p (c q) -> p c q", q=P)[:, :, 0:HG]))
            dve.wait_ge(s["setup_pe"], 3)
            link(dve.tensor_copy(gtab[0:HG, :, 2], O1[0:HG, 0:2]))
            link(dve.tensor_copy(gtab[0:HG, 0, 3:4], O1[0:HG, 2:3]))
            dve.tensor_copy(gtab[0:HG, 1, 3:4], O1[0:HG, 2:3]).then_inc(s["group_ready"], 1)
            dve.wait_ge(s["index_stored"], 16)
            stt(typ_i, src_i, float(NREL), typ_i, ALU.mult, ALU.add).then_inc(s["rel_index_ready"], 1)
            for k in range(D * D // 512):
                dve.wait_ge(s["setup_pe"], 4 + k)
                dve.tensor_copy(relw_flat[:, 512 * k:512 * (k + 1)], A1[0:NREL, :]).then_inc(s["relw_ready"], 1)
            link(dve.memset(acc[D:M1, :], 0.0))
            link(dve.memset(acc[0:D, NP:NACC], 0.0))
            dve.wait_ge(s["init_copied"], NCH)
            dve.wait_ge(s["group_loaded"], 16)
            dve.sem_inc(s["acc_added"], R)
            steps.end(0) if steps.per else None
            steps.done, steps.at = steps.at, 0

            def build_onehot(g, half):
                at = dstrel[:, bass.ds(g, 1), :].rearrange("p a c -> p (a c)")
                tt(onehot[:, half, :, :], iota[:, :].unsqueeze(1).to_broadcast([P, C, W]),
                   at.unsqueeze(2).to_broadcast([P, C, W]), ALU.is_equal).then_inc(s["onehot_ready"], 1)

            def further_onehot(ready):
                dve.drain()
                ts(dx[:, :], dx[:, :], -float(W), None, ALU.add)
                dve.drain()
                return tt(prod[:, :, :], iota[:, :].unsqueeze(1).to_broadcast([P, C, W]),
                          dx[:, :].unsqueeze(2).to_broadcast([P, C, W]), ALU.is_equal)

            def add_windows(p, g, k, width, w, nx):
                with dve.If(nx > 0):
                    before, total = group_values(dve, g, [2, 3])
                    dve.tensor_copy(dx[:, :], dstrel[:, bass.ds(g, 1), :].rearrange("p a c -> p (a c)"))
                    with dve.Fori(0, nx) as i:
                        further_onehot(None).then_inc(s["extra_ready"], 1)
                        dve.drain()
                        dve.wait_ge(s["extra_summed"], before + total * p + i + 1)
                        at = acc[0:width, further(dve, w, i)]
                        tt(at, at, H2[0:width, 512:512 + W], ALU.add)
                    dve.drain()
                dve.wait_ge(s["window_summed"], g + (p * NG + 1))
                dve.wait_ge(s["acc_added"], g + (p * NG + R))
                at = acc[0:width, bass.ds(w, W)]
                tt(at, at, [A1, O1][k % 2][0:width, 0:W], ALU.add).then_inc(s["acc_added"], 1)

            def pass_loop(p, per, body):
                build_onehot(0, 0)
                with dve.Fori(0, NI) as it:
                    steps.turn(it, per * R)
                    for k in range(R):
                        w, nx = group_values(dve, it * R + k, [0, 1])
                        body(it * R + k, k, it, w, nx)
                steps.end(NI)
                dve.wait_ge(s["acc_added"], acc_total(p))

            def newton(n, r, a):
                link(stt(a, n, 2.0, r, ALU.add, ALU.mult))
                link(stt(a, a, -2.0, r, ALU.add, ALU.mult))
                return stt(a, n, -1.0, a, ALU.mult, ALU.mult)

            def message_inputs(g, k, it):
                v, u = msg_v[k % 2], msg_u[k % 2]
                dve.wait_ge(s["attrs_mixed"], g + 1)
                dve.wait_ge(gathered[k], it * (C * 16) + C * 16)
                link(tt(blocks(v), blocks(S2[:, 512 * (k % 2):512 * (k % 2 + 1)]), rows[:, k, :, 0:D], ALU.add))
                ts(u, v, MISH_CAP, None, ALU.min).then_inc(s["exp_in"], 1)

            def numerator(g, k):
                u = msg_u[k % 2]
                dve.wait_ge(s["exp_out"], g + 1)
                stt(msg_n, u, 2.0, u, ALU.add, ALU.mult).then_inc(s["inverse_in"], 1)

            def mish_factor(g, k):
                dve.wait_ge(s["inverse_out"], g + 1)
                link(newton(msg_n, msg_r, msg_u[k % 2]))

            def message(k):
                tt(msg[:, :, 0:D], blocks(msg_u[k % 2]), blocks(msg_v[k % 2]), ALU.mult).then_inc(s["msg_ready"], 1)

            def message_step(g, k, it, more=True):
                w, nx = group_values(dve, g, [0, 1])
                numerator(g + 1, k + 1)
                if more:
                    dve.wait_ge(s["msg_ready"], g + 1)
                    message_inputs(g + 2, (k + 2) % R, it + (k + 2) // R)
                mish_factor(g + 1, k + 1)
                dve.sem_inc(s["dve_started"], 1)
                add_windows(MESSAGES, g, k, M1, w, nx)
                build_onehot(g + 2, k % 2)
                message(k + 1)

            steps.turn(0, 1 + 1 + 3)
            message_inputs(0, 0, 0)
            numerator(0, 0)
            message_inputs(1, 1, 0)
            mish_factor(0, 0)
            build_onehot(0, 0)
            build_onehot(1, 1)
            message(0)
            steps.end(1)
            with dve.Fori(0, NI - 1) as it:
                steps.turn(it, 4 * R)
                for k in range(R):
                    message_step(it * R + k, k, it)
            steps.end(NI - 1)
            steps.turn(0, 3 * (R - 1) + R - 2)
            for k in range(R - 1):
                message_step(NG - R + k, k, NI - 1, more=k < R - 2)
            steps.end(1)
            w, nx = group_values(dve, NG - 1, [0, 1])
            add_windows(MESSAGES, NG - 1, R - 1, M1, w, nx)
            dve.wait_ge(s["acc_added"], acc_total(MESSAGES))

            def root_newton(r, v, a):
                link(tt(a, v, r, ALU.mult))
                link(stt(a, a, -0.5, r, ALU.mult, ALU.mult))
                link(stt(r, a, 1.5, r, ALU.add, ALU.mult))
                return r

            def layernorm(y, it, roots):
                total, var = small[:, 0, :], small[:, 1, :]
                link(dve.tensor_reduce(total, y, AX, ALU.add))
                link(stt(centred, by_node(total), -1.0 / D, y, ALU.mult, ALU.add))
                link(tt(square, centred, centred, ALU.mult))
                link(dve.tensor_reduce(var, square, AX, ALU.add))
                ts(small[:, 2, :], var, 1.0 / D, EPS, ALU.mult, ALU.add).then_inc(s["root_in"], 1)
                dve.wait_ge(s["root_out"], it + (roots + 1))
                return root_newton(small[:, 5, :], small[:, 2, :], small[:, 0, :])

            y, centred = blocks(tmp[:, 0, 0:CD]), blocks(tmp[:, 0, CD:2 * CD])
            square = blocks(tmp[:, 1, 0:CD])
            out_stage = blocks(stage[:, :])

            q, p_now = st[MESSAGES], MESSAGES
            dve.wait_ge(s["init_copied"], NCH)
            with dve.Fori(0, NCH) as it:
                steps.turn(it, 7 + 3 + 1 + 7 + 3 + 2)
                halves = "p (q n) -> p q n"
                for m in range(2):
                    dve.wait_ge(q["hidden"], it * 2 + (m + 1))
                    ts(hid[:, m, :].rearrange(halves, q=2), [S2, T2][m][:, :].rearrange(halves, q=2)[:, :, 0:HALF],
                       cols[:, 4 + m:5 + m], MISH_CAP, ALU.add, ALU.min).then_inc(q["capped"], 1)
                for m in range(2):
                    dve.wait_ge(q["exp"], it * 2 + (m + 1))
                    u, n, r = hid[:, m, :], tmp[:, 0, :], tmp[:, 1, :]
                    stt(n, u, 2.0, u, ALU.add, ALU.mult).then_inc(s["inverse_in"], 1)
                    dve.wait_ge(s["inverse_out"], it * 2 + (NG + m + 1))
                    link(newton(n, r, u))
                    ins = stt(u.rearrange(halves, q=2), [S2, T2][m][:, :].rearrange(halves, q=2)[:, :, 0:HALF],
                              cols[:, 4 + m:5 + m], u.rearrange(halves, q=2), ALU.add, ALU.mult)
                    if m == 0:
                        link(ins)
                    else:
                        ins.then_inc(q["mish"], 1)
                dve.wait_ge(q["counts"], it + 1)
                count = A1[:, 0:M1 * CB].rearrange("p (b m) -> p b m", m=M1)[:, :, D]
                link(ts(small[:, 3, :], count, 1.0, None, ALU.add))
                link(ts(small[:, 4, :], count, 1.0, None, ALU.max))
                link(dve.reciprocal(nodes(cinv, it), small[:, 4, :]))
                dve.wait_ge(q["product"], it + 1)
                link(tt(y, blocks(O1[:, 0:CD]), nodes(xn, it), ALU.add))
                rstd = layernorm(y, it, ROOTS[p_now])
                root_newton(small[:, 6, :], small[:, 3, :], small[:, 0, :])
                link(dve.tensor_copy(nodes(dinv, it), small[:, 6, :]))
                link(tt(small[:, 7, :], rstd, small[:, 6, :], ALU.mult))
                tt(nodes(xn, it), centred, by_node(rstd), ALU.mult)
                dve.wait_ge(q["stage_free"], it + 1)
                tt(out_stage, centred, by_node(small[:, 7, :]), ALU.mult).then_inc(q["staged"], 1)
                dve.wait_ge(q["taken"], it + 1)
            steps.end(NCH)

            if stop >= 1:
                def hop_sum(p):
                    def body(g, k, it, w, nx):
                        build_onehot(g + 1, (k + 1) % 2)
                        add_windows(p, g, k, D, w, nx)
                    return body

                pass_loop(HOP1, 0, hop_sum(HOP1))
                q = st[HOP1]
                with dve.Fori(0, NCH) as it:
                    steps.turn(it, 1)
                    link(tt(small[:, 0, :], nodes(dinv, it), nodes(dinv, it), ALU.mult))
                    dve.wait_ge(q["product"], it + 1)
                    dve.wait_ge(q["stage_free"], it + 1)
                    tt(out_stage, blocks(A1[:, 0:CD]), by_node(small[:, 0, :]), ALU.mult).then_inc(q["staged"], 1)
                    dve.wait_ge(q["taken"], it + 1)
                steps.end(NCH)
                pass_loop(HOP2, 0, hop_sum(HOP2))
                dve.wait_ge(s["relw_loaded"], 16)
                dve.memset(zT[0:D, NP:NACC], 0.0).then_inc(s["zeros_ready"], 1)
                dve.memset(hid[:, 1, :], 0.0).then_inc(s["zeros_ready"], 1)
                q, p_now = st[HOP2], HOP2
                with dve.Fori(0, NCH) as it:
                    steps.turn(it, 3 + 7)
                    dve.wait_ge(q["product"], it + 1)
                    link(tt(y, blocks(A1[:, 0:CD]), by_node(nodes(dinv, it)), ALU.mult))
                    link(tt(y, y, nodes(xn, it), ALU.add))
                    link(tt(y, y, by_feature(bvec[:, 0, :]), ALU.add))
                    rstd = layernorm(y, it, ROOTS[p_now])
                    tt(nodes(xn, it), centred, by_node(rstd), ALU.mult)
                    dve.wait_ge(q["stage_free"], it + 1)
                    tt(out_stage, centred, by_node(rstd), ALU.mult).then_inc(q["staged"], 1)
                    dve.wait_ge(q["taken"], it + 1)
                steps.end(NCH)
            if stop >= 2:
                dve.sem_inc(s["scores_read"], 1)

                def attention(g, k, it, w, nx):
                    dve.wait_ge(s["scored"], g + 1)
                    dve.wait_ge(s["onehot_ready"], g + (ATTENTION * (NG + 1) + 1))
                    tt(prod[:, :, :], onehot[:, k % 2, :, :], S2[:, :].rearrange("p (c n) -> p c n", n=W),
                       ALU.mult).then_inc(s["scores_read"], 1)
                    dve.wait_ge(s["scores_read"], g + 2)
                    link(dve.tensor_reduce(score8[:, 0, :], prod[:, :, :], AX, ALU.add))
                    dve.sem_inc(s["dve_started"], 1)
                    with dve.If(nx > 0):
                        before, = group_values(dve, g, [2])
                        dve.tensor_copy(dx[:, :], dstrel[:, bass.ds(g, 1), :].rearrange("p a c -> p (a c)"))
                        with dve.Fori(0, nx) as i:
                            further_onehot(None).then_inc(s["score_extra_ready"], 1)
                            dve.drain()
                            dve.wait_ge(s["score_extra_summed"], before + i + 1)
                            tt(prod[:, :, :], prod[:, :, :], H2[:, :].rearrange("p (c n) -> p c n", n=W), ALU.mult)
                            dve.drain()
                            dve.tensor_reduce(score8[:, 2, :], prod[:, :, :], AX, ALU.add)
                            dve.drain()
                            tt(score8[:, 0, :], score8[:, 0, :], score8[:, 2, :], ALU.add)
                        dve.drain()
                    dve.sem_inc(s["exp_in"], 1)
                    dve.wait_ge(s["exp_out"], g + (NG + 1))
                    link(ts(score8[:, 3, :], score8[:, 1, :], 1.0, None, ALU.max))
                    tt(msg[:, :, :], rows[:, k, :, :], score8[:, 3, :].unsqueeze(2).to_broadcast([P, C, M1]),
                       ALU.mult).then_inc(s["msg_ready"], 1)
                    build_onehot(g + 1, (k + 1) % 2)
                    add_windows(ATTENTION, g, k, M1, w, nx)

                pass_loop(ATTENTION, 2, attention)
                q = st[ATTENTION]
                hsum = hid[:, 0, 0:CD]
                steps.turn(0, 0)
                link(dve.memset(hsum, 0.0))
                steps.done, steps.at = steps.done + steps.at, 0
                with dve.Fori(0, NCH) as it:
                    steps.turn(it, 4)
                    dve.wait_ge(q["product"], it + 1)
                    sums = A1[:, 0:M1 * CB].rearrange("p (b m) -> p b m", m=M1)
                    link(ts(small[:, 0, :], sums[:, :, D], TINY, None, ALU.max))
                    link(dve.reciprocal(small[:, 1, :], small[:, 0, :]))
                    link(tt(small[:, 2, :], small[:, 1, :], nodes(valid, it), ALU.mult))
                    ins = tt(nodes(hn, it), sums[:, :, 0:D], by_node(small[:, 2, :]), ALU.mult)
                    ins.then_inc(q["counts"], 1)
                    dve.wait_ge(q["counts"], it + 1)
                    link(tt(blocks(hsum), blocks(hsum), nodes(hn, it), ALU.add))
                steps.end(NCH)
            if stop >= 3:
                total, mean, scale, shift, sq = (bn[:, j, :] for j in range(5))
                steps.turn(0, 0)

                def column_sums(k):
                    dve.sem_inc(s["bn_sum_ready"], 1)
                    dve.wait_ge(s["bn_summed"], k + 1)
                    link(dve.tensor_reduce(total, O1[:, 0:CD].rearrange("p (b d) -> p d b", d=D), AX, ALU.add))

                column_sums(0)
                link(ts(mean, total, 1.0 / N, None, ALU.mult))
                link(dve.memset(hsum, 0.0))
                steps.done, steps.at = steps.done + steps.at, 0
                with dve.Fori(0, NCH) as it:
                    steps.turn(it, 3)
                    link(tt(centred, nodes(hn, it), by_feature(mean), ALU.subtract))
                    link(tt(square, centred, centred, ALU.mult))
                    link(tt(blocks(hsum), blocks(hsum), square, ALU.add))
                steps.end(NCH)
                steps.turn(0, 0)
                column_sums(1)
                link(tt(sq, mean, mean, ALU.mult))
                link(stt(total, sq, -float(NPAD), total, ALU.mult, ALU.add))
                link(ts(total, total, 1.0 / N, EPS, ALU.mult, ALU.add))
                dve.sem_inc(s["root_in"], 1)
                dve.wait_ge(s["root_out"], ROOTS["bn"] + 1)
                root_newton(bn[:, 5, :], total, sq)
                link(tt(scale, bn[:, 5, :], bvec[:, 1, :], ALU.mult))
                link(tt(sq, mean, scale, ALU.mult))
                link(tt(shift, bvec[:, 2, :], sq, ALU.subtract))
                steps.done, steps.at = steps.done + steps.at, 0
                dve.sem_inc(s["low_copied"], 1)
                p_now = ATTENTION
                with dve.Fori(0, NCH) as it:
                    steps.turn(it, 3 + 7 + 1)
                    link(tt(y, nodes(hn, it), by_feature(scale), ALU.mult))
                    link(tt(y, y, by_feature(shift), ALU.add))
                    link(stt(y, y, 0.0, nodes(xn, it), ALU.max, ALU.add))
                    rstd = layernorm(y, it, ROOTS[p_now])
                    tt(out_stage, centred, by_node(rstd), ALU.mult).then_inc(q["staged"], 1)
                    dve.wait_ge(q["hidden"], it + 1)
                    link(tt(nodes(xn, it), out_stage, blocks(A1[:, 0:CD]), ALU.add))
                    tt(nodes(xn, it), nodes(xn, it), by_feature(bvec[:, 3, :]), ALU.add)
                    for b in range(CB):
                        dve.wait_ge(s["product_ready"], it * (2 * CB) + (2 * b + 1))
                        dve.wait_ge(s["y_free"], it * CB + (max(b, 1) + 1))
                        dve.tensor_copy(ybuf[b % 2][:, 0:1024], S2[:, :]).then_inc(s["low_copied"], 1)
                steps.end(NCH)
                pass_loop(RELATIONS, 0, hop_sum(RELATIONS))
                q, p_now = st[RELATIONS], RELATIONS
                with dve.Fori(0, NCH) as it:
                    steps.turn(it, 1 + 7)
                    dve.wait_ge(q["product"], it + 1)
                    tt(y, blocks(A1[:, 0:CD]), by_node(nodes(cinv, it)), ALU.mult).then_inc(q["counts"], 1)
                    dve.wait_ge(q["counts"], it + 1)
                    link(tt(y, y, nodes(xn, it), ALU.add))
                    rstd = layernorm(y, it, ROOTS[p_now])
                    tt(nodes(xn, it), centred, by_node(rstd), ALU.mult)
                steps.end(NCH)
            dve.drain().then_inc(s["x_final"], 1)


_INS = ['x', 'src', 'dst', 'edge_attr_16', 'edge_type_32', 'L0_gnn_globals_', 'L0_gnn_We_kernel', 'L0_gnn_We_bias',
        'L0_gnn_epsilon', 'L0_gnn_W1', 'L0_gnn_b1', 'L0_gnn_W2', 'L0_gnn_b2', 'L1_gnn_weight', 'L1_gnn_bias',
        'L2_gnn_gamma', 'L2_gnn_beta', 'L3_gnn_basis', 'L3_gnn_coeff', 'L3_gnn_self_weight', 'L3_gnn_bias']
STOP = 9


def kernel(**inputs):
    import numpy as np
    import concourse.bacc as bacc
    from concourse.bass_utils import run_bass_kernel_spmd

    nc = bacc.Bacc("TRN2", target_bir_lowering=False, num_devices=1)
    arrays, handles = {}, {}
    for name in _INS:
        arrays[f"in_{name}"] = np.ascontiguousarray(inputs[name])
        handles[name] = nc.dram_tensor(f"in_{name}", arrays[f"in_{name}"].shape,
                                       mybir.dt.from_np(arrays[f"in_{name}"].dtype), kind="ExternalInput").ap()
    out = nc.dram_tensor("out", (N, D), F32, kind="ExternalOutput").ap()
    gnn(nc, handles, out, STOP)
    return run_bass_kernel_spmd(nc, [arrays], core_ids=[0]).results[0]["out"]
```

```python
from contextlib import ExitStack

import concourse.bass as bass
from concourse import mybir

F32 = mybir.dt.float32
I32 = mybir.dt.int32
ALU = mybir.AluOpType
ACT = mybir.ActivationFunctionType
AX = mybir.AxisListType.X

P = 128
N, E, D = 12500, 200000, 64
DE = 16
H = 256
NREL, NBASE = 32, 30
EPS = 1e-5
TINY = 1e-30
MISH_CAP = 10.0

C = 8
GE = P * C
NG = -(-E // GE)
TAIL = E - (NG - 1) * GE
TAILP = TAIL // C
R = 4
NI = NG // R
HG = NG // 2
W = 128
M1 = D + 1

CB = 7
NB = -(-N // P)
NCH = NB // CB
CW = CB * P
CD = CB * D
NP = NB * P
NACC = NP + W
LASTN = N - (NB - 1) * P
NPAD = NP - N
HALF = CW // 2
YW = NREL * D
assert NB * D + 2 * YW + 2 * CW <= NACC and NCH % 2 == 0
assert NI * R == NG and HG * 2 == NG and NB == NCH * CB and TAILP * C == TAIL and R % 2 == 0

MESSAGES, HOP1, HOP2, ATTENTION, RELATIONS = range(5)


class Steps:

    def __init__(self, eng, sem):
        self.eng, self.sem, self.done, self.at, self.index, self.per = eng, sem, 0, 0, 0, 0

    def turn(self, index, per):
        self.index, self.per, self.at = index, per, 0

    def link(self, ins):
        ins.then_inc(self.sem, 1)
        self.at += 1
        self.eng.wait_ge(self.sem, self.index * self.per + (self.done + self.at))

    def end(self, turns):
        assert self.at == self.per, (self.at, self.per)
        self.done += turns * self.per
        self.index, self.per, self.at = 0, 0, 0


def gnn(nc, a, out, stop=9):
    with ExitStack() as ctx:
        def sb(name, shape, dt=F32):
            return ctx.enter_context(nc.sbuf_tensor(name, shape, dt))

        def sem(name):
            return ctx.enter_context(nc.semaphore(name))

        def psum(name, cols):
            return ctx.enter_context(nc.psum_tensor(name, [P, cols], F32))

        def scratch(name, shape, dt=F32):
            return nc.dram_tensor(name, shape, dt, kind="Internal").ap()

        table = {HOP1: scratch("hop1_table", (NP, D)), HOP2: scratch("hop2_table", (NP, D)),
                 ATTENTION: scratch("attention_table", (NP, D)),
                 RELATIONS: scratch("relation_table", (NP * NREL, D))}
        src_index = scratch("src_index", (NG * GE,), I32)
        rel_index = scratch("rel_index", (NG * GE,), I32)
        group_dram = scratch("group_dram", (NG, 4), I32)
        relw_dram = scratch("relw_dram", (NREL, D, D))

        acc = sb("acc", [P, NACC])
        zT = sb("zT", [P, NACC])
        xn = sb("xn", [P, NB, D])
        dstrel = sb("dstrel", [P, NG + 1, C])
        grow = sb("grow", [1, NG * 4], I32)
        idx = sb("idx", [P, R, C], I32)
        rows = sb("rows", [P, R, C, M1])
        attrs = sb("attrs", [P, R, C * DE])
        attrT = sb("attrT", [P, 2, P])
        msg = sb("msg", [P, C, M1])
        onehot = sb("onehot", [P, 2, C, W])
        prod = sb("prod", [P, C, W])
        rowsT = sb("rowsT", [D, C * P])
        score8 = sb("score8", [P, 4, C])
        dx = sb("dx", [P, C])
        chunkT = sb("chunkT", [P, CW])
        hid = sb("hid", [P, 2, CW])
        tmp = sb("tmp", [P, 2, CW])
        stage = sb("stage", [P, CD])
        small = sb("small", [P, 8, CB])
        gtab = sb("gtab", [P, 2, 4], I32)
        dinv = sb("dinv", [P, NB])
        cinv = sb("cinv", [P, NB])
        valid = sb("valid", [P, NB])
        ident = sb("ident", [P, P])
        iota = sb("iota", [P, W])
        ones = sb("ones", [P, P])
        attrw = sb("attrw", [P, C * D])
        rowb = sb("rowb", [1, 2, C * D])
        w1 = sb("w1", [D, 2, H])
        w2 = sb("w2", [P, 2, D])
        cols = sb("cols", [P, 8])
        bvec = sb("bvec", [P, 4, D])
        bn = sb("bn", [P, 6, D])
        w3 = sb("w3", [D, 3, D])
        coeff = sb("coeff", [NREL, NBASE])
        coeffT = sb("coeffT", [NBASE, NREL])
        relw = sb("relw", [P, NREL, D])

        def edge_view(k):
            return zT[0:HG, 2 * GE * k:2 * GE * (k + 1)].rearrange("p (h e) -> p h e", h=2)
        dst_i, dst_f = edge_view(0).bitcast(I32), edge_view(1)
        src_i, typ_i = edge_view(2).bitcast(I32), edge_view(3).bitcast(I32)
        basis = zT[0:NBASE, 8 * GE:8 * GE + D * D]
        relw_flat = zT[0:NREL, 0:D * D]
        hn = zT[:, 0:NB * D].rearrange("p (b d) -> p b d", d=D)
        xT = [zT[:, NB * D + 2 * YW + CW * k:NB * D + 2 * YW + CW * (k + 1)] for k in range(2)]
        xT_both = zT[:, NB * D + 2 * YW:NB * D + 2 * YW + 2 * CW]
        ybuf = [zT[:, NB * D + YW * k:NB * D + YW * (k + 1)] for k in range(2)]

        tmp_flat, hid_flat = (t[:, :, :].rearrange("p m n -> p (m n)") for t in (tmp, hid))
        def third(t, j):
            return t[:, C * D * j:C * D * (j + 1)]
        msg_v, msg_u = [third(tmp_flat, j) for j in range(2)], [third(hid_flat, j) for j in range(2)]
        msg_n, msg_r = third(tmp_flat, 2), third(hid_flat, 2)

        chunk_buf = [chunkT[0:M1, :], hid[0:M1, 0, :]]
        x_next = [hid[:, k, 0:CD] for k in range(2)]

        def blocks(t):
            return t.rearrange("p (b d) -> p b d", d=D)

        S2, T2, H2 = psum("S2", 1024), psum("T2", 1024), psum("H2", 1024)
        A1, O1 = psum("A1", 512), psum("O1", 512)

        names = """pool_const iota_ready small_loaded edges_loaded x_loaded pads_ready dve_steps
            weights_zero matrices_ready setup_pe setup_dve index_stored rel_index_ready group_ready group_stored
            group_loaded relw_ready relw_stored relw_loaded
            gather_started onehot_ready window_summed acc_added extra_ready extra_summed
            score_extra_ready score_extra_summed attrs_turned attrs_copied attrs_mixed exp_in exp_out msg_ready
            rows_turned rows_copied scored scores_read
            inverse_in inverse_out log_done root_log
            init_staged init_turned init_copied zeros_ready zero_copied x_final out_stored
            act_started pe_started dve_started root_in root_out product_ready low_copied high_copied y_free acc_zeroed zero_row bn_squared bn_summed padding_zero""".split()
        s = {n: sem(n) for n in names}
        idx_ready = [sem(f"idx_ready{k}") for k in range(R)]
        gathered = [sem(f"gathered{k}") for k in range(R)]
        attr_loaded = [sem(f"attr_loaded{k}") for k in range(R)]
        y_stored = [sem(f"y_stored{k}") for k in range(2)]
        st = {p: {n: sem(f"stage{p}_{n}") for n in ["acc_copied", "hidden", "capped", "exp", "mish", "counts", "product", "staged",
                                                    "stage_free", "turned", "taken", "stored"]} for p in range(5)}

        block = ctx.enter_context(nc.Block())

        def table_chunk(p, it):
            return table[p].rearrange("(i b p) d -> i p b d", b=CB, p=P)[bass.ds(it, 1)].rearrange(
                "a p b d -> (a p) b d")

        def chunk_loop(eng, body, steps=None, per=0, per_last=0):
            with eng.Fori(0, NCH // 2 - 1) as it:
                if steps:
                    steps.turn(it, 2 * per)
                body(it * 2, 0, True)
                body(it * 2 + 1, 1, True)
            if steps:
                steps.end(NCH // 2 - 1)
                steps.turn(0, per + per_last)
            body(NCH - 2, 0, True)
            body(NCH - 1, 1, False)
            if steps:
                steps.end(1)

        def one(view, g):
            return view[bass.ds(g, 1)].rearrange("a p c -> (a p) c")

        def acc_chunk(m, it):
            return acc[0:m, bass.ds(it * CW, CW)]

        def acc_total(p):
            return (p + 1) * NG + R

        src_v = src_index.rearrange("(g p c) -> g p c", p=P, c=C)
        rel_v = rel_index.rearrange("(g p c) -> g p c", p=P, c=C)
        attr_v = a["edge_attr_16"][0:(NG - 1) * GE].rearrange("(g p c) k -> g p (c k)", p=P, c=C)
        attr_tail = a["edge_attr_16"][(NG - 1) * GE:E].rearrange("(p c) k -> p (c k)", c=C)
        ROOTS = {MESSAGES: 0, HOP2: NCH, "bn": 2 * NCH, ATTENTION: 2 * NCH + 1, RELATIONS: 3 * NCH + 1}
        SMALL_LOADS = 3 * C + 2 + 2 + 1 + 4 + 3

        def group_values(eng, g, words):
            most = (N, NP // W, NG * NP // W, NG * NP // W)
            return [eng.value_load(grow[0:1, bass.ds(g * 4 + j, 1)], min_val=0, max_val=most[j]) for j in words]

        def further(eng, w, i):
            return bass.ds(nc.s_assert_within(w + i * W + W, W, NP, skip_runtime_bounds_check_because="further windows end with the last node"), W)

        @block.sync
        def _(sp):
            def edges(view, name):
                x = a[name]
                full = x[0:(NG - 1) * GE].rearrange("(q e) -> q e", e=GE)
                sp.dma_start(view[:, 0, :], full[0:HG]).then_inc(s["edges_loaded"], 16)
                sp.dma_start(view[0:HG - 1, 1, :], full[HG:NG - 1]).then_inc(s["edges_loaded"], 16)
                sp.dma_start(view[HG - 1:HG, 1, 0:TAIL],
                             x[(NG - 1) * GE:E].rearrange("(q e) -> q e", q=1)).then_inc(s["edges_loaded"], 16)

            sp.wait_ge(s["pads_ready"], 4)
            edges(src_i, "src")
            edges(dst_i, "dst")
            edges(typ_i, "edge_type_32")
            sp.dma_start(xn[:, 0:NB - 1, :], a["x"][0:(NB - 1) * P].rearrange("(b p) d -> p b d", p=P)).then_inc(
                s["x_loaded"], 16)
            sp.dma_start(xn[0:LASTN, NB - 1, :], a["x"][(NB - 1) * P:N]).then_inc(s["x_loaded"], 16)
            sp.dma_start(basis, a["L3_gnn_basis"].rearrange("b i o -> b (i o)")).then_inc(s["x_loaded"], 16)
            sp.wait_ge(s["edges_loaded"], 16 * 9)
            sp.dma_start(src_index.rearrange("(h q e) -> q h e", h=2, e=GE), src_i).then_inc(s["index_stored"], 16)
            sp.wait_ge(s["index_stored"], 16)
            sp.wait_ge(s["group_ready"], 1)
            sp.dma_start(group_dram.rearrange("(h q) w -> q h w", h=2), gtab[0:HG]).then_inc(s["group_stored"], 16)
            sp.wait_ge(s["group_stored"], 16)
            sp.dma_start(grow[:, :], group_dram.rearrange("g w -> (g w)").rearrange("(a n) -> a n", a=1)).then_inc(
                s["group_loaded"], 16)
            sp.wait_ge(s["rel_index_ready"], 1)
            sp.dma_start(rel_index.rearrange("(h q e) -> q h e", h=2, e=GE), typ_i).then_inc(s["index_stored"], 16)
            sp.wait_ge(s["relw_ready"], 8)
            sp.dma_start(relw_dram.rearrange("r i o -> r (i o)"), relw_flat).then_inc(s["relw_stored"], 16)
            sp.wait_ge(s["relw_stored"], 16)
            sp.dma_start(relw[0:D, :, :], relw_dram.rearrange("r i o -> i r o")).then_inc(s["relw_loaded"], 16)

            def edge_pass(p, view):
                attributes = p == MESSAGES
                for k in range(R):
                    if p:
                        sp.wait_ge(gathered[k], p * NI * C * 16)
                    if p == RELATIONS and k == 0:
                        sp.wait_ge(s["index_stored"], 32)
                    sp.dma_start(idx[:, k, :], view[k]).then_inc(idx_ready[k], 16)
                    if attributes:
                        sp.dma_start(attrs[:, k, :], attr_v[k]).then_inc(attr_loaded[k], 16)
                with sp.Fori(0, NI - 2) as it:
                    for k in range(R):
                        sp.wait_ge(gathered[k], it * (C * 16) + (p * NI + 1) * (C * 16))
                        sp.dma_start(idx[:, k, :], one(view, it * R + (R + k))).then_inc(idx_ready[k], 16)
                        if attributes:
                            sp.wait_ge(s["attrs_turned"], it * R + (k + 1))
                            sp.dma_start(attrs[:, k, :], one(attr_v, it * R + (R + k))).then_inc(attr_loaded[k], 16)
                for k in range(R):
                    g = NG - R + k
                    sp.wait_ge(gathered[k], (p * NI + NI - 1) * (C * 16))
                    sp.dma_start(idx[:, k, :], view[g]).then_inc(idx_ready[k], 16)
                    if attributes:
                        sp.wait_ge(s["attrs_turned"], g - R + 1)
                        if g < NG - 1:
                            sp.dma_start(attrs[:, k, :], attr_v[g]).then_inc(attr_loaded[k], 16)
                        else:
                            sp.dma_start(attrs[0:TAILP, k, :], attr_tail).then_inc(attr_loaded[k], 16)

            def store_table(p):
                q = st[p - 1]
                sp.sem_inc(q["stage_free"], 1)
                with sp.Fori(0, NCH) as it:
                    sp.wait_ge(q["staged"], it + 1)
                    sp.dma_start(table_chunk(p, it), blocks(stage[:, :])).then_inc(q["stored"], 16)
                    sp.wait_ge(q["stored"], it * 16 + 16)
                    sp.sem_inc(q["stage_free"], 1)

            edge_pass(MESSAGES, src_v)
            store_table(HOP1)
            if stop >= 1:
                edge_pass(HOP1, src_v)
                store_table(HOP2)
                edge_pass(HOP2, src_v)
            if stop >= 2:
                store_table(ATTENTION)
                edge_pass(ATTENTION, src_v)
            if stop >= 3:
                sp.sem_inc(s["y_free"], 2)
                y_rows = table[RELATIONS].rearrange("(n p r) d -> n p (r d)", p=P, r=NREL)

                def store_products(it, j):
                    sp.wait_ge(s["low_copied"], it * (4 * CB) + (2 * j + 4))
                    sp.wait_ge(s["high_copied"], it * (4 * CB) + (2 * j + 4))
                    sp.dma_start(one(y_rows, it * (2 * CB) + j), ybuf[j % 2]).then_inc(y_stored[j % 2], 16)
                    if j:
                        sp.wait_ge(y_stored[(j - 1) % 2], it * (16 * CB) + 16 * ((j - 1) // 2 + 1))
                        sp.sem_inc(s["y_free"], 1)

                store_products(0, 0)
                with sp.Fori(0, NCH // 2 - 1) as it:
                    for j in range(1, 2 * CB + 1):
                        store_products(it, j)
                for j in range(1, 2 * CB):
                    store_products(NCH // 2 - 1, j)
                sp.wait_ge(y_stored[1], 16 * (NB // 2))
                sp.sem_inc(s["y_free"], 1)
                edge_pass(RELATIONS, rel_v)
            sp.wait_ge(s["index_stored"], 32)
            sp.wait_ge(s["relw_loaded"], 16)
            sp.wait_ge(s["x_final"], 1)
            sp.dma_start(out[0:(NB - 1) * P].rearrange("(b p) d -> p b d", p=P), xn[:, 0:NB - 1, :]).then_inc(
                s["out_stored"], 16)
            sp.dma_start(out[(NB - 1) * P:N], xn[0:LASTN, NB - 1, :]).then_inc(s["out_stored"], 16)
            sp.wait_ge(s["out_stored"], 32)

        @block.gpsimd
        def _(pool):
            pool.iota(prod[:, 0, :].bitcast(I32), pattern=[[1, W]], base=0, channel_multiplier=0).then_inc(
                s["iota_ready"], 1)
            pool.memset(ident[:, :], 0.0).then_inc(s["pool_const"], 1)
            pool.memset(valid[:, :], 1.0).then_inc(s["pool_const"], 1)
            pool.memset(prod[:, 1, :], 1.0).then_inc(s["pool_const"], 1)
            pool.wait_ge(s["pool_const"], 3)
            pool.affine_select(out=ident[:, :], in_=ident[:, :], compare_op=ALU.not_equal, fill=1.0, base=0,
                               pattern=[[-1, P]], channel_multiplier=1).then_inc(s["pool_const"], 1)
            pool.affine_select(out=valid[:, :], in_=valid[:, :], compare_op=ALU.is_ge, fill=0.0, base=N - 1,
                               pattern=[[-P, NB]], channel_multiplier=-1).then_inc(s["pool_const"], 1)
            pool.affine_select(out=prod[:, 1, :], in_=prod[:, 1, :], compare_op=ALU.is_ge, fill=0.0, base=-1,
                               pattern=[[1, P]], channel_multiplier=-1).then_inc(s["pool_const"], 1)

            def edge_pass(p, tab):
                with pool.Fori(0, NI) as it:
                    for k in range(R):
                        pool.wait_ge(s["acc_added"], it * R + (p * NG + k + 1))
                        pool.wait_ge(idx_ready[k], it * 16 + (p * NI + 1) * 16)
                        pool.sem_inc(s["gather_started"], 1)
                        for c in range(C):
                            pool.indirect_dma_start(
                                out=rows[:, k, c, 0:D], out_offset=None, in_=tab,
                                in_offset=bass.IndirectOffsetOnAxis(ap=idx[:, k, c:c + 1], axis=0)).then_inc(
                                gathered[k], 16)

            edge_pass(MESSAGES, a["x"])
            for p in [HOP1, HOP2] * (stop >= 1) + [ATTENTION] * (stop >= 2):
                pool.wait_ge(st[p - 1]["stored"], 16 * NCH)
                edge_pass(p, table[p])
            if stop >= 3:
                pool.wait_ge(st[ATTENTION]["acc_copied"], NCH)
                pool.memset(acc[0:D, :], 0.0).then_inc(s["acc_zeroed"], 1)
                pool.wait_ge(s["y_free"], 2 + NB)
                edge_pass(RELATIONS, table[RELATIONS])

        @block.scalar
        def _(act):
            act.preload_act_table_set("natural_log_exp_and_others")
            loads = []

            def load(dst, src):
                act.dma_start(dst, src).then_inc(s["small_loaded"], 16)
                loads.append(1)

            act.wait_ge(s["weights_zero"], 1)
            for c in range(C):
                load(attrw[DE * c:DE * (c + 1), D * c:D * (c + 1)], a["L0_gnn_We_kernel"])
                load(rowb[0:1, 0, D * c:D * (c + 1)], a["L0_gnn_We_bias"].rearrange("(a d) -> a d", a=1))
                load(rowb[0:1, 1, D * c:D * (c + 1)], a["L0_gnn_b2"].rearrange("(a d) -> a d", a=1))
            load(w1[:, :, :], a["L0_gnn_W1"].rearrange("(t p) h -> p t h", t=2))
            load(w2[:, :, :], a["L0_gnn_W2"].rearrange("(t p) h -> p t h", t=2))
            with nc.allow_non_contiguous_dma(reason="columns of small vectors"):
                load(cols[0:D, 0:1], a["L0_gnn_globals_"].rearrange("a d -> d a"))
                load(cols[:, 1:3], a["L0_gnn_b1"].rearrange("(m p) -> p m", m=2))
            load(cols[0:D, 3:4], a["L0_gnn_epsilon"][0].partition_broadcast(D))
            for k, name in enumerate(["L1_gnn_bias", "L2_gnn_gamma", "L2_gnn_beta", "L3_gnn_bias"]):
                load(bvec[:, k, :], a[name].partition_broadcast(P))
            load(w3[:, 0, :], a["L1_gnn_weight"])
            load(w3[:, 2, :], a["L3_gnn_self_weight"])
            load(coeff[:, :], a["L3_gnn_coeff"])
            assert len(loads) == SMALL_LOADS

            act.wait_ge(s["setup_dve"], 1)
            act.wait_ge(s["x_loaded"], 48)
            with act.Fori(0, NCH) as it:
                act.activation(stage[:, :], xn[:, bass.ds(it * CB, CB), :].rearrange("p b d -> p (b d)"),
                               ACT.Copy).then_inc(s["init_staged"], 1)
                act.wait_ge(s["init_turned"], it + 1)
                act.sem_inc(s["act_started"], 1)
                act.activation(acc_chunk(D, it), H2[0:D, 0:CW], ACT.Identity, bias=0.0,
                               scale=cols[0:D, 3:4]).then_inc(s["init_copied"], 1)

            def root(out_, in_, value):
                act.wait_ge(s["root_in"], value)
                act.activation(out_, in_, ACT.Ln).then_inc(s["root_log"], 1)
                act.wait_ge(s["root_log"], value)
                act.activation(out_, out_, ACT.Exp, scale=-0.5).then_inc(s["root_out"], 1)

            def reciprocal(out_, in_, value):
                act.activation(out_, in_, ACT.Ln, bias=cols[:, 6:7]).then_inc(s["log_done"], 1)
                act.wait_ge(s["log_done"], value)
                act.activation(out_, out_, ACT.Exp, scale=-1.0).then_inc(s["inverse_out"], 1)

            def copy_attrs(g, k):
                act.wait_ge(s["attrs_turned"], g + 1)
                act.activation(attrT[:, k % 2, :], T2[:, 512 * (k % 2):512 * (k % 2) + P], ACT.Copy).then_inc(
                    s["attrs_copied"], 1)

            def exp_messages(g, k):
                act.wait_ge(s["exp_in"], g + 1)
                act.activation(msg_u[k % 2], msg_u[k % 2], ACT.Exp).then_inc(s["exp_out"], 1)

            def invert(g):
                act.wait_ge(s["inverse_in"], g + 1)
                reciprocal(msg_r, msg_n, g + 1)

            def message_step(g, k, more=True):
                if more:
                    copy_attrs(g + 2, k + 2)
                invert(g + 1)
                if more:
                    exp_messages(g + 2, k + 2)

            copy_attrs(0, 0)
            exp_messages(0, 0)
            copy_attrs(1, 1)
            invert(0)
            exp_messages(1, 1)
            with act.Fori(0, NI - 1) as it:
                for k in range(R):
                    message_step(it * R + k, k)
            for k in range(R - 1):
                message_step(NG - R + k, k, k < R - 2)

            act.wait_ge(s["acc_added"], acc_total(MESSAGES))
            q = st[MESSAGES]
            with act.Fori(0, NCH) as it:
                act.activation(chunkT[0:M1, :], acc_chunk(M1, it), ACT.Copy).then_inc(q["acc_copied"], 1)
                for m in range(2):
                    act.wait_ge(q["capped"], it * 2 + (m + 1))
                    act.activation(hid[:, m, :], hid[:, m, :], ACT.Exp).then_inc(q["exp"], 1)
                for m in range(2):
                    act.wait_ge(s["inverse_in"], it * 2 + (NG + m + 1))
                    reciprocal(tmp[:, 1, :], tmp[:, 0, :], it * 2 + (NG + m + 1))
                root(small[:, 5:7, :], small[:, 2:4, :], it + (ROOTS[MESSAGES] + 1))
                act.wait_ge(q["turned"], it + 1)
                act.sem_inc(s["act_started"], 1)
                act.activation(acc_chunk(D, it), H2[0:D, 0:CW], ACT.Copy).then_inc(q["taken"], 1)

            if stop >= 1:
                act.wait_ge(s["acc_added"], acc_total(HOP1))
                q = st[HOP1]
                with act.Fori(0, NCH) as it:
                    act.activation(chunkT[0:D, :], acc_chunk(D, it), ACT.Copy).then_inc(q["acc_copied"], 1)
                    act.wait_ge(q["turned"], it + 1)
                    act.sem_inc(s["act_started"], 1)
                    act.activation(acc_chunk(D, it), H2[0:D, 0:CW], ACT.Copy).then_inc(q["taken"], 1)
                act.wait_ge(s["acc_added"], acc_total(HOP2))
                act.wait_ge(s["zeros_ready"], 2)
                q = st[HOP2]
                with act.Fori(0, NCH) as it:
                    act.activation(chunkT[0:D, :], acc_chunk(D, it), ACT.Copy).then_inc(q["acc_copied"], 1)
                    act.wait_ge(q["acc_copied"], it + 1)
                    act.sem_inc(s["act_started"], 1)
                    act.activation(acc_chunk(M1, it), hid[0:M1, 1, :], ACT.Copy).then_inc(s["zero_copied"], 1)
                    root(small[:, 5, :], small[:, 2, :], it + (ROOTS[HOP2] + 1))
                    act.wait_ge(q["turned"], it + 1)
                    act.sem_inc(s["act_started"], 1)
                    act.activation(zT[0:D, bass.ds(it * CW, CW)], H2[0:D, 0:CW], ACT.Copy).then_inc(q["taken"], 1)
            if stop >= 2:
                def copy_rows(g):
                    for h in range(2):
                        act.wait_ge(s["rows_turned"], g * 2 + (h + 1))
                        act.activation(rowsT[:, 512 * h:512 * (h + 1)], T2[0:D, 512 * h:512 * (h + 1)],
                                       ACT.Copy).then_inc(s["rows_copied"], 1)

                def exp_scores(g):
                    act.wait_ge(s["exp_in"], g + (NG + 1))
                    act.activation(score8[:, 1, :], score8[:, 0, :], ACT.Exp).then_inc(s["exp_out"], 1)

                copy_rows(0)
                copy_rows(1)
                exp_scores(0)
                with act.Fori(0, NI - 1) as it:
                    for k in range(R):
                        copy_rows(it * R + (k + 2))
                        exp_scores(it * R + (k + 1))
                for k in range(R - 1):
                    if k < R - 2:
                        copy_rows(NG - R + k + 2)
                    exp_scores(NG - R + k + 1)
                act.wait_ge(s["acc_added"], acc_total(ATTENTION))
                q = st[ATTENTION]

                def copy_sums(n, k, more):
                    act.wait_ge(q["product"], n + 1)
                    act.sem_inc(s["act_started"], 1)
                    act.activation(chunk_buf[k], acc_chunk(M1, n), ACT.Copy).then_inc(q["acc_copied"], 1)

                chunk_loop(act, copy_sums)
            if stop >= 3:
                q = st[RELATIONS]
                act.sem_inc(s["high_copied"], 2)
                root(bn[:, 5, :], bn[:, 0, :], ROOTS["bn"] + 1)

                def take_features(n, k):
                    act.wait_ge(st[ATTENTION]["turned"], n + 1)
                    act.activation(xT[k][0:D, :], H2[0:D, 0:CW], ACT.Copy).then_inc(st[ATTENTION]["taken"], 1)

                def copy_high(n, k, more):
                    for b in range(CB):
                        for j in range(2):
                            act.wait_ge(s["product_ready"], n * (2 * CB) + (2 * b + j + 1))
                            if j == 0:
                                act.wait_ge(s["y_free"], n * CB + (b + 1))
                            act.activation(ybuf[(CB * k + b) % 2][:, 1024 + 512 * j:1024 + 512 * (j + 1)],
                                           T2[:, 512 * j:512 * (j + 1)], ACT.Copy).then_inc(s["high_copied"], 1)
                        if more and b == 3:
                            root(small[:, 5, :], small[:, 2, :], n + (ROOTS[ATTENTION] + 2))
                        if more and b == 5:
                            take_features(n + 1, 1 - k)

                root(small[:, 5, :], small[:, 2, :], ROOTS[ATTENTION] + 1)
                take_features(0, 0)
                chunk_loop(act, copy_high)
                act.wait_ge(s["acc_added"], acc_total(RELATIONS))
                with act.Fori(0, NCH) as it:
                    act.activation(chunkT[0:D, :], acc_chunk(D, it), ACT.Copy).then_inc(q["acc_copied"], 1)
                    act.wait_ge(q["product"], it + 1)
                    root(small[:, 5, :], small[:, 2, :], it + (ROOTS[RELATIONS] + 1))

        @block.tensor
        def _(pe):
            def turn_chunk():
                pe.sem_inc(s["pe_started"], 1)
                for b in range(CB):
                    last = pe.transpose(H2[0:D, P * b:P * (b + 1)], stage[:, D * b:D * (b + 1)], ident[:, :])
                return last

            def turn_back(m):
                pe.sem_inc(s["pe_started"], 1)
                for b in range(CB):
                    last = pe.transpose(A1[:, m * b:m * (b + 1)], chunkT[0:m, P * b:P * (b + 1)], ident[0:m, 0:m])
                return last

            pe.wait_ge(s["pool_const"], 6)
            pe.wait_ge(s["matrices_ready"], 1)
            pe.wait_ge(s["small_loaded"], 16 * SMALL_LOADS)
            pe.transpose(A1[0:D, 0:D], w3[:, 0, :], ident[0:D, 0:D])
            pe.transpose(A1[0:NBASE, 64:64 + NREL], coeff[:, :], ident[0:NREL, 0:NREL])
            for m in range(2):
                last = pe.matmul(A1[:, 128 + m:129 + m], w1[:, 1, P * m:P * (m + 1)], cols[0:D, 0:1],
                                 start=True, stop=True)
            last.then_inc(s["setup_pe"], 1)
            pe.wait_ge(s["setup_dve"], 2)
            for h in range(2):
                for c in range(C):
                    last = pe.transpose([S2, T2][h][:, c * P:c * P + HG],
                                        dst_f[:, h, :].rearrange("q (p c) -> q c p", c=C)[:, c, :],
                                        ident[0:HG, 0:HG])
            last.then_inc(s["setup_pe"], 1)
            pe.wait_ge(s["setup_dve"], 3)
            tri, count = prod[0:HG, 1, 0:HG], [score8[0:HG, 0, h:h + 1] for h in range(2)]
            pe.matmul(O1[0:HG, 0:1], tri, count[0], start=True, stop=True)
            pe.matmul(O1[0:HG, 1:2], tri, count[1], start=True, stop=False)
            pe.matmul(O1[0:HG, 1:2], ones[0:HG, 0:HG], count[0], start=False, stop=True)
            pe.matmul(O1[0:HG, 2:3], ones[0:HG, 0:HG], count[0], start=True, stop=False)
            pe.matmul(O1[0:HG, 2:3], ones[0:HG, 0:HG], count[1], start=False, stop=True).then_inc(s["setup_pe"], 1)
            pe.wait_ge(s["x_loaded"], 48)
            pe.wait_ge(s["setup_dve"], 6)
            for k in range(D * D // 512):
                if k:
                    pe.wait_ge(s["relw_ready"], k)
                pe.matmul(A1[0:NREL, :], coeffT[:, :], basis[:, 512 * k:512 * (k + 1)], start=True,
                          stop=True).then_inc(s["setup_pe"], 1)
            with pe.Fori(0, NCH) as it:
                pe.wait_ge(s["init_staged"], it + 1)
                turn_chunk().then_inc(s["init_turned"], 1)
                pe.wait_ge(s["init_copied"], it + 1)
            pe.wait_ge(s["group_loaded"], 16)

            def ring_loop(step):
                with pe.Fori(0, NI - 1) as it:
                    for k in range(R):
                        step(it * R + k, k, it, 2)
                for k in range(R):
                    step(NG - R + k, k, NI - 1, min(2, R - 1 - k))

            def window_sum(p, lhs, width, wait_input):
                def now(g, k, it):
                    nx, = group_values(pe, g, [1])
                    wait_input(g, k, it)
                    pe.wait_ge(s["onehot_ready"], g + (p * (NG + 1) + 1))
                    pe.wait_ge(s["acc_added"], g + (p * NG + R - 1))
                    o = [A1, O1][k % 2][0:width, 0:W]
                    for c in range(C):
                        last = pe.matmul(o, lhs(k, c), onehot[:, k % 2, c, :], start=(c == 0), stop=(c == C - 1))
                    last.then_inc(s["window_summed"], 1)
                    with pe.If(nx > 0):
                        before, total = group_values(pe, g, [2, 3])
                        with pe.Fori(0, nx) as i:
                            pe.wait_ge(s["extra_ready"], before + total * p + i + 1)
                            for c in range(C):
                                last = pe.matmul(H2[0:width, 512:512 + W], lhs(k, c), prod[:, c, :], start=(c == 0),
                                                 stop=(c == C - 1))
                            last.then_inc(s["extra_summed"], 1)
                return now

            def mix_attrs(g, k, it):
                at = slice(512 * (k % 2), 512 * (k % 2) + 512)
                pe.wait_ge(attr_loaded[k], it * 16 + 16)
                pe.transpose(T2[:, at.start:at.start + P], attrs[:, k, :], ident[:, :]).then_inc(
                    s["attrs_turned"], 1)
                pe.matmul(S2[:, at], ones[0:1, :], rowb[0:1, 0, :], start=True, stop=False)
                pe.wait_ge(s["attrs_copied"], g + 1)
                pe.matmul(S2[:, at], attrT[:, k % 2, :], attrw[:, :], start=False, stop=True).then_inc(
                    s["attrs_mixed"], 1)

            sum_messages = window_sum(MESSAGES, lambda k, c: msg[:, c, :], M1,
                                      lambda g, k, it: pe.wait_ge(s["msg_ready"], g + 1))

            def message_step(g, k, it, more):
                if more == 2:
                    mix_attrs(g + 2, (k + 2) % R, it + (k + 2) // R)
                sum_messages(g, k, it)

            mix_attrs(0, 0, 0)
            mix_attrs(1, 1, 0)
            ring_loop(message_step)

            q = st[MESSAGES]
            with pe.Fori(0, NCH) as it:
                pe.wait_ge(q["acc_copied"], it + 1)
                for m in range(2):
                    for j in range(2):
                        last = pe.matmul([S2, T2][m][:, 512 * j:512 * j + HALF], w1[:, 0, P * m:P * (m + 1)],
                                         chunkT[0:D, HALF * j:HALF * (j + 1)], start=True, stop=True)
                    last.then_inc(q["hidden"], 1)
                turn_back(M1).then_inc(q["counts"], 1)
                pe.matmul(O1[:, 0:CD], ones[0:1, :], rowb[0:1, 1, 0:CD], start=True, stop=False,
                          skip_group_check=True)
                pe.wait_ge(q["mish"], it + 1)
                for b in range(CB):
                    for m in range(2):
                        last = pe.matmul(O1[:, D * b:D * (b + 1)], hid[:, m, P * b:P * (b + 1)], w2[:, m, :],
                                         start=False, stop=(b == CB - 1 and m == 1), skip_group_check=True)
                last.then_inc(q["product"], 1)
                pe.wait_ge(q["staged"], it + 1)
                turn_chunk().then_inc(q["turned"], 1)
                pe.wait_ge(q["taken"], it + 1)

            def hop(p):
                now = window_sum(p, lambda k, c: rows[:, k, c, 0:D], D,
                                 lambda g, k, it: pe.wait_ge(gathered[k], it * (C * 16) + (p * NI + 1) * (C * 16)))
                with pe.Fori(0, NI) as it:
                    for k in range(R):
                        now(it * R + k, k, it)

            if stop >= 1:
                for p in (HOP1, HOP2):
                    hop(p)
                    q = st[p]
                    with pe.Fori(0, NCH) as it:
                        pe.wait_ge(q["acc_copied"], it + 1)
                        if p == HOP1:
                            turn_back(D).then_inc(q["product"], 1)
                        else:
                            for b in range(CB):
                                last = pe.matmul(A1[:, D * b:D * (b + 1)], chunkT[0:D, P * b:P * (b + 1)],
                                                 w3[:, 1, :], start=True, stop=True)
                            last.then_inc(q["product"], 1)
                        pe.wait_ge(q["staged"], it + 1)
                        turn_chunk().then_inc(q["turned"], 1)
                        pe.wait_ge(q["taken"], it + 1)
            if stop >= 2:
                def turn_rows(g, k, it):
                    pe.wait_ge(gathered[k], it * (C * 16) + (ATTENTION * NI + 1) * (C * 16))
                    pe.sem_inc(s["pe_started"], 1)
                    for c in range(C):
                        ins = pe.transpose(T2[0:D, P * c:P * (c + 1)], rows[:, k, c, 0:D], ident[:, :])
                        if c % 4 == 3:
                            ins.then_inc(s["rows_turned"], 1)

                def score(g, w):
                    pe.wait_ge(s["scores_read"], g + 1)
                    for c in range(C):
                        if c % 4 == 0:
                            pe.wait_ge(s["rows_copied"], g * 2 + (c // 4 + 1))
                            pe.sem_inc(s["pe_started"], 1)
                        last = pe.matmul(S2[:, P * c:P * (c + 1)], rowsT[:, P * c:P * (c + 1)],
                                         zT[0:D, bass.ds(w, W)], start=True, stop=True)
                    last.then_inc(s["scored"], 1)

                def score_further(g):
                    w, nx = group_values(pe, g, [0, 1])
                    with pe.If(nx > 0):
                        before, = group_values(pe, g, [2])
                        with pe.Fori(0, nx) as i:
                            pe.wait_ge(s["score_extra_ready"], before + i + 1)
                            pe.sem_inc(s["pe_started"], 1)
                            for c in range(C):
                                last = pe.matmul(H2[:, P * c:P * (c + 1)], rowsT[:, P * c:P * (c + 1)],
                                                 zT[0:D, further(pe, w, i)], start=True, stop=True)
                            last.then_inc(s["score_extra_summed"], 1)

                sum_weighted = window_sum(ATTENTION, lambda k, c: msg[:, c, :], M1,
                                          lambda g, k, it: pe.wait_ge(s["msg_ready"], g + (NG + 1)))

                def attention_step(g, k, it, more):
                    if more:
                        score_further(g + 1)
                    if more == 2:
                        w, = group_values(pe, g + 2, [0])
                        turn_rows(g + 2, (k + 2) % R, it + (k + 2) // R)
                    sum_weighted(g, k, it)
                    if more == 2:
                        score(g + 2, w)

                for k in range(2):
                    w, = group_values(pe, k, [0])
                    turn_rows(k, k, 0)
                    score(k, w)
                    if k == 0:
                        score_further(0)
                ring_loop(attention_step)
                q = st[ATTENTION]
                pe.sem_inc(q["product"], 2)
                zeros = hid[0:1, 1, 0:CD]

                def turn_sums(n, k):
                    pe.wait_ge(q["acc_copied"], n + 1)
                    pe.wait_ge(q["counts"], n + 1)
                    pe.sem_inc(s["pe_started"], 1)
                    for b in range(CB):
                        last = pe.transpose([A1, O1][k][:, M1 * b:M1 * (b + 1)], chunk_buf[k][:, P * b:P * (b + 1)],
                                            ident[0:M1, 0:M1])
                    last.then_inc(q["product"], 1)

                def sum_nodes(n, k, more):
                    if more:
                        turn_sums(n + 1, 1 - k)
                    pe.wait_ge(q["counts"], n + 3)
                    pe.sem_inc(s["pe_started"], 1)
                    pe.matmul(H2[:, 0:CD], ones[:, :], hn[:, bass.ds(n * CB, CB), :].rearrange("p b d -> p (b d)"),
                              start=False, stop=False, skip_group_check=True)

                pe.wait_ge(s["zero_row"], 1)
                pe.matmul(H2[:, 0:CD], ones[0:1, :], zeros, start=True, stop=False, skip_group_check=True)
                turn_sums(0, 0)
                chunk_loop(pe, sum_nodes)
                pe.matmul(H2[:, 0:CD], ones[0:1, :], zeros, start=False, stop=True, skip_group_check=True).then_inc(
                    s["bn_summed"], 1)
            if stop >= 3:
                def sum_squares(n, k, more):
                    pe.wait_ge(s["bn_squared"], n + 1)
                    pe.matmul(H2[:, 512:512 + CD], ones[:, :], tmp[:, k, CD:2 * CD], start=False, stop=False,
                              skip_group_check=True).then_inc(s["bn_summed"], 1)

                pe.matmul(H2[:, 512:512 + CD], ones[0:1, :], zeros, start=True, stop=False,
                          skip_group_check=True).then_inc(s["bn_summed"], 1)
                chunk_loop(pe, sum_squares)
                pe.matmul(H2[:, 512:512 + CD], ones[0:1, :], zeros, start=False, stop=True,
                          skip_group_check=True).then_inc(s["bn_summed"], 1)

                def turn_features(n, k):
                    pe.wait_ge(q["staged"], n + 1)
                    pe.sem_inc(s["pe_started"], 1)
                    for b in range(CB):
                        last = pe.transpose(H2[0:D, P * b:P * (b + 1)], x_next[k][:, D * b:D * (b + 1)], ident[:, :])
                    last.then_inc(q["turned"], 1)

                def products(n, k, more):
                    pe.wait_ge(q["taken"], n + 1)
                    for b in range(CB):
                        for j in range(2):
                            pe.wait_ge(s["low_copied"], n * (2 * CB) + (2 * b + j + 1))
                            pe.wait_ge(s["high_copied"], n * (2 * CB) + (2 * b + j + 1))
                            for h in range(2):
                                last = pe.matmul([S2, T2][h][:, 512 * j:512 * (j + 1)],
                                                 xT[k][:, P * b:P * (b + 1)], relw[:, :, :].rearrange(
                                                     "p r d -> p (r d)")[:, 1024 * h + 512 * j:1024 * h + 512 * (j + 1)],
                                                 start=True, stop=True)
                            last.then_inc(s["product_ready"], 1)
                        if b == 1:
                            for c in range(CB):
                                last = pe.matmul(A1[:, D * c:D * (c + 1)], xT[k][0:D, P * c:P * (c + 1)], w3[:, 2, :],
                                                 start=True, stop=True)
                            last.then_inc(q["hidden"], 1)
                        if more and b == 5:
                            turn_features(n + 1, 1 - k)

                pe.wait_ge(s["padding_zero"], 2)
                turn_features(0, 0)
                chunk_loop(pe, products)
                hop(RELATIONS)
                q = st[RELATIONS]
                with pe.Fori(0, NCH) as it:
                    pe.wait_ge(q["acc_copied"], it + 1)
                    turn_back(D).then_inc(q["product"], 1)
                    pe.wait_ge(q["counts"], it + 1)

        @block.vector
        def _(dve):
            steps = Steps(dve, s["dve_steps"])
            link = steps.link
            tt, ts, stt = dve.tensor_tensor, dve.tensor_scalar, dve.scalar_tensor_tensor

            def by_node(t):
                return t.unsqueeze(2).to_broadcast([P, CB, D])

            def by_feature(t):
                return t.unsqueeze(1).to_broadcast([P, CB, D])

            def nodes(t, it):
                return t[:, bass.ds(it * CB, CB)]

            dve.memset(src_i, 0).then_inc(s["pads_ready"], 1)
            dve.memset(dst_i, N).then_inc(s["pads_ready"], 1)
            dve.memset(typ_i, 0).then_inc(s["pads_ready"], 1)
            dve.memset(xn[:, NB - 1, :], 0.0).then_inc(s["pads_ready"], 1)
            dve.memset(attrw[:, :], 0.0).then_inc(s["weights_zero"], 1)
            dve.memset(ones[:, :], 1.0).then_inc(s["matrices_ready"], 1)
            link(dve.memset(cols[:, 6:7], 2.0))
            link(dve.memset(msg[:, :, :], 1.0))
            link(dve.memset(rows[:, :, :, :], 1.0))
            link(dve.memset(gtab[:, :, :], 0))
            link(dve.memset(dstrel[:, NG, :], 0.0))
            dve.wait_ge(s["iota_ready"], 1)
            link(dve.tensor_copy(iota[:, :], prod[:, 0, :].bitcast(I32)))
            dve.wait_ge(s["small_loaded"], 16 * SMALL_LOADS)
            ts(cols[0:D, 3:4], cols[0:D, 3:4], 1.0, None, ALU.add).then_inc(s["setup_dve"], 1)

            dve.wait_ge(s["edges_loaded"], 16 * 9)
            link(dve.tensor_copy(dst_f, dst_i))
            lo, hi, span = (small[0:HG, k, 0:2] for k in range(3))
            link(dve.tensor_reduce(lo, dst_f, AX, ALU.min))
            link(dve.tensor_reduce(hi, dst_f, AX, ALU.max))
            link(tt(span, hi, lo, ALU.subtract))
            link(ts(dst_f[:, 0, :], dst_f[:, 0, :], small[0:HG, 0, 0:1], None, ALU.subtract))
            ts(dst_f[:, 1, :], dst_f[:, 1, :], small[0:HG, 0, 1:2], None, ALU.subtract).then_inc(s["setup_dve"], 1)
            link(dve.tensor_copy(gtab[0:HG, :, 0], lo))
            link(dve.tensor_copy(gtab[0:HG, :, 1], span))
            link(ts(gtab[0:HG, :, 1], gtab[0:HG, :, 1], W.bit_length() - 1, None, ALU.logical_shift_right))
            dve.tensor_copy(score8[0:HG, 0, 0:2], gtab[0:HG, :, 1]).then_inc(s["setup_dve"], 1)
            dve.wait_ge(s["setup_pe"], 1)
            dve.tensor_copy(w3[:, 1, :], A1[0:D, 0:D]).then_inc(s["setup_dve"], 1)
            dve.tensor_copy(coeffT[:, :], A1[0:NBASE, 64:64 + NREL]).then_inc(s["setup_dve"], 1)
            tt(cols[:, 4:6], A1[:, 128:130], cols[:, 1:3], ALU.add).then_inc(s["setup_dve"], 1)
            dve.wait_ge(s["setup_pe"], 2)
            for h in range(2):
                link(dve.tensor_copy(dstrel[:, HG * h:HG * (h + 1), :].rearrange("p q c -> p c q"),
                                     [S2, T2][h][:, :].rearrange("p (c q) -> p c q", q=P)[:, :, 0:HG]))
            dve.wait_ge(s["setup_pe"], 3)
            link(dve.tensor_copy(gtab[0:HG, :, 2], O1[0:HG, 0:2]))
            link(dve.tensor_copy(gtab[0:HG, 0, 3:4], O1[0:HG, 2:3]))
            dve.tensor_copy(gtab[0:HG, 1, 3:4], O1[0:HG, 2:3]).then_inc(s["group_ready"], 1)
            dve.wait_ge(s["index_stored"], 16)
            stt(typ_i, src_i, float(NREL), typ_i, ALU.mult, ALU.add).then_inc(s["rel_index_ready"], 1)
            for k in range(D * D // 512):
                dve.wait_ge(s["setup_pe"], 4 + k)
                dve.tensor_copy(relw_flat[:, 512 * k:512 * (k + 1)], A1[0:NREL, :]).then_inc(s["relw_ready"], 1)
            link(dve.memset(acc[D:M1, :], 0.0))
            link(dve.memset(acc[0:D, NP:NACC], 0.0))
            dve.wait_ge(s["init_copied"], NCH)
            dve.wait_ge(s["group_loaded"], 16)
            dve.sem_inc(s["acc_added"], R)
            steps.end(0) if steps.per else None
            steps.done, steps.at = steps.at, 0

            def build_onehot(g, half):
                at = dstrel[:, bass.ds(g, 1), :].rearrange("p a c -> p (a c)")
                tt(onehot[:, half, :, :], iota[:, :].unsqueeze(1).to_broadcast([P, C, W]),
                   at.unsqueeze(2).to_broadcast([P, C, W]), ALU.is_equal).then_inc(s["onehot_ready"], 1)

            def further_onehot(ready):
                dve.drain()
                ts(dx[:, :], dx[:, :], -float(W), None, ALU.add)
                dve.drain()
                return tt(prod[:, :, :], iota[:, :].unsqueeze(1).to_broadcast([P, C, W]),
                          dx[:, :].unsqueeze(2).to_broadcast([P, C, W]), ALU.is_equal)

            def add_windows(p, g, k, width, w, nx):
                with dve.If(nx > 0):
                    before, total = group_values(dve, g, [2, 3])
                    dve.tensor_copy(dx[:, :], dstrel[:, bass.ds(g, 1), :].rearrange("p a c -> p (a c)"))
                    with dve.Fori(0, nx) as i:
                        further_onehot(None).then_inc(s["extra_ready"], 1)
                        dve.drain()
                        dve.wait_ge(s["extra_summed"], before + total * p + i + 1)
                        at = acc[0:width, further(dve, w, i)]
                        tt(at, at, H2[0:width, 512:512 + W], ALU.add)
                    dve.drain()
                dve.wait_ge(s["window_summed"], g + (p * NG + 1))
                dve.wait_ge(s["acc_added"], g + (p * NG + R))
                at = acc[0:width, bass.ds(w, W)]
                tt(at, at, [A1, O1][k % 2][0:width, 0:W], ALU.add).then_inc(s["acc_added"], 1)

            def pass_loop(p, per, body):
                build_onehot(0, 0)
                with dve.Fori(0, NI) as it:
                    steps.turn(it, per * R)
                    for k in range(R):
                        w, nx = group_values(dve, it * R + k, [0, 1])
                        body(it * R + k, k, it, w, nx)
                steps.end(NI)
                dve.wait_ge(s["acc_added"], acc_total(p))

            def newton(n, r, a):
                link(stt(a, n, 2.0, r, ALU.add, ALU.mult))
                link(stt(a, a, -2.0, r, ALU.add, ALU.mult))
                return stt(a, n, -1.0, a, ALU.mult, ALU.mult)

            def message_inputs(g, k, it):
                v, u = msg_v[k % 2], msg_u[k % 2]
                dve.wait_ge(s["attrs_mixed"], g + 1)
                dve.wait_ge(gathered[k], it * (C * 16) + C * 16)
                link(tt(blocks(v), blocks(S2[:, 512 * (k % 2):512 * (k % 2 + 1)]), rows[:, k, :, 0:D], ALU.add))
                ts(u, v, MISH_CAP, None, ALU.min).then_inc(s["exp_in"], 1)

            def numerator(g, k):
                u = msg_u[k % 2]
                dve.wait_ge(s["exp_out"], g + 1)
                stt(msg_n, u, 2.0, u, ALU.add, ALU.mult).then_inc(s["inverse_in"], 1)

            def mish_factor(g, k):
                dve.wait_ge(s["inverse_out"], g + 1)
                link(newton(msg_n, msg_r, msg_u[k % 2]))

            def message(k):
                tt(msg[:, :, 0:D], blocks(msg_u[k % 2]), blocks(msg_v[k % 2]), ALU.mult).then_inc(s["msg_ready"], 1)

            def message_step(g, k, it, more=True):
                w, nx = group_values(dve, g, [0, 1])
                numerator(g + 1, k + 1)
                if more:
                    dve.wait_ge(s["msg_ready"], g + 1)
                    message_inputs(g + 2, (k + 2) % R, it + (k + 2) // R)
                mish_factor(g + 1, k + 1)
                dve.sem_inc(s["dve_started"], 1)
                add_windows(MESSAGES, g, k, M1, w, nx)
                build_onehot(g + 2, k % 2)
                message(k + 1)

            steps.turn(0, 1 + 1 + 3)
            message_inputs(0, 0, 0)
            numerator(0, 0)
            message_inputs(1, 1, 0)
            mish_factor(0, 0)
            build_onehot(0, 0)
            build_onehot(1, 1)
            message(0)
            steps.end(1)
            with dve.Fori(0, NI - 1) as it:
                steps.turn(it, 4 * R)
                for k in range(R):
                    message_step(it * R + k, k, it)
            steps.end(NI - 1)
            steps.turn(0, 3 * (R - 1) + R - 2)
            for k in range(R - 1):
                message_step(NG - R + k, k, NI - 1, more=k < R - 2)
            steps.end(1)
            w, nx = group_values(dve, NG - 1, [0, 1])
            add_windows(MESSAGES, NG - 1, R - 1, M1, w, nx)
            dve.wait_ge(s["acc_added"], acc_total(MESSAGES))

            def root_newton(r, v, a):
                link(tt(a, v, r, ALU.mult))
                link(stt(a, a, -0.5, r, ALU.mult, ALU.mult))
                link(stt(r, a, 1.5, r, ALU.add, ALU.mult))
                return r

            def layernorm(y, it, roots):
                total, var = small[:, 0, :], small[:, 1, :]
                link(dve.tensor_reduce(total, y, AX, ALU.add))
                link(stt(centred, by_node(total), -1.0 / D, y, ALU.mult, ALU.add))
                link(tt(square, centred, centred, ALU.mult))
                link(dve.tensor_reduce(var, square, AX, ALU.add))
                ts(small[:, 2, :], var, 1.0 / D, EPS, ALU.mult, ALU.add).then_inc(s["root_in"], 1)
                dve.wait_ge(s["root_out"], it + (roots + 1))
                return root_newton(small[:, 5, :], small[:, 2, :], small[:, 0, :])

            y, centred = blocks(tmp[:, 0, 0:CD]), blocks(tmp[:, 0, CD:2 * CD])
            square = blocks(tmp[:, 1, 0:CD])
            out_stage = blocks(stage[:, :])

            q, p_now = st[MESSAGES], MESSAGES
            dve.wait_ge(s["init_copied"], NCH)
            with dve.Fori(0, NCH) as it:
                steps.turn(it, 7 + 3 + 1 + 7 + 3 + 2)
                halves = "p (q n) -> p q n"
                for m in range(2):
                    dve.wait_ge(q["hidden"], it * 2 + (m + 1))
                    ts(hid[:, m, :].rearrange(halves, q=2), [S2, T2][m][:, :].rearrange(halves, q=2)[:, :, 0:HALF],
                       cols[:, 4 + m:5 + m], MISH_CAP, ALU.add, ALU.min).then_inc(q["capped"], 1)
                for m in range(2):
                    dve.wait_ge(q["exp"], it * 2 + (m + 1))
                    u, n, r = hid[:, m, :], tmp[:, 0, :], tmp[:, 1, :]
                    stt(n, u, 2.0, u, ALU.add, ALU.mult).then_inc(s["inverse_in"], 1)
                    dve.wait_ge(s["inverse_out"], it * 2 + (NG + m + 1))
                    link(newton(n, r, u))
                    ins = stt(u.rearrange(halves, q=2), [S2, T2][m][:, :].rearrange(halves, q=2)[:, :, 0:HALF],
                              cols[:, 4 + m:5 + m], u.rearrange(halves, q=2), ALU.add, ALU.mult)
                    if m == 0:
                        link(ins)
                    else:
                        ins.then_inc(q["mish"], 1)
                dve.wait_ge(q["counts"], it + 1)
                count = A1[:, 0:M1 * CB].rearrange("p (b m) -> p b m", m=M1)[:, :, D]
                link(ts(small[:, 3, :], count, 1.0, None, ALU.add))
                link(ts(small[:, 4, :], count, 1.0, None, ALU.max))
                link(dve.reciprocal(nodes(cinv, it), small[:, 4, :]))
                dve.wait_ge(q["product"], it + 1)
                link(tt(y, blocks(O1[:, 0:CD]), nodes(xn, it), ALU.add))
                rstd = layernorm(y, it, ROOTS[p_now])
                root_newton(small[:, 6, :], small[:, 3, :], small[:, 0, :])
                link(dve.tensor_copy(nodes(dinv, it), small[:, 6, :]))
                link(tt(small[:, 7, :], rstd, small[:, 6, :], ALU.mult))
                tt(nodes(xn, it), centred, by_node(rstd), ALU.mult)
                dve.wait_ge(q["stage_free"], it + 1)
                tt(out_stage, centred, by_node(small[:, 7, :]), ALU.mult).then_inc(q["staged"], 1)
                dve.wait_ge(q["taken"], it + 1)
            steps.end(NCH)

            if stop >= 1:
                def hop_sum(p):
                    def body(g, k, it, w, nx):
                        build_onehot(g + 1, (k + 1) % 2)
                        add_windows(p, g, k, D, w, nx)
                    return body

                pass_loop(HOP1, 0, hop_sum(HOP1))
                q = st[HOP1]
                with dve.Fori(0, NCH) as it:
                    steps.turn(it, 1)
                    link(tt(small[:, 0, :], nodes(dinv, it), nodes(dinv, it), ALU.mult))
                    dve.wait_ge(q["product"], it + 1)
                    dve.wait_ge(q["stage_free"], it + 1)
                    tt(out_stage, blocks(A1[:, 0:CD]), by_node(small[:, 0, :]), ALU.mult).then_inc(q["staged"], 1)
                    dve.wait_ge(q["taken"], it + 1)
                steps.end(NCH)
                pass_loop(HOP2, 0, hop_sum(HOP2))
                dve.wait_ge(s["relw_loaded"], 16)
                dve.memset(zT[0:D, NP:NACC], 0.0).then_inc(s["zeros_ready"], 1)
                dve.memset(hid[:, 1, :], 0.0).then_inc(s["zeros_ready"], 1)
                q, p_now = st[HOP2], HOP2
                with dve.Fori(0, NCH) as it:
                    steps.turn(it, 3 + 7)
                    dve.wait_ge(q["product"], it + 1)
                    link(tt(y, blocks(A1[:, 0:CD]), by_node(nodes(dinv, it)), ALU.mult))
                    link(tt(y, y, nodes(xn, it), ALU.add))
                    link(tt(y, y, by_feature(bvec[:, 0, :]), ALU.add))
                    rstd = layernorm(y, it, ROOTS[p_now])
                    tt(nodes(xn, it), centred, by_node(rstd), ALU.mult)
                    dve.wait_ge(q["stage_free"], it + 1)
                    tt(out_stage, centred, by_node(rstd), ALU.mult).then_inc(q["staged"], 1)
                    dve.wait_ge(q["taken"], it + 1)
                steps.end(NCH)
            if stop >= 2:
                dve.sem_inc(s["scores_read"], 1)

                def scores(g, k):
                    nx, = group_values(dve, g, [1])
                    dve.wait_ge(s["scored"], g + 1)
                    dve.wait_ge(s["onehot_ready"], g + (ATTENTION * (NG + 1) + 1))
                    tt(prod[:, :, :], onehot[:, k % 2, :, :], S2[:, :].rearrange("p (c n) -> p c n", n=W),
                       ALU.mult).then_inc(s["scores_read"], 1)
                    dve.wait_ge(s["scores_read"], g + 2)
                    link(dve.tensor_reduce(score8[:, 0, :], prod[:, :, :], AX, ALU.add))
                    dve.sem_inc(s["dve_started"], 1)
                    with dve.If(nx > 0):
                        before, = group_values(dve, g, [2])
                        dve.tensor_copy(dx[:, :], dstrel[:, bass.ds(g, 1), :].rearrange("p a c -> p (a c)"))
                        with dve.Fori(0, nx) as i:
                            further_onehot(None).then_inc(s["score_extra_ready"], 1)
                            dve.drain()
                            dve.wait_ge(s["score_extra_summed"], before + i + 1)
                            tt(prod[:, :, :], prod[:, :, :], H2[:, :].rearrange("p (c n) -> p c n", n=W), ALU.mult)
                            dve.drain()
                            dve.tensor_reduce(score8[:, 2, :], prod[:, :, :], AX, ALU.add)
                            dve.drain()
                            tt(score8[:, 0, :], score8[:, 0, :], score8[:, 2, :], ALU.add)
                        dve.drain()
                    dve.sem_inc(s["exp_in"], 1)

                def weigh(g, k):
                    dve.wait_ge(s["exp_out"], g + (NG + 1))
                    link(ts(score8[:, 3, :], score8[:, 1, :], 1.0, None, ALU.max))
                    tt(msg[:, :, :], rows[:, k, :, :], score8[:, 3, :].unsqueeze(2).to_broadcast([P, C, M1]),
                       ALU.mult).then_inc(s["msg_ready"], 1)

                def attention_step(g, k):
                    w, nx = group_values(dve, g, [0, 1])
                    scores(g + 1, k + 1)
                    add_windows(ATTENTION, g, k, M1, w, nx)
                    build_onehot(g + 2, k % 2)
                    weigh(g + 1, (k + 1) % R)

                build_onehot(0, 0)
                build_onehot(1, 1)
                steps.turn(0, 2)
                scores(0, 0)
                weigh(0, 0)
                steps.end(1)
                with dve.Fori(0, NI - 1) as it:
                    steps.turn(it, 2 * R)
                    for k in range(R):
                        attention_step(it * R + k, k)
                steps.end(NI - 1)
                steps.turn(0, 2 * (R - 1))
                for k in range(R - 1):
                    attention_step(NG - R + k, k)
                steps.end(1)
                w, nx = group_values(dve, NG - 1, [0, 1])
                add_windows(ATTENTION, NG - 1, R - 1, M1, w, nx)
                dve.wait_ge(s["acc_added"], acc_total(ATTENTION))
                q = st[ATTENTION]
                dve.memset(hid[0:1, 1, :], 0.0).then_inc(s["zero_row"], 1)
                dve.sem_inc(q["counts"], 2)

                def node_means(n, k, more):
                    dve.wait_ge(q["product"], n + 3)
                    sums = [A1, O1][k][:, 0:M1 * CB].rearrange("p (b m) -> p b m", m=M1)
                    weight, inverse, factor = (small[:, 3 * k + j, :] for j in range(3))
                    link(ts(weight, sums[:, :, D], TINY, None, ALU.max))
                    link(dve.reciprocal(inverse, weight))
                    link(tt(factor, inverse, nodes(valid, n), ALU.mult))
                    tt(nodes(hn, n), sums[:, :, 0:D], by_node(factor), ALU.mult).then_inc(q["counts"], 1)

                chunk_loop(dve, node_means, steps, 3, 3)
            if stop >= 3:
                total, mean, scale, shift, sq = (bn[:, j, :] for j in range(5))

                def column_sums(value, bank):
                    dve.wait_ge(s["bn_summed"], value)
                    link(dve.tensor_reduce(total, H2[:, 512 * bank:512 * bank + CD].rearrange("p (b d) -> p d b", d=D), AX,
                                           ALU.add))

                dve.memset(xT_both[D:P, :], 0.0).then_inc(s["padding_zero"], 1)
                dve.memset(relw[D:P, :, :], 0.0).then_inc(s["padding_zero"], 1)
                steps.turn(0, 2)
                column_sums(1, 0)
                link(ts(mean, total, 1.0 / N, None, ALU.mult))
                steps.end(1)

                def squares(n, k, more):
                    dve.wait_ge(s["bn_summed"], n + 1)
                    link(tt(blocks(tmp[:, k, 0:CD]), nodes(hn, n), by_feature(mean), ALU.subtract))
                    tt(tmp[:, k, CD:2 * CD], tmp[:, k, 0:CD], tmp[:, k, 0:CD], ALU.mult).then_inc(s["bn_squared"], 1)

                chunk_loop(dve, squares, steps, 1, 1)
                steps.turn(0, 3 + 1 + 3 + 3)
                column_sums(NCH + 3, 1)
                link(tt(sq, mean, mean, ALU.mult))
                link(stt(total, sq, -float(NPAD), total, ALU.mult, ALU.add))
                link(ts(total, total, 1.0 / N, EPS, ALU.mult, ALU.add))
                dve.sem_inc(s["root_in"], 1)
                dve.wait_ge(s["root_out"], ROOTS["bn"] + 1)
                root_newton(bn[:, 5, :], total, sq)
                link(tt(scale, bn[:, 5, :], bvec[:, 1, :], ALU.mult))
                link(tt(sq, mean, scale, ALU.mult))
                link(tt(shift, bvec[:, 2, :], sq, ALU.subtract))
                steps.end(1)

                def normalise(n, k, piece):
                    if piece == 0:
                        link(tt(y, nodes(hn, n), by_feature(scale), ALU.mult))
                        link(tt(y, y, by_feature(shift), ALU.add))
                    elif piece == 1:
                        link(stt(y, y, 0.0, nodes(xn, n), ALU.max, ALU.add))
                        link(dve.tensor_reduce(small[:, 0, :], y, AX, ALU.add))
                    elif piece == 2:
                        link(stt(centred, by_node(small[:, 0, :]), -1.0 / D, y, ALU.mult, ALU.add))
                        link(tt(square, centred, centred, ALU.mult))
                    elif piece == 3:
                        link(dve.tensor_reduce(small[:, 1, :], square, AX, ALU.add))
                        ts(small[:, 2, :], small[:, 1, :], 1.0 / D, EPS, ALU.mult, ALU.add).then_inc(s["root_in"], 1)
                    elif piece == 4:
                        dve.wait_ge(s["root_out"], n + (ROOTS[ATTENTION] + 1))
                        rstd = root_newton(small[:, 5, :], small[:, 2, :], small[:, 0, :])
                        tt(blocks(x_next[k]), centred, by_node(rstd), ALU.mult).then_inc(q["staged"], 1)

                def copy_low(n, k, more):
                    for b in range(CB):
                        for j in range(2):
                            dve.wait_ge(s["product_ready"], n * (2 * CB) + (2 * b + j + 1))
                            if j == 0:
                                dve.wait_ge(s["y_free"], n * CB + (b + 1))
                            dve.tensor_copy(ybuf[(CB * k + b) % 2][:, 512 * j:512 * (j + 1)],
                                            S2[:, 512 * j:512 * (j + 1)]).then_inc(s["low_copied"], 1)
                        if b < 5 and more:
                            normalise(n + 1, 1 - k, b)
                        if b == 5:
                            dve.wait_ge(q["hidden"], n + 1)
                            link(tt(nodes(xn, n), blocks(x_next[k]), blocks(A1[:, 0:CD]), ALU.add))
                        if b == 6:
                            link(tt(nodes(xn, n), nodes(xn, n), by_feature(bvec[:, 3, :]), ALU.add))

                steps.turn(0, 10)
                for piece in range(5):
                    normalise(0, 0, piece)
                steps.end(1)
                dve.sem_inc(s["low_copied"], 2)
                chunk_loop(dve, copy_low, steps, 12, 2)
                dve.wait_ge(s["acc_zeroed"], 1)
                pass_loop(RELATIONS, 0, hop_sum(RELATIONS))
                q, p_now = st[RELATIONS], RELATIONS
                with dve.Fori(0, NCH) as it:
                    steps.turn(it, 1 + 7)
                    dve.wait_ge(q["product"], it + 1)
                    tt(y, blocks(A1[:, 0:CD]), by_node(nodes(cinv, it)), ALU.mult).then_inc(q["counts"], 1)
                    dve.wait_ge(q["counts"], it + 1)
                    link(tt(y, y, nodes(xn, it), ALU.add))
                    rstd = layernorm(y, it, ROOTS[p_now])
                    tt(nodes(xn, it), centred, by_node(rstd), ALU.mult)
                steps.end(NCH)
            dve.drain().then_inc(s["x_final"], 1)


_INS = ['x', 'src', 'dst', 'edge_attr_16', 'edge_type_32', 'L0_gnn_globals_', 'L0_gnn_We_kernel', 'L0_gnn_We_bias',
        'L0_gnn_epsilon', 'L0_gnn_W1', 'L0_gnn_b1', 'L0_gnn_W2', 'L0_gnn_b2', 'L1_gnn_weight', 'L1_gnn_bias',
        'L2_gnn_gamma', 'L2_gnn_beta', 'L3_gnn_basis', 'L3_gnn_coeff', 'L3_gnn_self_weight', 'L3_gnn_bias']
STOP = 9


def kernel(**inputs):
    import numpy as np
    import concourse.bacc as bacc
    from concourse.bass_utils import run_bass_kernel_spmd

    nc = bacc.Bacc("TRN2", target_bir_lowering=False, num_devices=1)
    arrays, handles = {}, {}
    for name in _INS:
        arrays[f"in_{name}"] = np.ascontiguousarray(inputs[name])
        handles[name] = nc.dram_tensor(f"in_{name}", arrays[f"in_{name}"].shape,
                                       mybir.dt.from_np(arrays[f"in_{name}"].dtype), kind="ExternalInput").ap()
    out = nc.dram_tensor("out", (N, D), F32, kind="ExternalOutput").ap()
    gnn(nc, handles, out, STOP)
    return run_bass_kernel_spmd(nc, [arrays], core_ids=[0]).results[0]["out"]
```

```python
from contextlib import ExitStack

import concourse.bass as bass
from concourse import mybir

F32 = mybir.dt.float32
I32 = mybir.dt.int32
ALU = mybir.AluOpType
ACT = mybir.ActivationFunctionType
AX = mybir.AxisListType.X

P = 128
N, E, D = 12500, 200000, 64
DE = 16
H = 256
NREL, NBASE = 32, 30
EPS = 1e-5
TINY = 1e-30
MISH_CAP = 10.0

C = 8
GE = P * C
NG = -(-E // GE)
TAIL = E - (NG - 1) * GE
TAILP = TAIL // C
R = 4
NI = NG // R
HG = NG // 2
W = 128
M1 = D + 1

CB = 7
NB = -(-N // P)
NCH = NB // CB
CW = CB * P
CD = CB * D
NP = NB * P
NACC = NP + W
LASTN = N - (NB - 1) * P
NPAD = NP - N
HALF = CW // 2
YW = NREL * D
assert NB * D + 2 * YW + 2 * CW <= NACC and NCH % 2 == 0
assert NI * R == NG and HG * 2 == NG and NB == NCH * CB and TAILP * C == TAIL and R % 2 == 0

MESSAGES, HOP1, HOP2, ATTENTION, RELATIONS = range(5)


class Steps:

    def __init__(self, eng, sem):
        self.eng, self.sem, self.done, self.at, self.index, self.per = eng, sem, 0, 0, 0, 0

    def turn(self, index, per):
        self.index, self.per, self.at = index, per, 0

    def link(self, ins):
        ins.then_inc(self.sem, 1)
        self.at += 1
        self.eng.wait_ge(self.sem, self.index * self.per + (self.done + self.at))

    def straight(self):
        self.done, self.at = self.done + self.at, 0

    def end(self, turns):
        assert self.at == self.per, (self.at, self.per)
        self.done += turns * self.per
        self.index, self.per, self.at = 0, 0, 0


def gnn(nc, a, out, stop=9):
    with ExitStack() as ctx:
        def sb(name, shape, dt=F32):
            return ctx.enter_context(nc.sbuf_tensor(name, shape, dt))

        def sem(name):
            return ctx.enter_context(nc.semaphore(name))

        def psum(name, cols):
            return ctx.enter_context(nc.psum_tensor(name, [P, cols], F32))

        def scratch(name, shape, dt=F32):
            return nc.dram_tensor(name, shape, dt, kind="Internal").ap()

        table = {HOP1: scratch("hop1_table", (NP, D)), HOP2: scratch("hop2_table", (NP, D)),
                 ATTENTION: scratch("attention_table", (NP, D)),
                 RELATIONS: scratch("relation_table", (NP * NREL, D))}
        src_index = scratch("src_index", (NG * GE,), I32)
        rel_index = scratch("rel_index", (NG * GE,), I32)
        group_dram = scratch("group_dram", (NG, 4), I32)
        relw_dram = scratch("relw_dram", (NREL, D, D))

        acc = sb("acc", [P, NACC])
        zT = sb("zT", [P, NACC])
        xn = sb("xn", [P, NB, D])
        dstrel = sb("dstrel", [P, NG + 1, C])
        grow = sb("grow", [1, NG * 4], I32)
        idx = sb("idx", [P, R, C], I32)
        rows = sb("rows", [P, R, C, M1])
        attrs = sb("attrs", [P, R, C * DE])
        attrT = sb("attrT", [P, 2, P])
        msg = sb("msg", [P, C, M1])
        onehot = sb("onehot", [P, 2, C, W])
        prod = sb("prod", [P, C, W])
        rowsT = sb("rowsT", [D, C * P])
        score8 = sb("score8", [P, 4, C])
        dx = sb("dx", [P, C])
        chunkT = sb("chunkT", [P, CW])
        hid = sb("hid", [P, 2, CW])
        tmp = sb("tmp", [P, 2, CW])
        stage = sb("stage", [P, CD])
        small = sb("small", [P, 8, CB])
        gtab = sb("gtab", [P, 2, 4], I32)
        dinv = sb("dinv", [P, NB])
        cinv = sb("cinv", [P, NB])
        valid = sb("valid", [P, NB])
        ident = sb("ident", [P, P])
        iota = sb("iota", [P, W])
        ones = sb("ones", [P, P])
        attrw = sb("attrw", [P, C * D])
        rowb = sb("rowb", [1, 2, C * D])
        w1 = sb("w1", [P, 2, H])
        w2 = sb("w2", [P, 2, D])
        cols = sb("cols", [P, 8])
        bvec = sb("bvec", [P, 4, D])
        bn = sb("bn", [P, 6, D])
        w3 = sb("w3", [D, 3, D])
        coeff = sb("coeff", [NREL, NBASE])
        coeffT = sb("coeffT", [NBASE, NREL])
        relw = sb("relw", [P, NREL, D])

        def edge_view(k):
            return zT[0:HG, 2 * GE * k:2 * GE * (k + 1)].rearrange("p (h e) -> p h e", h=2)
        dst_i, dst_f = edge_view(0).bitcast(I32), edge_view(1)
        src_i, typ_i = edge_view(2).bitcast(I32), edge_view(3).bitcast(I32)
        basis = zT[0:NBASE, 8 * GE:8 * GE + D * D]
        relw_flat = zT[0:NREL, 0:D * D]
        hn = zT[:, 0:NB * D].rearrange("p (b d) -> p b d", d=D)
        xT = [zT[:, NB * D + 2 * YW + CW * k:NB * D + 2 * YW + CW * (k + 1)] for k in range(2)]
        prod_flat = prod[:, :, :].rearrange("p c n -> p (c n)")
        xT_both = zT[:, NB * D + 2 * YW:NB * D + 2 * YW + 2 * CW]
        ybuf = [zT[:, NB * D + YW * k:NB * D + YW * (k + 1)] for k in range(2)]

        tmp_flat, hid_flat = (t[:, :, :].rearrange("p m n -> p (m n)") for t in (tmp, hid))
        def third(t, j):
            return t[:, C * D * j:C * D * (j + 1)]
        msg_v, msg_u = [third(tmp_flat, j) for j in range(2)], [third(hid_flat, j) for j in range(2)]
        msg_n, msg_r = third(tmp_flat, 2), third(hid_flat, 2)

        chunk_pair = [chunkT[:, :], zT[:, 0:CW]]
        inverse = [onehot[:, m, :, :].rearrange("p c n -> p (c n)")[:, 0:CW] for m in range(2)]
        init_buf = [stage[:, :], hid[:, 0, 0:CD]]
        out_buf = [stage[:, :], tmp[:, 1, CD:2 * CD]]
        chunk_buf = [chunkT[0:M1, :], hid[0:M1, 0, :]]
        x_next = [hid[:, k, 0:CD] for k in range(2)]

        def blocks(t):
            return t.rearrange("p (b d) -> p b d", d=D)

        S2, T2, H2 = psum("S2", 1024), psum("T2", 1024), psum("H2", 1024)
        A1, O1 = psum("A1", 512), psum("O1", 512)

        names = """pool_const iota_ready small_loaded epsilon_loaded biases_ready src_loaded dst_loaded edge_type_32_loaded x_loaded basis_loaded pads_ready dve_steps
            weights_zero matrices_ready setup_pe setup_dve index_stored rel_index_ready group_ready group_stored
            group_loaded relw_ready relw_stored relw_loaded
            gather_started onehot_ready window_summed acc_added extra_ready extra_summed
            score_extra_ready score_extra_summed attrs_turned attrs_copied attrs_mixed exp_in exp_out msg_ready
            rows_turned rows_copied scored scores_read
            inverse_in inverse_out log_done root_log
            init_staged init_turned init_copied zeros_ready zero_copied x_final out_stored
            act_started pe_started dve_started root_in root_out product_ready low_copied high_copied y_free acc_zeroed zero_row bn_squared bn_summed padding_zero chunk_padding""".split()
        s = {n: sem(n) for n in names}
        idx_ready = [sem(f"idx_ready{k}") for k in range(R)]
        gathered = [sem(f"gathered{k}") for k in range(R)]
        attr_loaded = [sem(f"attr_loaded{k}") for k in range(R)]
        y_stored = [sem(f"y_stored{k}") for k in range(2)]
        st = {p: {n: sem(f"stage{p}_{n}") for n in ["acc_copied", "hidden", "capped", "exp", "mish", "counts", "product", "staged",
                                                    "stage_free", "turned", "taken", "stored"]} for p in range(5)}

        block = ctx.enter_context(nc.Block())

        def table_chunk(p, it):
            return table[p].rearrange("(i b p) d -> i p b d", b=CB, p=P)[bass.ds(it, 1)].rearrange(
                "a p b d -> (a p) b d")

        def chunk_loop(eng, body, steps=None, per=0, per_last=0):
            with eng.Fori(0, NCH // 2 - 1) as it:
                if steps:
                    steps.turn(it, 2 * per)
                body(it * 2, 0, 2)
                body(it * 2 + 1, 1, 2)
            if steps:
                steps.end(NCH // 2 - 1)
                steps.turn(0, per + per_last)
            body(NCH - 2, 0, 1)
            body(NCH - 1, 1, 0)
            if steps:
                steps.end(1)

        def one(view, g):
            return view[bass.ds(g, 1)].rearrange("a p c -> (a p) c")

        def acc_chunk(m, it):
            return acc[0:m, bass.ds(it * CW, CW)]

        def acc_total(p):
            return (p + 1) * NG + R

        src_v = src_index.rearrange("(g p c) -> g p c", p=P, c=C)
        rel_v = rel_index.rearrange("(g p c) -> g p c", p=P, c=C)
        attr_v = a["edge_attr_16"][0:(NG - 1) * GE].rearrange("(g p c) k -> g p (c k)", p=P, c=C)
        attr_tail = a["edge_attr_16"][(NG - 1) * GE:E].rearrange("(p c) k -> p (c k)", c=C)
        ROOTS = {MESSAGES: 0, HOP2: NCH, "bn": 2 * NCH, ATTENTION: 2 * NCH + 1, RELATIONS: 3 * NCH + 1}
        SMALL_LOADS = C + 2 + 2 + 2 + 4 + 3

        def group_values(eng, g, words):
            most = (N, NP // W, NG * NP // W, NG * NP // W)
            return [eng.value_load(grow[0:1, bass.ds(g * 4 + j, 1)], min_val=0, max_val=most[j]) for j in words]

        def further(eng, w, i):
            return bass.ds(nc.s_assert_within(w + i * W + W, W, NP, skip_runtime_bounds_check_because="further windows end with the last node"), W)

        @block.sync
        def _(sp):
            def first_loads(p, view):
                for k in range(R):
                    if p:
                        sp.wait_ge(gathered[k], p * NI * C * 16)
                    if p == RELATIONS and k == 0:
                        sp.wait_ge(s["index_stored"], 32)
                    sp.dma_start(idx[:, k, :], view[k]).then_inc(idx_ready[k], 16)
                    if p == MESSAGES:
                        sp.dma_start(attrs[:, k, :], attr_v[k]).then_inc(attr_loaded[k], 16)

            def edges(view, name):
                x = a[name]
                full = x[0:(NG - 1) * GE].rearrange("(q e) -> q e", e=GE)
                sp.dma_start(view[:, 0, :], full[0:HG]).then_inc(s[name + "_loaded"], 16)
                sp.dma_start(view[0:HG - 1, 1, :], full[HG:NG - 1]).then_inc(s[name + "_loaded"], 16)
                sp.dma_start(view[HG - 1:HG, 1, 0:TAIL],
                             x[(NG - 1) * GE:E].rearrange("(q e) -> q e", q=1)).then_inc(s[name + "_loaded"], 16)

            sp.wait_ge(s["pads_ready"], 1)
            sp.dma_start(xn[:, 0:NB - 1, :], a["x"][0:(NB - 1) * P].rearrange("(b p) d -> p b d", p=P)).then_inc(
                s["x_loaded"], 16)
            sp.dma_start(xn[0:LASTN, NB - 1, :], a["x"][(NB - 1) * P:N]).then_inc(s["x_loaded"], 16)
            sp.wait_ge(s["pads_ready"], 4)
            edges(dst_i, "dst")
            edges(src_i, "src")
            edges(typ_i, "edge_type_32")
            sp.dma_start(basis, a["L3_gnn_basis"].rearrange("b i o -> b (i o)")).then_inc(s["basis_loaded"], 16)
            sp.wait_ge(s["src_loaded"], 48)
            sp.dma_start(src_index.rearrange("(h q e) -> q h e", h=2, e=GE), src_i).then_inc(s["index_stored"], 16)
            sp.wait_ge(s["index_stored"], 16)
            first_loads(MESSAGES, src_v)
            sp.wait_ge(s["group_ready"], 1)
            sp.dma_start(group_dram.rearrange("(h q) w -> q h w", h=2), gtab[0:HG]).then_inc(s["group_stored"], 16)
            sp.wait_ge(s["group_stored"], 16)
            sp.dma_start(grow[:, :], group_dram.rearrange("g w -> (g w)").rearrange("(a n) -> a n", a=1)).then_inc(
                s["group_loaded"], 16)
            sp.wait_ge(s["rel_index_ready"], 1)
            sp.dma_start(rel_index.rearrange("(h q e) -> q h e", h=2, e=GE), typ_i).then_inc(s["index_stored"], 16)
            sp.wait_ge(s["relw_ready"], 8)
            sp.dma_start(relw_dram.rearrange("r i o -> r (i o)"), relw_flat).then_inc(s["relw_stored"], 16)
            sp.wait_ge(s["relw_stored"], 16)
            sp.dma_start(relw[0:D, :, :], relw_dram.rearrange("r i o -> i r o")).then_inc(s["relw_loaded"], 16)

            def edge_pass(p, view):
                attributes = p == MESSAGES
                if p:
                    first_loads(p, view)
                with sp.Fori(0, NI - 2) as it:
                    for k in range(R):
                        sp.wait_ge(gathered[k], it * (C * 16) + (p * NI + 1) * (C * 16))
                        sp.dma_start(idx[:, k, :], one(view, it * R + (R + k))).then_inc(idx_ready[k], 16)
                        if attributes:
                            sp.wait_ge(s["attrs_turned"], it * R + (k + 1))
                            sp.dma_start(attrs[:, k, :], one(attr_v, it * R + (R + k))).then_inc(attr_loaded[k], 16)
                for k in range(R):
                    g = NG - R + k
                    sp.wait_ge(gathered[k], (p * NI + NI - 1) * (C * 16))
                    sp.dma_start(idx[:, k, :], view[g]).then_inc(idx_ready[k], 16)
                    if attributes:
                        sp.wait_ge(s["attrs_turned"], g - R + 1)
                        if g < NG - 1:
                            sp.dma_start(attrs[:, k, :], attr_v[g]).then_inc(attr_loaded[k], 16)
                        else:
                            sp.dma_start(attrs[0:TAILP, k, :], attr_tail).then_inc(attr_loaded[k], 16)

            def store_table(p):
                q, buffers = st[p - 1], out_buf[0:1] if p == HOP1 else out_buf

                def store_chunk(n, k, more):
                    sp.wait_ge(q["staged"], n + 1)
                    sp.dma_start(table_chunk(p, n), blocks(buffers[k % len(buffers)])).then_inc(q["stored"], 16)
                    sp.wait_ge(q["stored"], n * 16 + 16)
                    sp.sem_inc(q["stage_free"], 1)

                sp.sem_inc(q["stage_free"], len(buffers))
                chunk_loop(sp, store_chunk)

            edge_pass(MESSAGES, src_v)
            store_table(HOP1)
            if stop >= 1:
                edge_pass(HOP1, src_v)
                store_table(HOP2)
                edge_pass(HOP2, src_v)
            if stop >= 2:
                store_table(ATTENTION)
                edge_pass(ATTENTION, src_v)
            if stop >= 3:
                sp.sem_inc(s["y_free"], 2)
                y_rows = table[RELATIONS].rearrange("(n p r) d -> n p (r d)", p=P, r=NREL)

                def store_products(it, j):
                    sp.wait_ge(s["low_copied"], it * (4 * CB) + (2 * j + 4))
                    sp.wait_ge(s["high_copied"], it * (4 * CB) + (2 * j + 4))
                    sp.dma_start(one(y_rows, it * (2 * CB) + j), ybuf[j % 2]).then_inc(y_stored[j % 2], 16)
                    if j:
                        sp.wait_ge(y_stored[(j - 1) % 2], it * (16 * CB) + 16 * ((j - 1) // 2 + 1))
                        sp.sem_inc(s["y_free"], 1)

                store_products(0, 0)
                with sp.Fori(0, NCH // 2 - 1) as it:
                    for j in range(1, 2 * CB + 1):
                        store_products(it, j)
                for j in range(1, 2 * CB):
                    store_products(NCH // 2 - 1, j)
                sp.wait_ge(y_stored[1], 16 * (NB // 2))
                sp.sem_inc(s["y_free"], 1)
                edge_pass(RELATIONS, rel_v)
            sp.wait_ge(s["index_stored"], 32)
            sp.wait_ge(s["relw_loaded"], 16)
            out_chunks = out[0:(NCH - 1) * CW].rearrange("(i b p) d -> i p b d", b=CB, p=P)
            with sp.Fori(0, NCH - 1) as it:
                sp.wait_ge(s["x_final"], it + 1)
                sp.dma_start(out_chunks[bass.ds(it, 1)].rearrange("a p b d -> (a p) b d"),
                             xn[:, bass.ds(it * CB, CB), :]).then_inc(s["out_stored"], 16)
            sp.wait_ge(s["x_final"], NCH)
            sp.dma_start(out[(NCH - 1) * CW:(NB - 1) * P].rearrange("(b p) d -> p b d", p=P),
                         xn[:, (NCH - 1) * CB:NB - 1, :]).then_inc(s["out_stored"], 16)
            sp.dma_start(out[(NB - 1) * P:N], xn[0:LASTN, NB - 1, :]).then_inc(s["out_stored"], 16)
            sp.wait_ge(s["out_stored"], 16 * (NCH + 1))

        @block.gpsimd
        def _(pool):
            pool.iota(prod[:, 0, :].bitcast(I32), pattern=[[1, W]], base=0, channel_multiplier=0).then_inc(
                s["iota_ready"], 1)
            pool.memset(ident[:, :], 0.0).then_inc(s["pool_const"], 1)
            pool.memset(valid[:, :], 1.0).then_inc(s["pool_const"], 1)
            pool.memset(prod[:, 1, :], 1.0).then_inc(s["pool_const"], 1)
            pool.wait_ge(s["pool_const"], 3)
            pool.affine_select(out=ident[:, :], in_=ident[:, :], compare_op=ALU.not_equal, fill=1.0, base=0,
                               pattern=[[-1, P]], channel_multiplier=1).then_inc(s["pool_const"], 1)
            pool.affine_select(out=valid[:, :], in_=valid[:, :], compare_op=ALU.is_ge, fill=0.0, base=N - 1,
                               pattern=[[-P, NB]], channel_multiplier=-1).then_inc(s["pool_const"], 1)
            pool.affine_select(out=prod[:, 1, :], in_=prod[:, 1, :], compare_op=ALU.is_ge, fill=0.0, base=-1,
                               pattern=[[1, P]], channel_multiplier=-1).then_inc(s["pool_const"], 1)

            pool.wait_ge(s["pool_const"], 6)
            pool.memset(acc[D:M1, :], 0.0).then_inc(s["acc_zeroed"], 1)
            pool.wait_ge(s["acc_zeroed"], 1)
            pool.memset(acc[0:D, NP:NACC], 0.0).then_inc(s["acc_zeroed"], 1)

            def edge_pass(p, tab):
                with pool.Fori(0, NI) as it:
                    for k in range(R):
                        pool.wait_ge(s["acc_added"], it * R + (p * NG + k + 1))
                        pool.wait_ge(idx_ready[k], it * 16 + (p * NI + 1) * 16)
                        pool.sem_inc(s["gather_started"], 1)
                        for c in range(C):
                            pool.indirect_dma_start(
                                out=rows[:, k, c, 0:D], out_offset=None, in_=tab,
                                in_offset=bass.IndirectOffsetOnAxis(ap=idx[:, k, c:c + 1], axis=0)).then_inc(
                                gathered[k], 16)

            edge_pass(MESSAGES, a["x"])
            for p in [HOP1, HOP2] * (stop >= 1) + [ATTENTION] * (stop >= 2):
                pool.wait_ge(st[p - 1]["stored"], 16 * NCH)
                edge_pass(p, table[p])
            if stop >= 3:
                pool.wait_ge(st[ATTENTION]["acc_copied"], NCH)
                pool.memset(acc[0:D, :], 0.0).then_inc(s["acc_zeroed"], 1)
                pool.wait_ge(s["y_free"], 2 + NB)
                edge_pass(RELATIONS, table[RELATIONS])

        @block.scalar
        def _(act):
            act.preload_act_table_set("natural_log_exp_and_others")
            loads = []

            def load(dst, src):
                act.dma_start(dst, src).then_inc(s["small_loaded"], 16)
                loads.append(1)

            act.dma_start(cols[0:D, 3:4], a["L0_gnn_epsilon"][0].partition_broadcast(D)).then_inc(
                s["epsilon_loaded"], 16)
            act.wait_ge(s["weights_zero"], 1)
            for c in range(C):
                load(attrw[DE * c:DE * (c + 1), D * c:D * (c + 1)], a["L0_gnn_We_kernel"])
            load(rowb[0:1, 0, 0:D], a["L0_gnn_We_bias"].rearrange("(a d) -> a d", a=1))
            load(rowb[0:1, 1, 0:D], a["L0_gnn_b2"].rearrange("(a d) -> a d", a=1))
            load(w1[0:D, :, :], a["L0_gnn_W1"].rearrange("(t p) h -> p t h", t=2))
            load(w2[:, :, :], a["L0_gnn_W2"].rearrange("(t p) h -> p t h", t=2))
            with nc.allow_non_contiguous_dma(reason="columns of small vectors"):
                load(cols[0:D, 0:1], a["L0_gnn_globals_"].rearrange("a d -> d a"))
                load(cols[:, 1:3], a["L0_gnn_b1"].rearrange("(m p) -> p m", m=2))
            for k, name in enumerate(["L1_gnn_bias", "L2_gnn_gamma", "L2_gnn_beta", "L3_gnn_bias"]):
                load(bvec[:, k, :], a[name].partition_broadcast(P))
            load(w3[:, 0, :], a["L1_gnn_weight"])
            load(w3[:, 2, :], a["L3_gnn_self_weight"])
            load(coeff[:, :], a["L3_gnn_coeff"])
            assert len(loads) == SMALL_LOADS

            act.wait_ge(s["setup_dve"], 1)
            act.wait_ge(s["x_loaded"], 32)
            act.sem_inc(s["init_copied"], 2)

            def stage_x(n, k):
                act.activation(init_buf[k], xn[:, bass.ds(n * CB, CB), :].rearrange("p b d -> p (b d)"),
                               ACT.Copy).then_inc(s["init_staged"], 1)

            def scale_x(n, k, more):
                if more:
                    stage_x(n + 1, 1 - k)
                act.wait_ge(s["init_turned"], n + 1)
                act.sem_inc(s["act_started"], 1)
                act.activation(acc_chunk(D, n), [H2, T2][k][0:D, 0:CW], ACT.Identity, bias=0.0,
                               scale=cols[0:D, 3:4]).then_inc(s["init_copied"], 1)

            stage_x(0, 0)
            chunk_loop(act, scale_x)

            def root(out_, in_, value):
                act.wait_ge(s["root_in"], value)
                act.activation(out_, in_, ACT.Ln).then_inc(s["root_log"], 1)
                act.wait_ge(s["root_log"], value)
                act.activation(out_, out_, ACT.Exp, scale=-0.5).then_inc(s["root_out"], 1)

            def reciprocal(out_, in_, value):
                act.activation(out_, in_, ACT.Ln, bias=cols[:, 6:7]).then_inc(s["log_done"], 1)
                act.wait_ge(s["log_done"], value)
                act.activation(out_, out_, ACT.Exp, scale=-1.0).then_inc(s["inverse_out"], 1)

            def copy_attrs(g, k):
                act.wait_ge(s["attrs_turned"], g + 1)
                act.activation(attrT[:, k % 2, :], T2[:, 512 * (k % 2):512 * (k % 2) + P], ACT.Copy).then_inc(
                    s["attrs_copied"], 1)

            def exp_messages(g, k):
                act.wait_ge(s["exp_in"], g + 1)
                act.activation(msg_u[k % 2], msg_u[k % 2], ACT.Exp).then_inc(s["exp_out"], 1)

            def invert(g):
                act.wait_ge(s["inverse_in"], g + 1)
                reciprocal(msg_r, msg_n, g + 1)

            def message_step(g, k, more=True):
                if more:
                    copy_attrs(g + 2, k + 2)
                invert(g + 1)
                if more:
                    exp_messages(g + 2, k + 2)

            copy_attrs(0, 0)
            exp_messages(0, 0)
            copy_attrs(1, 1)
            invert(0)
            exp_messages(1, 1)
            with act.Fori(0, NI - 1) as it:
                for k in range(R):
                    message_step(it * R + k, k)
            for k in range(R - 1):
                message_step(NG - R + k, k, k < R - 2)

            act.wait_ge(s["acc_added"], acc_total(MESSAGES))
            act.wait_ge(s["chunk_padding"], 2)
            q = st[MESSAGES]
            act.sem_inc(q["taken"], 1)

            def copy_sums(n, k):
                if not isinstance(n, int) or n > 0:
                    act.wait_ge(q["counts"], n)
                act.sem_inc(s["act_started"], 1)
                act.activation(chunk_pair[k][0:M1, :], acc_chunk(M1, n), ACT.Copy).then_inc(q["acc_copied"], 1)

            def take_next(n):
                act.wait_ge(q["turned"], n + 2)
                act.sem_inc(s["act_started"], 1)
                act.activation(acc_chunk(D, n), H2[0:D, 0:CW], ACT.Copy).then_inc(q["taken"], 1)

            def hidden_step(n, k, take=True, ahead=True, back=True):
                for m in range(2):
                    act.wait_ge(q["capped"], n * 2 + (m + 1))
                    act.activation(hid[:, m, :], hid[:, m, :], ACT.Exp).then_inc(q["exp"], 1)
                if take:
                    take_next(n - 2)
                if ahead:
                    copy_sums(n + 1, 1 - k)
                for m in range(2):
                    act.wait_ge(s["inverse_in"], n * 2 + (NG + m + 1))
                    reciprocal(inverse[m], tmp[:, m, :], n * 2 + (NG + m + 1))
                if back:
                    root(small[:, 5:7, :], small[:, 2:4, :], n + ROOTS[MESSAGES])

            copy_sums(0, 0)
            hidden_step(0, 0, take=False, back=False)
            hidden_step(1, 1, take=False)
            with act.Fori(0, NCH // 2 - 2) as it:
                for k in range(2):
                    hidden_step(it * 2 + (k + 2), k)
            hidden_step(NCH - 2, 0)
            hidden_step(NCH - 1, 1, ahead=False)
            root(small[:, 5:7, :], small[:, 2:4, :], NCH + ROOTS[MESSAGES])
            take_next(NCH - 2)
            take_next(NCH - 1)

            if stop >= 1:
                def node_stage(p, rows_used, take, zero=False, roots=None):
                    q = st[p]

                    def copy_chunk(n, k):
                        act.activation(chunk_buf[k][0:rows_used, :], acc_chunk(rows_used, n), ACT.Copy).then_inc(
                            q["acc_copied"], 1)

                    def step(n, k, more):
                        if more == 2:
                            act.wait_ge(q["product"], n + 2)
                            act.sem_inc(s["act_started"], 1)
                            copy_chunk(n + 2, k)
                        if zero:
                            act.wait_ge(q["acc_copied"], n + 1)
                            act.sem_inc(s["act_started"], 1)
                            act.activation(acc_chunk(M1, n), hid[0:M1, 1, :], ACT.Copy).then_inc(s["zero_copied"], 1)
                        if roots is not None:
                            root(small[:, 5, :], small[:, 2, :], n + (roots + 1))
                        if take:
                            act.wait_ge(q["turned"], n + 3)
                            act.sem_inc(s["act_started"], 1)
                            act.activation(take(n), H2[0:D, 0:CW], ACT.Copy).then_inc(q["taken"], 1)

                    act.wait_ge(s["acc_added"], acc_total(p))
                    if take:
                        act.sem_inc(q["taken"], 1)
                    copy_chunk(0, 0)
                    copy_chunk(1, 1)
                    chunk_loop(act, step)

                node_stage(HOP1, D, lambda n: acc_chunk(D, n))
                act.wait_ge(s["zeros_ready"], 2)
                node_stage(HOP2, D, lambda n: zT[0:D, bass.ds(n * CW, CW)], zero=True, roots=ROOTS[HOP2])
            if stop >= 2:
                def copy_rows(g):
                    for h in range(2):
                        act.wait_ge(s["rows_turned"], g * 2 + (h + 1))
                        act.activation(rowsT[:, 512 * h:512 * (h + 1)], T2[0:D, 512 * h:512 * (h + 1)],
                                       ACT.Copy).then_inc(s["rows_copied"], 1)

                def exp_scores(g):
                    act.wait_ge(s["exp_in"], g + (NG + 1))
                    act.activation(score8[:, 1, :], score8[:, 0, :], ACT.Exp).then_inc(s["exp_out"], 1)

                copy_rows(0)
                copy_rows(1)
                exp_scores(0)
                with act.Fori(0, NI - 1) as it:
                    for k in range(R):
                        copy_rows(it * R + (k + 2))
                        exp_scores(it * R + (k + 1))
                for k in range(R - 1):
                    if k < R - 2:
                        copy_rows(NG - R + k + 2)
                    exp_scores(NG - R + k + 1)
                act.wait_ge(s["acc_added"], acc_total(ATTENTION))
                q = st[ATTENTION]

                def copy_sums(n, k, more):
                    act.wait_ge(q["product"], n + 1)
                    act.sem_inc(s["act_started"], 1)
                    act.activation(chunk_buf[k], acc_chunk(M1, n), ACT.Copy).then_inc(q["acc_copied"], 1)

                chunk_loop(act, copy_sums)
            if stop >= 3:
                q = st[RELATIONS]
                act.sem_inc(s["high_copied"], 2)
                root(bn[:, 5, :], bn[:, 0, :], ROOTS["bn"] + 1)

                def take_features(n, k):
                    act.wait_ge(st[ATTENTION]["turned"], n + 1)
                    act.activation(xT[k][0:D, :], H2[0:D, 0:CW], ACT.Copy).then_inc(st[ATTENTION]["taken"], 1)

                def copy_high(n, k, more):
                    for b in range(CB):
                        for j in range(2):
                            act.wait_ge(s["product_ready"], n * (2 * CB) + (2 * b + j + 1))
                            if j == 0:
                                act.wait_ge(s["y_free"], n * CB + (b + 1))
                            act.activation(ybuf[(CB * k + b) % 2][:, 1024 + 512 * j:1024 + 512 * (j + 1)],
                                           T2[:, 512 * j:512 * (j + 1)], ACT.Copy).then_inc(s["high_copied"], 1)
                        if more and b == 3:
                            root(small[:, 5, :], small[:, 2, :], n + (ROOTS[ATTENTION] + 2))
                        if more and b == 5:
                            take_features(n + 1, 1 - k)

                root(small[:, 5, :], small[:, 2, :], ROOTS[ATTENTION] + 1)
                take_features(0, 0)
                chunk_loop(act, copy_high)
                node_stage(RELATIONS, D, None, roots=ROOTS[RELATIONS])

        @block.tensor
        def _(pe):
            def turn_chunk(to=H2, rows_of=stage):
                pe.sem_inc(s["pe_started"], 1)
                for b in range(CB):
                    last = pe.transpose(to[0:D, P * b:P * (b + 1)], rows_of[:, D * b:D * (b + 1)], ident[:, :])
                return last

            def turn_back(m):
                pe.sem_inc(s["pe_started"], 1)
                for b in range(CB):
                    last = pe.transpose(A1[:, m * b:m * (b + 1)], chunkT[0:m, P * b:P * (b + 1)], ident[0:m, 0:m])
                return last

            pe.wait_ge(s["pool_const"], 6)
            pe.wait_ge(s["matrices_ready"], 1)

            def turn_x(n, k, more):
                pe.wait_ge(s["init_staged"], n + 1)
                pe.wait_ge(s["init_copied"], n + 1)
                turn_chunk([H2, T2][k], init_buf[k]).then_inc(s["init_turned"], 1)

            chunk_loop(pe, turn_x)
            pe.wait_ge(s["init_copied"], NCH + 2)
            pe.wait_ge(s["small_loaded"], 16 * SMALL_LOADS)
            pe.transpose(A1[0:D, 0:D], w3[:, 0, :], ident[0:D, 0:D])
            pe.transpose(A1[0:NBASE, 64:64 + NREL], coeff[:, :], ident[0:NREL, 0:NREL])
            for m in range(2):
                last = pe.matmul(A1[:, 128 + m:129 + m], w1[0:D, 1, P * m:P * (m + 1)], cols[0:D, 0:1],
                                 start=True, stop=True)
            last.then_inc(s["setup_pe"], 1)
            pe.wait_ge(s["setup_dve"], 2)
            for h in range(2):
                for c in range(C):
                    last = pe.transpose([S2, T2][h][:, c * P:c * P + HG],
                                        dst_f[:, h, :].rearrange("q (p c) -> q c p", c=C)[:, c, :],
                                        ident[0:HG, 0:HG])
            last.then_inc(s["setup_pe"], 1)
            pe.wait_ge(s["setup_dve"], 3)
            tri, count = prod[0:HG, 1, 0:HG], [score8[0:HG, 0, h:h + 1] for h in range(2)]
            pe.matmul(O1[0:HG, 0:1], tri, count[0], start=True, stop=True)
            pe.matmul(O1[0:HG, 1:2], tri, count[1], start=True, stop=False)
            pe.matmul(O1[0:HG, 1:2], ones[0:HG, 0:HG], count[0], start=False, stop=True)
            pe.matmul(O1[0:HG, 2:3], ones[0:HG, 0:HG], count[0], start=True, stop=False)
            pe.matmul(O1[0:HG, 2:3], ones[0:HG, 0:HG], count[1], start=False, stop=True).then_inc(s["setup_pe"], 1)
            pe.wait_ge(s["basis_loaded"], 16)
            pe.wait_ge(s["setup_dve"], 6)
            pe.wait_ge(s["biases_ready"], 1)
            pe.wait_ge(s["group_ready"], 1)
            for k in range(D * D // 512):
                if k > 1:
                    pe.wait_ge(s["relw_ready"], k - 1)
                pe.matmul([A1, O1][k % 2][0:NREL, :], coeffT[:, :], basis[:, 512 * k:512 * (k + 1)], start=True,
                          stop=True).then_inc(s["setup_pe"], 1)
            pe.wait_ge(s["relw_ready"], D * D // 512)
            pe.wait_ge(s["group_loaded"], 16)

            def ring_loop(step):
                with pe.Fori(0, NI - 1) as it:
                    for k in range(R):
                        step(it * R + k, k, it, 2)
                for k in range(R):
                    step(NG - R + k, k, NI - 1, min(2, R - 1 - k))

            def window_sum(p, lhs, width, wait_input):
                def now(g, k, it):
                    nx, = group_values(pe, g, [1])
                    wait_input(g, k, it)
                    pe.wait_ge(s["onehot_ready"], g + (p * (NG + 1) + 1))
                    pe.wait_ge(s["acc_added"], g + (p * NG + R - 1))
                    o = [A1, O1][k % 2][0:width, 0:W]
                    for c in range(C):
                        last = pe.matmul(o, lhs(k, c), onehot[:, k % 2, c, :], start=(c == 0), stop=(c == C - 1))
                    last.then_inc(s["window_summed"], 1)
                    with pe.If(nx > 0):
                        before, total = group_values(pe, g, [2, 3])
                        with pe.Fori(0, nx) as i:
                            pe.wait_ge(s["extra_ready"], before + total * p + i + 1)
                            for c in range(C):
                                last = pe.matmul(H2[0:width, 512:512 + W], lhs(k, c), prod[:, c, :], start=(c == 0),
                                                 stop=(c == C - 1))
                            last.then_inc(s["extra_summed"], 1)
                return now

            def mix_attrs(g, k, it):
                at = slice(512 * (k % 2), 512 * (k % 2) + 512)
                pe.wait_ge(attr_loaded[k], it * 16 + 16)
                pe.transpose(T2[:, at.start:at.start + P], attrs[:, k, :], ident[:, :]).then_inc(
                    s["attrs_turned"], 1)
                pe.matmul(S2[:, at], ones[0:1, :], rowb[0:1, 0, :], start=True, stop=False)
                pe.wait_ge(s["attrs_copied"], g + 1)
                pe.matmul(S2[:, at], attrT[:, k % 2, :], attrw[:, :], start=False, stop=True).then_inc(
                    s["attrs_mixed"], 1)

            sum_messages = window_sum(MESSAGES, lambda k, c: msg[:, c, :], M1,
                                      lambda g, k, it: pe.wait_ge(s["msg_ready"], g + 1))

            def message_step(g, k, it, more):
                if more == 2:
                    mix_attrs(g + 2, (k + 2) % R, it + (k + 2) // R)
                sum_messages(g, k, it)

            mix_attrs(0, 0, 0)
            mix_attrs(1, 1, 0)
            ring_loop(message_step)

            q = st[MESSAGES]
            pe.sem_inc(q["turned"], 1)
            pe.sem_inc(q["counts"], 1)

            def hidden(n, k):
                pe.wait_ge(q["acc_copied"], n + 1)
                for m in range(2):
                    if not isinstance(n, int) or n > 0:
                        pe.wait_ge(q["mish"], n * 2 + (m - 1))
                    for j in range(2):
                        last = pe.matmul([S2, T2][m][:, 512 * j:512 * j + HALF], w1[:, 0, P * m:P * (m + 1)],
                                         chunk_pair[k][:, HALF * j:HALF * (j + 1)], start=True, stop=True)
                    last.then_inc(q["hidden"], 1)

            def output_step(n, k, ahead=True, behind=True):
                if ahead:
                    hidden(n + 1, 1 - k)
                pe.wait_ge(q["mish"], n * 2 + 2)
                pe.matmul(O1[:, 0:CD], ones[0:1, :], rowb[0:1, 1, 0:CD], start=True, stop=False,
                          skip_group_check=True)
                for b in range(CB):
                    for m in range(2):
                        last = pe.matmul(O1[:, D * b:D * (b + 1)], inverse[m][:, P * b:P * (b + 1)], w2[:, m, :],
                                         start=False, stop=(b == CB - 1 and m == 1), skip_group_check=True)
                last.then_inc(q["product"], 1)
                for b in range(CB):
                    last = pe.transpose(A1[:, M1 * b:M1 * (b + 1)], chunk_pair[k][0:M1, P * b:P * (b + 1)],
                                        ident[0:M1, 0:M1])
                last.then_inc(q["counts"], 1)
                if behind:
                    turn_next(n - 1)

            def turn_next(n):
                pe.wait_ge(q["staged"], n + 1)
                pe.wait_ge(q["taken"], n + 1)
                turn_chunk().then_inc(q["turned"], 1)

            hidden(0, 0)
            output_step(0, 0, behind=False)
            with pe.Fori(0, NCH // 2 - 1) as it:
                for j in range(1, 3):
                    output_step(it * 2 + j, j % 2)
            output_step(NCH - 1, 1, ahead=False)
            turn_next(NCH - 1)

            def hop(p):
                now = window_sum(p, lambda k, c: rows[:, k, c, 0:D], D,
                                 lambda g, k, it: pe.wait_ge(gathered[k], it * (C * 16) + (p * NI + 1) * (C * 16)))
                with pe.Fori(0, NI) as it:
                    for k in range(R):
                        now(it * R + k, k, it)

            def node_stage(p, turn=True):
                q = st[p]

                def product(n, k):
                    pe.wait_ge(q["acc_copied"], n + 1)
                    pe.sem_inc(s["pe_started"], 1)
                    for b in range(CB):
                        o, x = [A1, O1][k][:, D * b:D * (b + 1)], chunk_buf[k][0:D, P * b:P * (b + 1)]
                        if p == HOP2:
                            last = pe.matmul(o, x, w3[:, 1, :], start=True, stop=True)
                        else:
                            last = pe.transpose(o, x, ident[0:D, 0:D])
                    last.then_inc(q["product"], 1)

                def step(n, k, more):
                    if more:
                        pe.wait_ge(q["counts"], n + 1)
                        product(n + 1, 1 - k)
                    if turn:
                        pe.wait_ge(q["staged"], n + 1)
                        pe.wait_ge(q["taken"], n + 1)
                        turn_chunk(H2, out_buf[k]).then_inc(q["turned"], 1)

                pe.sem_inc(q["product"], 1)
                if turn:
                    pe.sem_inc(q["turned"], 2)
                product(0, 0)
                chunk_loop(pe, step)
                pe.wait_ge(q["counts"], NCH + 1)

            if stop >= 1:
                for p in (HOP1, HOP2):
                    hop(p)
                    node_stage(p)
            if stop >= 2:
                def turn_rows(g, k, it):
                    pe.wait_ge(gathered[k], it * (C * 16) + (ATTENTION * NI + 1) * (C * 16))
                    pe.sem_inc(s["pe_started"], 1)
                    for c in range(C):
                        ins = pe.transpose(T2[0:D, P * c:P * (c + 1)], rows[:, k, c, 0:D], ident[:, :])
                        if c % 4 == 3:
                            ins.then_inc(s["rows_turned"], 1)

                def score(g, w):
                    pe.wait_ge(s["scores_read"], g + 1)
                    for c in range(C):
                        if c % 4 == 0:
                            pe.wait_ge(s["rows_copied"], g * 2 + (c // 4 + 1))
                            pe.sem_inc(s["pe_started"], 1)
                        last = pe.matmul(S2[:, P * c:P * (c + 1)], rowsT[:, P * c:P * (c + 1)],
                                         zT[0:D, bass.ds(w, W)], start=True, stop=True)
                    last.then_inc(s["scored"], 1)

                def score_further(g):
                    w, nx = group_values(pe, g, [0, 1])
                    with pe.If(nx > 0):
                        before, = group_values(pe, g, [2])
                        with pe.Fori(0, nx) as i:
                            pe.wait_ge(s["score_extra_ready"], before + i + 1)
                            pe.sem_inc(s["pe_started"], 1)
                            for c in range(C):
                                last = pe.matmul(H2[:, P * c:P * (c + 1)], rowsT[:, P * c:P * (c + 1)],
                                                 zT[0:D, further(pe, w, i)], start=True, stop=True)
                            last.then_inc(s["score_extra_summed"], 1)

                sum_weighted = window_sum(ATTENTION, lambda k, c: msg[:, c, :], M1,
                                          lambda g, k, it: pe.wait_ge(s["msg_ready"], g + (NG + 1)))

                def attention_step(g, k, it, more):
                    if more:
                        score_further(g + 1)
                    if more == 2:
                        w, = group_values(pe, g + 2, [0])
                        turn_rows(g + 2, (k + 2) % R, it + (k + 2) // R)
                    sum_weighted(g, k, it)
                    if more == 2:
                        score(g + 2, w)

                for k in range(2):
                    w, = group_values(pe, k, [0])
                    turn_rows(k, k, 0)
                    score(k, w)
                    if k == 0:
                        score_further(0)
                ring_loop(attention_step)
                q = st[ATTENTION]
                pe.sem_inc(q["product"], 2)
                zeros = hid[0:1, 1, 0:CD]

                def turn_sums(n, k):
                    pe.wait_ge(q["acc_copied"], n + 1)
                    pe.wait_ge(q["counts"], n + 1)
                    pe.sem_inc(s["pe_started"], 1)
                    for b in range(CB):
                        last = pe.transpose([A1, O1][k][:, M1 * b:M1 * (b + 1)], chunk_buf[k][:, P * b:P * (b + 1)],
                                            ident[0:M1, 0:M1])
                    last.then_inc(q["product"], 1)

                def sum_nodes(n, k, more):
                    if more:
                        turn_sums(n + 1, 1 - k)
                    pe.wait_ge(q["counts"], n + 3)
                    pe.sem_inc(s["pe_started"], 1)
                    pe.matmul(H2[:, 0:CD], ones[:, :], hn[:, bass.ds(n * CB, CB), :].rearrange("p b d -> p (b d)"),
                              start=False, stop=False, skip_group_check=True)

                pe.wait_ge(s["zero_row"], 1)
                pe.matmul(H2[:, 0:CD], ones[0:1, :], zeros, start=True, stop=False, skip_group_check=True)
                turn_sums(0, 0)
                chunk_loop(pe, sum_nodes)
                pe.matmul(H2[:, 0:CD], ones[0:1, :], zeros, start=False, stop=True, skip_group_check=True).then_inc(
                    s["bn_summed"], 1)
            if stop >= 3:
                def sum_squares(n, k, more):
                    pe.wait_ge(s["bn_squared"], n + 1)
                    pe.matmul(H2[:, 512:512 + CD], ones[:, :], tmp[:, k, CD:2 * CD], start=False, stop=False,
                              skip_group_check=True).then_inc(s["bn_summed"], 1)

                pe.matmul(H2[:, 512:512 + CD], ones[0:1, :], zeros, start=True, stop=False,
                          skip_group_check=True).then_inc(s["bn_summed"], 1)
                chunk_loop(pe, sum_squares)
                pe.matmul(H2[:, 512:512 + CD], ones[0:1, :], zeros, start=False, stop=True,
                          skip_group_check=True).then_inc(s["bn_summed"], 1)

                def turn_features(n, k):
                    pe.wait_ge(q["staged"], n + 1)
                    pe.sem_inc(s["pe_started"], 1)
                    for b in range(CB):
                        last = pe.transpose(H2[0:D, P * b:P * (b + 1)], x_next[k][:, D * b:D * (b + 1)], ident[:, :])
                    last.then_inc(q["turned"], 1)

                def products(n, k, more):
                    pe.wait_ge(q["taken"], n + 1)
                    for b in range(CB):
                        for j in range(2):
                            pe.wait_ge(s["low_copied"], n * (2 * CB) + (2 * b + j + 1))
                            pe.wait_ge(s["high_copied"], n * (2 * CB) + (2 * b + j + 1))
                            for h in range(2):
                                last = pe.matmul([S2, T2][h][:, 512 * j:512 * (j + 1)],
                                                 xT[k][:, P * b:P * (b + 1)], relw[:, :, :].rearrange(
                                                     "p r d -> p (r d)")[:, 1024 * h + 512 * j:1024 * h + 512 * (j + 1)],
                                                 start=True, stop=True)
                            last.then_inc(s["product_ready"], 1)
                        if b == 1:
                            for c in range(CB):
                                last = pe.matmul(A1[:, D * c:D * (c + 1)], xT[k][0:D, P * c:P * (c + 1)], w3[:, 2, :],
                                                 start=True, stop=True)
                            last.then_inc(q["hidden"], 1)
                        if more and b == 5:
                            turn_features(n + 1, 1 - k)

                pe.wait_ge(s["padding_zero"], 2)
                turn_features(0, 0)
                chunk_loop(pe, products)
                hop(RELATIONS)
                node_stage(RELATIONS, turn=False)

        @block.vector
        def _(dve):
            steps = Steps(dve, s["dve_steps"])
            link = steps.link
            tt, ts, stt = dve.tensor_tensor, dve.tensor_scalar, dve.scalar_tensor_tensor

            def by_node(t):
                return t.unsqueeze(2).to_broadcast([P, CB, D])

            def by_feature(t):
                return t.unsqueeze(1).to_broadcast([P, CB, D])

            def nodes(t, it):
                return t[:, bass.ds(it * CB, CB)]

            dve.memset(xn[:, NB - 1, :], 0.0).then_inc(s["pads_ready"], 1)
            dve.memset(dst_i, N).then_inc(s["pads_ready"], 1)
            dve.memset(src_i, 0).then_inc(s["pads_ready"], 1)
            dve.memset(typ_i, 0).then_inc(s["pads_ready"], 1)
            dve.memset(attrw[:, :], 0.0).then_inc(s["weights_zero"], 1)
            dve.memset(ones[:, :], 1.0).then_inc(s["matrices_ready"], 1)
            link(dve.memset(cols[:, 6:7], 2.0))
            link(dve.memset(w1[D:P, :, :], 0.0))
            link(dve.memset(msg[:, :, :], 1.0))
            link(dve.memset(rows[:, :, :, :], 1.0))
            dve.sem_inc(s["acc_added"], R)
            link(dve.memset(gtab[:, :, :], 0))
            link(dve.memset(dstrel[:, NG, :], 0.0))
            dve.wait_ge(s["iota_ready"], 1)
            link(dve.tensor_copy(iota[:, :], prod[:, 0, :].bitcast(I32)))
            dve.wait_ge(s["epsilon_loaded"], 16)
            ts(cols[0:D, 3:4], cols[0:D, 3:4], 1.0, None, ALU.add).then_inc(s["setup_dve"], 1)

            dve.wait_ge(s["dst_loaded"], 48)
            link(dve.tensor_copy(dst_f, dst_i))
            lo, hi, span = (small[0:HG, k, 0:2] for k in range(3))
            link(dve.tensor_reduce(lo, dst_f, AX, ALU.min))
            link(dve.tensor_reduce(hi, dst_f, AX, ALU.max))
            link(tt(span, hi, lo, ALU.subtract))
            link(ts(dst_f[:, 0, :], dst_f[:, 0, :], small[0:HG, 0, 0:1], None, ALU.subtract))
            ts(dst_f[:, 1, :], dst_f[:, 1, :], small[0:HG, 0, 1:2], None, ALU.subtract).then_inc(s["setup_dve"], 1)
            link(dve.tensor_copy(gtab[0:HG, :, 0], lo))
            link(dve.tensor_copy(gtab[0:HG, :, 1], span))
            link(ts(gtab[0:HG, :, 1], gtab[0:HG, :, 1], W.bit_length() - 1, None, ALU.logical_shift_right))
            dve.tensor_copy(score8[0:HG, 0, 0:2], gtab[0:HG, :, 1]).then_inc(s["setup_dve"], 1)
            dve.wait_ge(s["small_loaded"], 16 * SMALL_LOADS)
            dve.tensor_copy(rowb[0:1, :, D:C * D].rearrange("p t (c d) -> p t c d", d=D),
                            rowb[0:1, :, 0:D].unsqueeze(2).to_broadcast([1, 2, C - 1, D])).then_inc(s["biases_ready"], 1)
            dve.wait_ge(s["setup_pe"], 1)
            dve.tensor_copy(w3[:, 1, :], A1[0:D, 0:D]).then_inc(s["setup_dve"], 1)
            dve.tensor_copy(coeffT[:, :], A1[0:NBASE, 64:64 + NREL]).then_inc(s["setup_dve"], 1)
            tt(cols[:, 4:6], A1[:, 128:130], cols[:, 1:3], ALU.add).then_inc(s["setup_dve"], 1)
            dve.wait_ge(s["setup_pe"], 2)
            for h in range(2):
                link(dve.tensor_copy(dstrel[:, HG * h:HG * (h + 1), :].rearrange("p q c -> p c q"),
                                     [S2, T2][h][:, :].rearrange("p (c q) -> p c q", q=P)[:, :, 0:HG]))
            dve.wait_ge(s["setup_pe"], 3)
            link(dve.tensor_copy(gtab[0:HG, :, 2], O1[0:HG, 0:2]))
            link(dve.tensor_copy(gtab[0:HG, 0, 3:4], O1[0:HG, 2:3]))
            dve.tensor_copy(gtab[0:HG, 1, 3:4], O1[0:HG, 2:3]).then_inc(s["group_ready"], 1)
            dve.wait_ge(s["index_stored"], 16)
            dve.wait_ge(s["edge_type_32_loaded"], 48)
            stt(typ_i, src_i, float(NREL), typ_i, ALU.mult, ALU.add).then_inc(s["rel_index_ready"], 1)
            for k in range(D * D // 512):
                dve.wait_ge(s["setup_pe"], 4 + k)
                dve.tensor_copy(relw_flat[:, 512 * k:512 * (k + 1)], [A1, O1][k % 2][0:NREL, :]).then_inc(s["relw_ready"], 1)
            dve.wait_ge(s["acc_zeroed"], 2)
            dve.wait_ge(s["init_copied"], NCH + 2)
            dve.wait_ge(s["group_loaded"], 16)
            steps.straight()

            def build_onehot(g, half):
                at = dstrel[:, bass.ds(g, 1), :].rearrange("p a c -> p (a c)")
                tt(onehot[:, half, :, :], iota[:, :].unsqueeze(1).to_broadcast([P, C, W]),
                   at.unsqueeze(2).to_broadcast([P, C, W]), ALU.is_equal).then_inc(s["onehot_ready"], 1)

            def further_onehot():
                dve.drain()
                ts(dx[:, :], dx[:, :], -float(W), None, ALU.add)
                dve.drain()
                return tt(prod[:, :, :], iota[:, :].unsqueeze(1).to_broadcast([P, C, W]),
                          dx[:, :].unsqueeze(2).to_broadcast([P, C, W]), ALU.is_equal)

            def add_windows(p, g, k, width, w, nx):
                with dve.If(nx > 0):
                    before, total = group_values(dve, g, [2, 3])
                    dve.tensor_copy(dx[:, :], dstrel[:, bass.ds(g, 1), :].rearrange("p a c -> p (a c)"))
                    with dve.Fori(0, nx) as i:
                        further_onehot().then_inc(s["extra_ready"], 1)
                        dve.drain()
                        dve.wait_ge(s["extra_summed"], before + total * p + i + 1)
                        at = acc[0:width, further(dve, w, i)]
                        tt(at, at, H2[0:width, 512:512 + W], ALU.add)
                    dve.drain()
                dve.wait_ge(s["window_summed"], g + (p * NG + 1))
                dve.wait_ge(s["acc_added"], g + (p * NG + R))
                at = acc[0:width, bass.ds(w, W)]
                tt(at, at, [A1, O1][k % 2][0:width, 0:W], ALU.add).then_inc(s["acc_added"], 1)

            def pass_loop(p, per, body):
                build_onehot(0, 0)
                with dve.Fori(0, NI) as it:
                    steps.turn(it, per * R)
                    for k in range(R):
                        w, nx = group_values(dve, it * R + k, [0, 1])
                        body(it * R + k, k, it, w, nx)
                steps.end(NI)
                dve.wait_ge(s["acc_added"], acc_total(p))

            def newton(n, r, a):
                link(stt(a, n, 2.0, r, ALU.add, ALU.mult))
                link(stt(a, a, -2.0, r, ALU.add, ALU.mult))
                return stt(a, n, -1.0, a, ALU.mult, ALU.mult)

            def message_inputs(g, k, it):
                v, u = msg_v[k % 2], msg_u[k % 2]
                dve.wait_ge(s["attrs_mixed"], g + 1)
                dve.wait_ge(gathered[k], it * (C * 16) + C * 16)
                link(tt(blocks(v), blocks(S2[:, 512 * (k % 2):512 * (k % 2 + 1)]), rows[:, k, :, 0:D], ALU.add))
                ts(u, v, MISH_CAP, None, ALU.min).then_inc(s["exp_in"], 1)

            def numerator(g, k):
                u = msg_u[k % 2]
                dve.wait_ge(s["exp_out"], g + 1)
                stt(msg_n, u, 2.0, u, ALU.add, ALU.mult).then_inc(s["inverse_in"], 1)

            def mish_factor(g, k):
                dve.wait_ge(s["inverse_out"], g + 1)
                link(newton(msg_n, msg_r, msg_u[k % 2]))

            def message(k):
                tt(msg[:, :, 0:D], blocks(msg_u[k % 2]), blocks(msg_v[k % 2]), ALU.mult).then_inc(s["msg_ready"], 1)

            def message_step(g, k, it, more=True):
                w, nx = group_values(dve, g, [0, 1])
                numerator(g + 1, k + 1)
                if more:
                    dve.wait_ge(s["msg_ready"], g + 1)
                    message_inputs(g + 2, (k + 2) % R, it + (k + 2) // R)
                mish_factor(g + 1, k + 1)
                dve.sem_inc(s["dve_started"], 1)
                add_windows(MESSAGES, g, k, M1, w, nx)
                build_onehot(g + 2, k % 2)
                message(k + 1)

            steps.turn(0, 1 + 1 + 3)
            message_inputs(0, 0, 0)
            numerator(0, 0)
            message_inputs(1, 1, 0)
            mish_factor(0, 0)
            build_onehot(0, 0)
            build_onehot(1, 1)
            message(0)
            steps.end(1)
            with dve.Fori(0, NI - 1) as it:
                steps.turn(it, 4 * R)
                for k in range(R):
                    message_step(it * R + k, k, it)
            steps.end(NI - 1)
            steps.turn(0, 3 * (R - 1) + R - 2)
            for k in range(R - 1):
                message_step(NG - R + k, k, NI - 1, more=k < R - 2)
            steps.end(1)
            w, nx = group_values(dve, NG - 1, [0, 1])
            add_windows(MESSAGES, NG - 1, R - 1, M1, w, nx)
            dve.wait_ge(s["acc_added"], acc_total(MESSAGES))

            def root_newton(r, v, a):
                link(tt(a, v, r, ALU.mult))
                link(stt(a, a, -0.5, r, ALU.mult, ALU.mult))
                link(stt(r, a, 1.5, r, ALU.add, ALU.mult))
                return r

            def layernorm(y, it, roots):
                total, var = small[:, 0, :], small[:, 1, :]
                link(dve.tensor_reduce(total, y, AX, ALU.add))
                link(stt(centred, by_node(total), -1.0 / D, y, ALU.mult, ALU.add))
                link(tt(square, centred, centred, ALU.mult))
                link(dve.tensor_reduce(var, square, AX, ALU.add))
                ts(small[:, 2, :], var, 1.0 / D, EPS, ALU.mult, ALU.add).then_inc(s["root_in"], 1)
                dve.wait_ge(s["root_out"], it + (roots + 1))
                return root_newton(small[:, 5, :], small[:, 2, :], small[:, 0, :])

            y, centred = blocks(tmp[:, 0, 0:CD]), blocks(tmp[:, 0, CD:2 * CD])
            square = blocks(tmp[:, 1, 0:CD])
            out_stage = blocks(stage[:, :])

            q = st[MESSAGES]
            halves = "p (q n) -> p q n"
            y_out, y_centred = blocks(prod_flat[:, 0:CD]), blocks(prod_flat[:, CD:2 * CD])
            y_square = blocks(msg[:, :, :].rearrange("p c d -> p (c d)")[:, 0:CD])

            def cap(n):
                for m in range(2):
                    dve.wait_ge(q["hidden"], n * 2 + (m + 1))
                    ts(hid[:, m, :].rearrange(halves, q=2), [S2, T2][m][:, :].rearrange(halves, q=2)[:, :, 0:HALF],
                       cols[:, 4 + m:5 + m], MISH_CAP, ALU.add, ALU.min).then_inc(q["capped"], 1)

            def numerators(n):
                for m in range(2):
                    dve.wait_ge(q["exp"], n * 2 + (m + 1))
                    stt(tmp[:, m, :], hid[:, m, :], 2.0, hid[:, m, :], ALU.add, ALU.mult).then_inc(s["inverse_in"], 1)

            def mish_hidden(n):
                for m in range(2):
                    u = hid[:, m, :]
                    dve.wait_ge(s["inverse_out"], n * 2 + (NG + m + 1))
                    link(newton(tmp[:, m, :], inverse[m], u))
                    stt(inverse[m].rearrange(halves, q=2), [S2, T2][m][:, :].rearrange(halves, q=2)[:, :, 0:HALF],
                        cols[:, 4 + m:5 + m], u.rearrange(halves, q=2), ALU.add, ALU.mult).then_inc(q["mish"], 1)

            def centre(n):
                dve.wait_ge(q["product"], n + 1)
                link(tt(y_out, blocks(O1[:, 0:CD]), nodes(xn, n), ALU.add))
                link(dve.tensor_reduce(small[:, 0, :], y_out, AX, ALU.add))
                link(stt(y_centred, by_node(small[:, 0, :]), -1.0 / D, y_out, ALU.mult, ALU.add))
                dve.wait_ge(q["counts"], n + 2)
                count = A1[:, 0:M1 * CB].rearrange("p (b m) -> p b m", m=M1)[:, :, D]
                link(ts(small[:, 3, :], count, 1.0, None, ALU.add))
                link(ts(small[:, 4, :], count, 1.0, None, ALU.max))
                link(dve.reciprocal(nodes(cinv, n), small[:, 4, :]))

            def spread(n):
                link(tt(y_square, y_centred, y_centred, ALU.mult))
                link(dve.tensor_reduce(small[:, 1, :], y_square, AX, ALU.add))
                ts(small[:, 2, :], small[:, 1, :], 1.0 / D, EPS, ALU.mult, ALU.add).then_inc(s["root_in"], 1)

            def finish(n):
                dve.wait_ge(s["root_out"], n + (ROOTS[MESSAGES] + 1))
                rstd = root_newton(small[:, 5, :], small[:, 2, :], small[:, 0, :])
                root_newton(small[:, 6, :], small[:, 3, :], small[:, 0, :])
                link(dve.tensor_copy(nodes(dinv, n), small[:, 6, :]))
                link(tt(small[:, 7, :], rstd, small[:, 6, :], ALU.mult))
                dve.wait_ge(q["stage_free"], n + 1)
                dve.wait_ge(q["turned"], n + 1)
                tt(out_stage, y_centred, by_node(small[:, 7, :]), ALU.mult).then_inc(q["staged"], 1)
                link(tt(nodes(xn, n), y_centred, by_node(rstd), ALU.mult))

            dve.memset(chunkT[D:P, :], 0.0).then_inc(s["chunk_padding"], 1)
            dve.wait_ge(s["relw_loaded"], 16)
            dve.memset(zT[D:P, 0:CW], 0.0).then_inc(s["chunk_padding"], 1)
            steps.turn(0, 6)
            cap(0)
            numerators(0)
            mish_hidden(0)
            steps.end(1)
            with dve.Fori(0, NCH - 1) as it:
                steps.turn(it, 6 + 6 + 2 + 9)
                cap(it + 1)
                centre(it)
                numerators(it + 1)
                spread(it)
                mish_hidden(it + 1)
                finish(it)
            steps.end(NCH - 1)
            steps.turn(0, 6 + 2 + 9)
            centre(NCH - 1)
            spread(NCH - 1)
            finish(NCH - 1)
            steps.end(1)
            dve.wait_ge(q["taken"], NCH + 1)

            if stop >= 1:
                def hop_sum(p):
                    def body(g, k, it, w, nx):
                        build_onehot(g + 1, (k + 1) % 2)
                        add_windows(p, g, k, D, w, nx)
                    return body

                pass_loop(HOP1, 0, hop_sum(HOP1))
                q = st[HOP1]
                dve.sem_inc(q["counts"], 1)

                def between_hops(n, k, more):
                    link(tt(small[:, k, :], nodes(dinv, n), nodes(dinv, n), ALU.mult))
                    dve.wait_ge(q["product"], n + 2)
                    dve.wait_ge(q["stage_free"], n + 1)
                    dve.wait_ge(q["turned"], n + 1)
                    tt(blocks(out_buf[k]), blocks([A1, O1][k][:, 0:CD]), by_node(small[:, k, :]), ALU.mult).then_inc(
                        q["staged"], 1)
                    dve.wait_ge(q["staged"], n + 1)
                    dve.sem_inc(q["counts"], 1)

                chunk_loop(dve, between_hops, steps, 1, 1)
                dve.wait_ge(q["taken"], NCH + 1)
                pass_loop(HOP2, 0, hop_sum(HOP2))
                dve.wait_ge(s["relw_loaded"], 16)
                dve.memset(zT[0:D, NP:NACC], 0.0).then_inc(s["zeros_ready"], 1)
                dve.memset(hid[:, 1, :], 0.0).then_inc(s["zeros_ready"], 1)
                q = st[HOP2]
                dve.sem_inc(q["counts"], 1)

                def after_hops(n, k, more):
                    q = st[HOP2]
                    dve.wait_ge(q["product"], n + 2)
                    tt(y, blocks([A1, O1][k][:, 0:CD]), by_node(nodes(dinv, n)), ALU.mult).then_inc(q["counts"], 1)
                    dve.wait_ge(q["counts"], n + 2)
                    link(tt(y, y, nodes(xn, n), ALU.add))
                    link(tt(y, y, by_feature(bvec[:, 0, :]), ALU.add))
                    rstd = layernorm(y, n, ROOTS[HOP2])
                    dve.wait_ge(q["stage_free"], n + 1)
                    dve.wait_ge(q["turned"], n + 1)
                    tt(blocks(out_buf[k]), centred, by_node(rstd), ALU.mult).then_inc(q["staged"], 1)
                    link(tt(nodes(xn, n), centred, by_node(rstd), ALU.mult))

                chunk_loop(dve, after_hops, steps, 10, 10)
                dve.wait_ge(q["taken"], NCH + 1)
                dve.wait_ge(s["zero_copied"], NCH)
            if stop >= 2:
                dve.sem_inc(s["scores_read"], 1)

                def scores(g, k):
                    nx, = group_values(dve, g, [1])
                    dve.wait_ge(s["scored"], g + 1)
                    dve.wait_ge(s["onehot_ready"], g + (ATTENTION * (NG + 1) + 1))
                    tt(prod[:, :, :], onehot[:, k % 2, :, :], S2[:, :].rearrange("p (c n) -> p c n", n=W),
                       ALU.mult).then_inc(s["scores_read"], 1)
                    dve.wait_ge(s["scores_read"], g + 2)
                    link(dve.tensor_reduce(score8[:, 0, :], prod[:, :, :], AX, ALU.add))
                    dve.sem_inc(s["dve_started"], 1)
                    with dve.If(nx > 0):
                        before, = group_values(dve, g, [2])
                        dve.tensor_copy(dx[:, :], dstrel[:, bass.ds(g, 1), :].rearrange("p a c -> p (a c)"))
                        with dve.Fori(0, nx) as i:
                            further_onehot().then_inc(s["score_extra_ready"], 1)
                            dve.drain()
                            dve.wait_ge(s["score_extra_summed"], before + i + 1)
                            tt(prod[:, :, :], prod[:, :, :], H2[:, :].rearrange("p (c n) -> p c n", n=W), ALU.mult)
                            dve.drain()
                            dve.tensor_reduce(score8[:, 2, :], prod[:, :, :], AX, ALU.add)
                            dve.drain()
                            tt(score8[:, 0, :], score8[:, 0, :], score8[:, 2, :], ALU.add)
                        dve.drain()
                    dve.sem_inc(s["exp_in"], 1)

                def weigh(g, k):
                    dve.wait_ge(s["exp_out"], g + (NG + 1))
                    link(ts(score8[:, 3, :], score8[:, 1, :], 1.0, None, ALU.max))
                    tt(msg[:, :, :], rows[:, k, :, :], score8[:, 3, :].unsqueeze(2).to_broadcast([P, C, M1]),
                       ALU.mult).then_inc(s["msg_ready"], 1)

                def attention_step(g, k):
                    w, nx = group_values(dve, g, [0, 1])
                    scores(g + 1, k + 1)
                    add_windows(ATTENTION, g, k, M1, w, nx)
                    build_onehot(g + 2, k % 2)
                    weigh(g + 1, (k + 1) % R)

                build_onehot(0, 0)
                build_onehot(1, 1)
                steps.turn(0, 2)
                scores(0, 0)
                weigh(0, 0)
                steps.end(1)
                with dve.Fori(0, NI - 1) as it:
                    steps.turn(it, 2 * R)
                    for k in range(R):
                        attention_step(it * R + k, k)
                steps.end(NI - 1)
                steps.turn(0, 2 * (R - 1))
                for k in range(R - 1):
                    attention_step(NG - R + k, k)
                steps.end(1)
                w, nx = group_values(dve, NG - 1, [0, 1])
                add_windows(ATTENTION, NG - 1, R - 1, M1, w, nx)
                dve.wait_ge(s["acc_added"], acc_total(ATTENTION))
                q = st[ATTENTION]
                dve.memset(hid[0:1, 1, :], 0.0).then_inc(s["zero_row"], 1)
                dve.sem_inc(q["counts"], 2)

                def node_means(n, k, more):
                    dve.wait_ge(q["product"], n + 3)
                    sums = [A1, O1][k][:, 0:M1 * CB].rearrange("p (b m) -> p b m", m=M1)
                    weight, inverse, factor = (small[:, 3 * k + j, :] for j in range(3))
                    link(ts(weight, sums[:, :, D], TINY, None, ALU.max))
                    link(dve.reciprocal(inverse, weight))
                    link(tt(factor, inverse, nodes(valid, n), ALU.mult))
                    tt(nodes(hn, n), sums[:, :, 0:D], by_node(factor), ALU.mult).then_inc(q["counts"], 1)

                chunk_loop(dve, node_means, steps, 3, 3)
            if stop >= 3:
                total, mean, scale, shift, sq = (bn[:, j, :] for j in range(5))

                def column_sums(value, bank):
                    dve.wait_ge(s["bn_summed"], value)
                    link(dve.tensor_reduce(total, H2[:, 512 * bank:512 * bank + CD].rearrange("p (b d) -> p d b", d=D), AX,
                                           ALU.add))

                dve.memset(xT_both[D:P, :], 0.0).then_inc(s["padding_zero"], 1)
                dve.memset(relw[D:P, :, :], 0.0).then_inc(s["padding_zero"], 1)
                steps.turn(0, 2)
                column_sums(1, 0)
                link(ts(mean, total, 1.0 / N, None, ALU.mult))
                steps.end(1)

                def squares(n, k, more):
                    dve.wait_ge(s["bn_summed"], n + 1)
                    link(tt(blocks(tmp[:, k, 0:CD]), nodes(hn, n), by_feature(mean), ALU.subtract))
                    tt(tmp[:, k, CD:2 * CD], tmp[:, k, 0:CD], tmp[:, k, 0:CD], ALU.mult).then_inc(s["bn_squared"], 1)

                chunk_loop(dve, squares, steps, 1, 1)
                steps.turn(0, 3 + 1 + 3 + 3)
                column_sums(NCH + 3, 1)
                link(tt(sq, mean, mean, ALU.mult))
                link(stt(total, sq, -float(NPAD), total, ALU.mult, ALU.add))
                link(ts(total, total, 1.0 / N, EPS, ALU.mult, ALU.add))
                dve.sem_inc(s["root_in"], 1)
                dve.wait_ge(s["root_out"], ROOTS["bn"] + 1)
                root_newton(bn[:, 5, :], total, sq)
                link(tt(scale, bn[:, 5, :], bvec[:, 1, :], ALU.mult))
                link(tt(sq, mean, scale, ALU.mult))
                link(tt(shift, bvec[:, 2, :], sq, ALU.subtract))
                steps.end(1)

                def normalise(n, k, piece):
                    if piece == 0:
                        link(tt(y, nodes(hn, n), by_feature(scale), ALU.mult))
                        link(tt(y, y, by_feature(shift), ALU.add))
                    elif piece == 1:
                        link(stt(y, y, 0.0, nodes(xn, n), ALU.max, ALU.add))
                        link(dve.tensor_reduce(small[:, 0, :], y, AX, ALU.add))
                    elif piece == 2:
                        link(stt(centred, by_node(small[:, 0, :]), -1.0 / D, y, ALU.mult, ALU.add))
                        link(tt(square, centred, centred, ALU.mult))
                    elif piece == 3:
                        link(dve.tensor_reduce(small[:, 1, :], square, AX, ALU.add))
                        ts(small[:, 2, :], small[:, 1, :], 1.0 / D, EPS, ALU.mult, ALU.add).then_inc(s["root_in"], 1)
                    elif piece == 4:
                        dve.wait_ge(s["root_out"], n + (ROOTS[ATTENTION] + 1))
                        rstd = root_newton(small[:, 5, :], small[:, 2, :], small[:, 0, :])
                        tt(blocks(x_next[k]), centred, by_node(rstd), ALU.mult).then_inc(q["staged"], 1)

                def copy_low(n, k, more):
                    for b in range(CB):
                        for j in range(2):
                            dve.wait_ge(s["product_ready"], n * (2 * CB) + (2 * b + j + 1))
                            if j == 0:
                                dve.wait_ge(s["y_free"], n * CB + (b + 1))
                            dve.tensor_copy(ybuf[(CB * k + b) % 2][:, 512 * j:512 * (j + 1)],
                                            S2[:, 512 * j:512 * (j + 1)]).then_inc(s["low_copied"], 1)
                        if b < 5 and more:
                            normalise(n + 1, 1 - k, b)
                        if b == 5:
                            dve.wait_ge(q["hidden"], n + 1)
                            link(tt(nodes(xn, n), blocks(x_next[k]), blocks(A1[:, 0:CD]), ALU.add))
                        if b == 6:
                            link(tt(nodes(xn, n), nodes(xn, n), by_feature(bvec[:, 3, :]), ALU.add))

                steps.turn(0, 10)
                for piece in range(5):
                    normalise(0, 0, piece)
                steps.end(1)
                dve.sem_inc(s["low_copied"], 2)
                chunk_loop(dve, copy_low, steps, 12, 2)
                dve.wait_ge(s["acc_zeroed"], 3)
                pass_loop(RELATIONS, 0, hop_sum(RELATIONS))
                q = st[RELATIONS]
                dve.sem_inc(q["counts"], 1)

                def last_layer(n, k, more):
                    dve.wait_ge(q["product"], n + 2)
                    tt(y, blocks([A1, O1][k][:, 0:CD]), by_node(nodes(cinv, n)), ALU.mult).then_inc(q["counts"], 1)
                    dve.wait_ge(q["counts"], n + 2)
                    link(tt(y, y, nodes(xn, n), ALU.add))
                    rstd = layernorm(y, n, ROOTS[RELATIONS])
                    tt(nodes(xn, n), centred, by_node(rstd), ALU.mult).then_inc(s["x_final"], 1)
                    dve.wait_ge(s["x_final"], n + 1)

                chunk_loop(dve, last_layer, steps, 8, 8)
            else:
                dve.drain().then_inc(s["x_final"], NCH)


_INS = ['x', 'src', 'dst', 'edge_attr_16', 'edge_type_32', 'L0_gnn_globals_', 'L0_gnn_We_kernel', 'L0_gnn_We_bias',
        'L0_gnn_epsilon', 'L0_gnn_W1', 'L0_gnn_b1', 'L0_gnn_W2', 'L0_gnn_b2', 'L1_gnn_weight', 'L1_gnn_bias',
        'L2_gnn_gamma', 'L2_gnn_beta', 'L3_gnn_basis', 'L3_gnn_coeff', 'L3_gnn_self_weight', 'L3_gnn_bias']
STOP = 9


def kernel(**inputs):
    import numpy as np
    import concourse.bacc as bacc
    from concourse.bass_utils import run_bass_kernel_spmd

    nc = bacc.Bacc("TRN2", target_bir_lowering=False, num_devices=1)
    arrays, handles = {}, {}
    for name in _INS:
        arrays[f"in_{name}"] = np.ascontiguousarray(inputs[name])
        handles[name] = nc.dram_tensor(f"in_{name}", arrays[f"in_{name}"].shape,
                                       mybir.dt.from_np(arrays[f"in_{name}"].dtype), kind="ExternalInput").ap()
    out = nc.dram_tensor("out", (N, D), F32, kind="ExternalOutput").ap()
    gnn(nc, handles, out, STOP)
    return run_bass_kernel_spmd(nc, [arrays], core_ids=[0]).results[0]["out"]
```
